# Optimizing a Trainium2 kernel written in Bass

```python
import numpy as np
import jax
import jax.numpy as jnp

def _softmax(x, axis=-1):
    return jax.nn.softmax(x, axis=axis)

def _gelu(x):
    return jax.nn.gelu(x, approximate=True)

def _silu(x):
    return jax.nn.silu(x)

def _sigmoid(x):
    return jax.nn.sigmoid(x)

def _layernorm(x, axis=-1, eps=1e-05):
    m = jnp.mean(x, axis=axis, keepdims=True)
    v = jnp.var(x, axis=axis, keepdims=True)
    return (x - m) / jnp.sqrt(v + eps)

def _scatter_add(tgt, idx, src, axis=0):
    return tgt.at[idx].add(src)

def _segment_sum(src, seg, n):
    return jax.ops.segment_sum(src, seg, n)
kernel_name = 'mk_macaron_d1_jaxref_r4_fecf1a'

def setup_inputs(seed: int=0):
    np.random.seed(seed)
    _w = jnp.asarray

    def _L0_attn_setup():
        import jax, jax.numpy as jnp
        import numpy as np
        import math
        B, T, C = (2, 512, 256)
        H, L = (16, 64)
        DH = C // H
        DHE = DH // 2
        THETA = 10000.0

        def _rope_cache(t, dim):
            inv_freq = 1.0 / THETA ** (jnp.arange(0, dim, 2, dtype=jnp.float32) / dim)
            freqs = jnp.arange(t, dtype=jnp.float32)[:, None] * inv_freq[None, :]
            emb = jnp.concatenate((freqs, freqs), axis=-1)
            return (jnp.cos(emb), jnp.sin(emb))

        def _apply_rope(x, cos, sin):
            x1 = x[..., 0::2]
            x2 = x[..., 1::2]
            rot = jnp.stack((-x2, x1), axis=-1).reshape(x.shape)
            return x * cos[None, None] + rot * sin[None, None]
        key = jax.random.key(seed)
        ks = jax.random.split(key, 10)
        s = 0.02
        return {'x': jax.random.normal(ks[0], (B, T, C), jnp.float32), 'Wq_down': jax.random.normal(ks[1], (C, H * L), jnp.float32) * s, 'Wk_down': jax.random.normal(ks[2], (C, H * L), jnp.float32) * s, 'Wv_down': jax.random.normal(ks[3], (C, H * L), jnp.float32) * s, 'Wq_up_c': jax.random.normal(ks[4], (L, DHE), jnp.float32) * s, 'Wq_up_e': jax.random.normal(ks[5], (L, DHE), jnp.float32) * s, 'Wk_up_c': jax.random.normal(ks[6], (L, DHE), jnp.float32) * s, 'Wk_up_e': jax.random.normal(ks[7], (L, DHE), jnp.float32) * s, 'Wv_up': jax.random.normal(ks[8], (L, DH), jnp.float32) * s, 'Wc': jax.random.normal(ks[9], (C, C), jnp.float32) * s}
    _L0_attn_in = _L0_attn_setup()

    def _L0_ffn_setup():
        import jax, jax.numpy as jnp
        import numpy as np
        E = 8
        K = 2
        S = 1
        THRESHOLD = 0.7
        NORM_TOPK = True
        H = 256
        F = 256
        B, SEQ = (2, 256)
        key = jax.random.key(seed)
        k1, k2, k3, k4, k5 = jax.random.split(key, 5)
        hidden_states = jax.random.normal(k1, (B, SEQ, H), jnp.float32)
        gate_weight = jax.random.normal(k2, (E, H), jnp.float32) * 0.02
        gate_up_proj = jax.random.normal(k3, (E, 2 * F, H), jnp.float32) * 0.02
        down_proj = jax.random.normal(k4, (E, H, F), jnp.float32) * 0.02
        sim = jax.random.uniform(k5, (E, E), jnp.float32)
        sim = (sim + sim.T) / 2.0
        sim = sim.at[jnp.arange(E), jnp.arange(E)].set(1.0)
        return {'hidden_states': hidden_states, 'gate_weight': gate_weight, 'gate_up_proj': gate_up_proj, 'down_proj': down_proj, 'similarity_matrix': sim}
    _L0_ffn_in = _L0_ffn_setup()
    _d = {'L0_attn_x': _L0_attn_in['x'], 'L0_attn_Wq_down': _L0_attn_in['Wq_down'], 'L0_attn_Wk_down': _L0_attn_in['Wk_down'], 'L0_attn_Wv_down': _L0_attn_in['Wv_down'], 'L0_attn_Wq_up_c': _L0_attn_in['Wq_up_c'], 'L0_attn_Wq_up_e': _L0_attn_in['Wq_up_e'], 'L0_attn_Wk_up_c': _L0_attn_in['Wk_up_c'], 'L0_attn_Wk_up_e': _L0_attn_in['Wk_up_e'], 'L0_attn_Wv_up': _L0_attn_in['Wv_up'], 'L0_attn_Wc': _L0_attn_in['Wc'], 'L0_ffn_gate_weight': _L0_ffn_in['gate_weight'], 'L0_ffn_gate_up_proj': _L0_ffn_in['gate_up_proj'], 'L0_ffn_down_proj': _L0_ffn_in['down_proj'], 'L0_ffn_similarity_matrix': _L0_ffn_in['similarity_matrix']}
    _x0 = _d['L0_attn_x']
    _d['L0_attn_x'] = jax.random.normal(jax.random.fold_in(jax.random.key(seed), 1), (4, 1024, 256), dtype=_x0.dtype)
    del _x0
    return _d

def reference(L0_attn_x, L0_attn_Wq_down, L0_attn_Wk_down, L0_attn_Wv_down, L0_attn_Wq_up_c, L0_attn_Wq_up_e, L0_attn_Wk_up_c, L0_attn_Wk_up_e, L0_attn_Wv_up, L0_attn_Wc, L0_ffn_gate_weight, L0_ffn_gate_up_proj, L0_ffn_down_proj, L0_ffn_similarity_matrix):

    def _L0_attn_ref(x, Wq_down, Wk_down, Wv_down, Wq_up_c, Wq_up_e, Wk_up_c, Wk_up_e, Wv_up, Wc):
        import jax, jax.numpy as jnp
        import numpy as np
        import math
        B, T, C = (2, 512, 256)
        H, L = (16, 64)
        DH = C // H
        DHE = DH // 2
        THETA = 10000.0

        def _rope_cache(t, dim):
            inv_freq = 1.0 / THETA ** (jnp.arange(0, dim, 2, dtype=jnp.float32) / dim)
            freqs = jnp.arange(t, dtype=jnp.float32)[:, None] * inv_freq[None, :]
            emb = jnp.concatenate((freqs, freqs), axis=-1)
            return (jnp.cos(emb), jnp.sin(emb))

        def _apply_rope(x, cos, sin):
            x1 = x[..., 0::2]
            x2 = x[..., 1::2]
            rot = jnp.stack((-x2, x1), axis=-1).reshape(x.shape)
            return x * cos[None, None] + rot * sin[None, None]
        b, t, c = x.shape
        q_lat = (x @ Wq_down).reshape(b, t, H, L)
        k_lat = (x @ Wk_down).reshape(b, t, H, L)
        v_lat = (x @ Wv_down).reshape(b, t, H, L)
        q_c = jnp.einsum('bthl,ld->bhtd', q_lat, Wq_up_c)
        q_e = jnp.einsum('bthl,ld->bhtd', q_lat, Wq_up_e)
        k_c = jnp.einsum('bthl,ld->bhtd', k_lat, Wk_up_c)
        k_e = jnp.einsum('bthl,ld->bhtd', k_lat, Wk_up_e)
        v = jnp.einsum('bthl,ld->bhtd', v_lat, Wv_up)
        cos, sin = _rope_cache(t, DHE)
        q = jnp.concatenate([q_c, _apply_rope(q_e, cos, sin)], axis=-1)
        k = jnp.concatenate([k_c, _apply_rope(k_e, cos, sin)], axis=-1)
        scale = 1.0 / math.sqrt(DH)
        scores = jnp.einsum('bhqd,bhkd->bhqk', q, k) * scale
        causal = jnp.tril(jnp.ones((t, t), dtype=bool))
        scores = jnp.where(causal[None, None], scores, -jnp.inf)
        att = jax.nn.softmax(scores, axis=-1)
        y = jnp.einsum('bhqk,bhkd->bhqd', att, v)
        y = y.transpose(0, 2, 1, 3).reshape(b, t, c)
        return y @ Wc

    def _L0_ffn_ref(hidden_states, gate_weight, gate_up_proj, down_proj, similarity_matrix):
        import jax, jax.numpy as jnp
        import numpy as np
        E = 8
        K = 2
        S = 1
        THRESHOLD = 0.7
        NORM_TOPK = True
        H = 256
        F = 256
        B, SEQ = (2, 256)
        b, s, h = hidden_states.shape
        x = hidden_states.reshape(-1, h)
        N = x.shape[0]
        logits = x @ gate_weight.T
        probs = jax.nn.softmax(logits.astype(jnp.float32), axis=-1)
        top_w, top_i = jax.lax.top_k(probs, K)
        if NORM_TOPK:
            top_w = top_w / jnp.clip(jnp.sum(top_w, -1, keepdims=True), 1e-12)
        primary_mask = jnp.zeros((E,), bool).at[top_i[:, :S].reshape(-1)].set(True)
        sim = jnp.where(primary_mask[None, :], similarity_matrix.astype(jnp.float32), -jnp.inf)
        best_j = jnp.argmax(sim, axis=-1)
        best_sim = jnp.max(sim, axis=-1)
        ids = jnp.arange(E)
        expert_map = jnp.where(~primary_mask & (best_sim >= THRESHOLD), best_j, ids)
        rerouted = expert_map[top_i]
        rows = jnp.arange(N)[:, None]
        dense = jnp.zeros((N, E), top_w.dtype).at[rows, rerouted].add(top_w)
        fw, fi = jax.lax.top_k(dense, K)
        combine = jnp.zeros((N, E), fw.dtype).at[rows, fi].add(jnp.where(fw > 0, fw, 0.0))
        gu = jnp.einsum('nh,efh->enf', x, gate_up_proj)
        g, u = jnp.split(gu, 2, axis=-1)
        hmid = jax.nn.silu(g) * u
        y = jnp.einsum('enf,ehf->enh', hmid, down_proj)
        out = jnp.einsum('ne,enh->nh', combine, y)
        return out.reshape(b, s, h)
    x = L0_attn_x
    x = x + 0.5 * _L0_ffn_ref(_layernorm(x, axis=-1), L0_ffn_gate_weight, L0_ffn_gate_up_proj, L0_ffn_down_proj, L0_ffn_similarity_matrix)
    x = x + _L0_attn_ref(_layernorm(x, axis=-1), L0_attn_Wq_down, L0_attn_Wk_down, L0_attn_Wv_down, L0_attn_Wq_up_c, L0_attn_Wq_up_e, L0_attn_Wk_up_c, L0_attn_Wk_up_e, L0_attn_Wv_up, L0_attn_Wc)
    x = x + 0.5 * _L0_ffn_ref(_layernorm(x, axis=-1), L0_ffn_gate_weight, L0_ffn_gate_up_proj, L0_ffn_down_proj, L0_ffn_similarity_matrix)
    return x

_drawn_inputs = setup_inputs


def setup_inputs(seed=0):
    import zlib

    import numpy as np

    out = dict(_drawn_inputs(seed))
    spreads = {}
    factors = {'L0_attn_Wq_down': 8.0,
     'L0_attn_Wk_down': 8.0,
     'L0_attn_Wv_down': 8.0,
     'L0_attn_Wq_up_c': 8.0,
     'L0_attn_Wq_up_e': 8.0,
     'L0_attn_Wk_up_c': 8.0,
     'L0_attn_Wk_up_e': 8.0,
     'L0_attn_Wv_up': 8.0,
     'L0_attn_Wc': 8.0,
     'L0_ffn_gate_weight': 5.385,
     'L0_ffn_gate_up_proj': 4.69,
     'L0_ffn_down_proj': 4.69}
    for name, (base, spread) in spreads.items():
        noise = np.random.default_rng([zlib.crc32(name.encode()), seed]).standard_normal(out[name].shape)
        drawn = base * np.exp(spread * noise) if base else spread * noise
        out[name] = jnp.asarray(drawn.astype(out[name].dtype))
    for name, factor in factors.items():
        out[name] = (out[name] * factor).astype(out[name].dtype)
    return out
```

```python
from contextlib import ExitStack

import numpy as np

import concourse.bass as bass
import concourse.mybir as mybir

F32 = mybir.dt.float32
F32R = mybir.dt.float32r
BF16 = mybir.dt.bfloat16
I32 = mybir.dt.int32
U32 = mybir.dt.uint32
ALU = mybir.AluOpType
ACT = mybir.ActivationFunctionType
AX = mybir.AxisListType

P = 128
EPS = 1e-5
THRESHOLD = 0.7
BIG = 1e30


class Shapes:

    def __init__(self, x, gate_up, H=16):
        self.B, self.T, self.C = x.shape
        self.N = self.B * self.T
        self.NT = self.N // P
        self.E, f2, _ = gate_up.shape
        self.F = f2 // 2
        self.K = 2
        self.NB = -(-(self.K * self.N // P + self.E - 1) // 4) * 4
        self.CC = self.C // P
        self.H = H
        self.DH = self.C // H
        assert self.C == 256 and self.F == 256 and self.NT % 8 == 0 and self.NB <= P


def at_least(engine, sem, value):
    if not isinstance(value, int) or value > 0:
        engine.wait_ge(sem, value)


def ahead(engine, sem, n):
    engine.sem_inc(sem, n)


def wait_apart(engine, sem, value, passed):
    engine.wait_ge(sem, value)
    engine.sem_inc(passed, 1)


class Seq:

    def __init__(self, engine, sem):
        self.engine, self.sem, self.n = engine, sem, 0

    def then(self, instruction):
        self.n += 1
        instruction.then_inc(self.sem, 1)
        self.engine.wait_ge(self.sem, self.n)


def bcast(ap, shape):
    return ap.to_broadcast(shape)


def load_weights(nc, sh, name, gu_d, dn_d, wgu, wdn, passed):
    E, CC, F, C = sh.E, sh.CC, sh.F, sh.C
    with ExitStack() as ctx:
        sb = lambda n, s, d=F32: ctx.enter_context(nc.sbuf_tensor(f"{name}_{n}", s, d))
        sem = lambda n: ctx.enter_context(nc.semaphore(f"{name}_{n}"))
        stage = [sb(f"w_stage{j}", [P, CC * (2 * F + C)]) for j in range(2)]
        loaded = [sem(f"w_loaded{j}") for j in range(2)]
        hi_done, lo_done = sem("w_hi_done"), sem("w_lo_done")
        ng = CC * 2 * F
        block = ctx.enter_context(nc.Block(f"{name}_weights"))

        @block.sync
        def _(sp):
            ahead(sp, lo_done, 2 + 1)
            with sp.Fori(0, E // 2) as i:
                for j in range(2):
                    wait_apart(sp, lo_done, 2 * (2 * i + j) + 1, passed)
                    sp.dma_start(stage[j][:, 0:ng].rearrange("p (c f) -> p c f", c=CC),
                                 gu_d[bass.ds(i * 2 + j, 1), :, :].rearrange("e (c p) f -> p (e c) f", p=P)
                                 ).then_inc(loaded[j], 16)
                    sp.dma_start(stage[j][:, ng:].rearrange("p (c f) -> p c f", c=CC),
                                 dn_d[bass.ds(i * 2 + j, 1), :, :].rearrange("e (c p) f -> p (e c) f", p=P)
                                 ).then_inc(loaded[j], 16)

        def parts(j, i):
            yield stage[j][:, 0:ng], [w[:, bass.ds((i * 2 + j) * ng, ng)] for w in wgu]
            yield stage[j][:, ng:], [w[:, bass.ds((i * 2 + j) * CC * C, CC * C)] for w in wdn]

        @block.scalar
        def _(act):
            with act.Fori(0, E // 2) as i:
                for j in range(2):
                    act.wait_ge(loaded[j], 32 * i + 32)
                    for src, (hi, _) in parts(j, i):
                        act.activation(hi, src, ACT.Copy).then_inc(hi_done, 1)

        @block.vector
        def _(dve):
            with dve.Fori(0, E // 2) as i:
                for j in range(2):
                    dve.wait_ge(loaded[j], 32 * i + 32)
                    for n, (src, (hi, lo)) in enumerate(parts(j, i)):
                        dve.wait_ge(hi_done, 2 * (2 * i + j) + n + 1)
                        dve.tensor_tensor(lo, src, hi.bitcast(F32), ALU.subtract).then_inc(lo_done, 1)


def moe(nc, sh, name, X, x_d, out_d, gate_d, sim_d, xn_d, ys_d, wgu, wdn, consts, passed):
    NT, E, C, F, CC, NB = sh.NT, sh.E, sh.C, sh.F, sh.CC, sh.NB
    G = 8
    NG = NT // G
    ctx = ExitStack()
    with ctx:
        sb = lambda n, s, d=F32: ctx.enter_context(nc.sbuf_tensor(f"{name}_{n}", s, d))
        sem = lambda n: ctx.enter_context(nc.semaphore(f"{name}_{n}"))
        weight = sb("weight", [P, 2, NT])
        pos_u = sb("pos_u", [P, NT, 2], U32)
        slot_u = sb("slot_u", [P, NB], U32)
        block_expert = sb("block_expert", [P, NB], I32)

        with ExitStack() as c1:
            sb1 = lambda n, s, d=F32: c1.enter_context(nc.sbuf_tensor(f"{name}_{n}", s, d))
            ps1 = lambda n, s, d=F32: c1.enter_context(nc.psum_tensor(f"{name}_{n}", s, d))
            sem1 = lambda n: c1.enter_context(nc.semaphore(f"{name}_{n}"))
            logits = ps1("logits", [P, 512])
            with ExitStack() as c2:
                sb2 = lambda n, s, d=F32: c2.enter_context(nc.sbuf_tensor(f"{name}_{n}", s, d))
                XN = [sb2(f"XN{j}", [P, G, C]) for j in range(2)]
                gate = sb2("gate", [P, CC, E])
                stats = sb2("stats", [P, G, 6])
                mv = sb2("mv", [P, G, 2])
                std, rstd = sb2("std", [P, G]), sb2("rstd", [P, G])
                xT = [sb2(f"xT{r}", [P, 2, CC, P]) for r in range(2)]
                psT = [c2.enter_context(nc.psum_tensor(f"{name}_psT{r}", [P, 2, CC, P], F32)) for r in range(2)]
                sem2 = lambda n: c2.enter_context(nc.semaphore(f"{name}_{n}"))
                x_in = [sem2(f"x_in{j}") for j in range(2)]
                xn_out = [sem2(f"xn_out{j}") for j in range(2)]
                gate_in, dv, xn_ready, std_done = (sem2(n) for n in ("gate_in", "dv", "xn_ready", "std_done"))
                turned, evacuated, scored = sem2("turned"), sem2("evacuated"), sem2("scored")
                x_t = x_d.rearrange("(t p) c -> p t c", p=P) if x_d is not None else None
                xn_t = xn_d.rearrange("(t p) c -> p t c", p=P)
                NI = NG // 2
                ND = 2 * G + 1
                block = c2.enter_context(nc.Block(f"{name}_norm"))

                @block.sync
                def _(sp):
                    sp.dma_start(gate[:, :, :], gate_d.rearrange("(c p) e -> p c e", p=P)).then_inc(gate_in, 16)
                    with sp.Fori(0, NI) as i:
                        for j in range(2 if x_d is not None else 0):
                            sp.dma_start(X[:, bass.ds((2 * i + j) * G, G), :],
                                         x_t[:, bass.ds((2 * i + j) * G, G), :]).then_inc(x_in[j], 16)
                        for j in range(2):
                            wait_apart(sp, xn_ready, (2 * i + j) * G + G, passed)
                            sp.dma_start(xn_t[:, bass.ds((2 * i + j) * G, G), :],
                                         XN[j][:, :, :]).then_inc(xn_out[j], 16)
                    for j in range(2):
                        sp.wait_ge(xn_out[j], 16 * NI + 1)

                @block.vector
                def _(dve):
                    ahead(dve, turned, G // 2 + 1)
                    for j in range(2):
                        ahead(dve, xn_out[j], 1)
                    with dve.Fori(0, NI) as i:
                        for j in range(2):
                            g = 2 * i + j
                            if x_d is not None:
                                dve.wait_ge(x_in[j], 16 * i + 16)
                            for k in range(G):
                                dve.bn_stats(stats[:, k, :], X[:, bass.ds(g * G + k, 1), :].rearrange("p a c -> p (a c)")
                                             ).then_inc(dv, 1)
                            for k in range(G):
                                wait_apart(dve, dv, g * ND + k + 1, passed)
                                dve.bn_aggr(mv[:, k, :], stats[:, k, :]).then_inc(dv, 1)
                            dve.wait_ge(std_done, g + 1)
                            dve.reciprocal(rstd[:, :], std[:, :]).then_inc(dv, 1)
                            dve.wait_ge(dv, g * ND + ND)
                            dve.wait_ge(xn_out[j], 16 * i + 1)
                            dve.wait_ge(turned, G // 2 * (2 * i + j) + 1)
                            for k in range(G):
                                dve.tensor_scalar(XN[j][:, k, :], X[:, bass.ds(g * G + k, 1), :].rearrange("p a c -> p (a c)"),
                                                  mv[:, k, 0:1], rstd[:, k:k + 1], ALU.subtract, ALU.mult
                                                  ).then_inc(xn_ready, 1)

                @block.tensor
                def _(pe):
                    pe.wait_ge(gate_in, 16)
                    ahead(pe, evacuated, 1 + 1)
                    NP = G

                    def turn(i, p):
                        j, k = p // (G // 2), 2 * (p % (G // 2))
                        q = i * NP + p
                        pe.wait_ge(xn_ready, q * 2 + 2)
                        pe.wait_ge(evacuated, q + 1)
                        for a in range(2):
                            for c in range(CC):
                                m = pe.transpose(psT[p % 2][:, a, c, :], XN[j][:, k + a, c * P:(c + 1) * P],
                                                 consts["ident"][:, :])
                        m.then_inc(turned, 1)

                    def score(i, p):
                        q = i * NP + p
                        pe.wait_ge(evacuated, q + 3)
                        for a in range(2):
                            for c in range(CC):
                                m = pe.matmul(logits[:, bass.ds((q * 2 + a) * E, E)], xT[p % 2][:, a, c, :],
                                              gate[:, c, :], start=(c == 0), stop=(c == CC - 1))
                        m.then_inc(scored, 1)

                    with pe.Fori(0, NI) as i:
                        for p in range(NP + 1):
                            if p < NP:
                                turn(i, p)
                            if p:
                                score(i, p - 1)

                @block.scalar
                def _(act):
                    ahead(act, scored, 1 + 1)
                    with act.Fori(0, NI) as i:
                        for p in range(G):
                            q = i * G + p
                            if p % (G // 2) == 0:
                                g = 2 * i + p // (G // 2)
                                act.wait_ge(dv, g * ND + 2 * G)
                                act.activation(std[:, :], mv[:, :, 1], ACT.Sqrt, bias=consts["eps"][:, 0:1]
                                               ).then_inc(std_done, 1)
                            act.wait_ge(turned, q + 2 + G // 2)
                            act.wait_ge(scored, q + 1)
                            act.activation(xT[p % 2][:, :, :, :].rearrange("p a c n -> p (a c n)"),
                                           psT[p % 2][:, :, :, :].rearrange("p a c n -> p (a c n)"),
                                           ACT.Copy).then_inc(evacuated, 1)

            TE = [P, NT, E]
            t3 = lambda n: sb1(n, TE)
            t2 = lambda n: sb1(n, [P, NT])
            t1 = lambda n, d=F32: sb1(n, [P, E], d)
            z, ez, prob, prob2, eq, cand = t3("z"), t3("ez"), t3("prob"), t3("prob2"), t3("eq"), t3("cand")
            one_hot = [t3("one_hot0"), t3("one_hot1")]
            routed = [t3("routed0"), t3("routed1")]
            total, rtotal, top = t2("total"), t2("rtotal"), [t2("top0"), t2("top1")]
            first, both = t2("first"), t2("both")
            wide = sb1("wide", [P, NT, E, E])
            count = t3("count")
            cum = [t3("cum0"), t3("cum1")]
            before = t3("before")
            pos = sb1("pos", [P, NT, 2])
            sim = sb1("sim", [P, E, E])
            simm, eqs, moved, remap = (sb1(n, [P, E, E]) for n in ("simm", "eqs", "moved", "remap"))
            primary, gap, best, best_j, use, stay = (t1(n) for n in ("primary", "gap", "best", "best_j", "use", "stay"))
            counts1 = t1("counts1")
            nblk_i, nblk_j = t1("nblk_i", I32), t1("nblk_j", I32)
            blocks = [t1("blocks0"), t1("blocks1"), t1("blocks2")]
            starts = t1("starts")
            started = sb1("started", [P, NB, E - 1])
            be_f = sb1("be_f", [P, NB])
            pos_i = sb1("pos_i", [P, NT, 2], I32)
            lohi_i = [sb1(f"lohi_i{k}", [P, NT, 2], I32) for k in range(2)]
            lohi = [sb1(f"lohi{k}", [P, NT, 2]) for k in range(2)]
            oh_lo = [sb1(f"oh_lo{r}", [P, 8, P], BF16) for r in range(2)]
            oh_hi = [sb1(f"oh_hi{r}", [P, 8, NB], BF16) for r in range(2)]
            oh_tp = [sb1(f"oh_tp{r}", [P, 8, 2, NB], BF16) for r in range(2)]
            slot_p = sb1("slot_p", [P, NB])
            counts_ps = ps1("counts_ps", [P, E])
            prefix_ps = ps1("prefix_ps", [P, 2, NT, E])
            slots_ps = ps1("slots_ps", [P, 2, NB])
            sim_in, dvs, z_ready, ez_ready = sem1("sim_in"), sem1("dvs"), sem1("z_ready"), sem1("ez_ready")
            counted, summed = sem1("counted"), sem1("summed")
            oh_ready, oh_used, rb = sem1("oh_ready"), sem1("oh_used"), sem1("rb")
            iota_e, iota_e8, iota_f, iota_b, eye_e, t_idx, p_idx = (
                consts[k] for k in ("iota_e", "iota_e8", "iota_f", "iota_b", "eye_e", "t_idx", "p_idx"))
            block = c1.enter_context(nc.Block(f"{name}_route"))
            lg = logits[:, 0:NT * E].rearrange("p (t e) -> p t e", e=E)
            over_e = lambda a: a.unsqueeze(2).to_broadcast([P, NT, E])
            over_t = lambda a: a.unsqueeze(1).to_broadcast([P, NT, E])

            @block.sync
            def _(sp):
                sp.dma_start(sim[:, :, :], sim_d.unsqueeze(0).to_broadcast([P, E, E])).then_inc(sim_in, 16)

            @block.scalar
            def _(act):
                act.wait_ge(z_ready, 1)
                act.activation(ez[:, :, :], z[:, :, :], ACT.Exp).then_inc(ez_ready, 1)

            NQ = NT * 2 // 8

            @block.tensor
            def _(pe):
                pe.wait_ge(counted, 1)
                pe.matmul(counts_ps[:, :], consts["ones"][:, :], counts1[:, :], start=True, stop=True).then_inc(summed, 1)
                pe.wait_ge(counted, 2)
                flat = count[:, :, :].rearrange("p t e -> p (t e)")
                pe.matmul(prefix_ps[:, 0, :, :].rearrange("p t e -> p (t e)"), consts["upper"][:, :], flat,
                          start=True, stop=True)
                pe.matmul(prefix_ps[:, 1, :, :].rearrange("p t e -> p (t e)"), consts["ones"][:, :], flat,
                          start=True, stop=True).then_inc(summed, 1)

                def group(q, r, first_group, last_group):
                    pe.wait_ge(oh_ready, q + 1)
                    for a in range(8):
                        m = pe.matmul(slots_ps[:, :, :].rearrange("p a b -> p (a b)"), oh_lo[r][:, a, :],
                                      oh_tp[r][:, a, :, :].rearrange("p a b -> p (a b)"),
                                      start=first_group and a == 0, stop=last_group and a == 7)
                    m.then_inc(oh_used, 1)

                group(0, 0, True, False)
                group(1, 1, False, False)
                with pe.Fori(1, NQ // 2 - 1) as i:
                    group(2 * i, 0, False, False)
                    group(2 * i + 1, 1, False, False)
                group(NQ - 2, 0, False, False)
                group(NQ - 1, 1, False, True)

            @block.vector
            def _(dve):
                seq = Seq(dve, dvs)
                T = seq.then

                def argfirst(out, source, value, eqt, candt, shape, over, iotas):
                    T(dve.tensor_tensor(eqt, source, value, ALU.is_equal))
                    T(dve.scalar_tensor_tensor(candt, eqt, -float(E), iotas, ALU.mult, ALU.add))
                    T(dve.tensor_reduce(out, candt, AX.X, ALU.min))

                T(dve.tensor_reduce(total[:, :], lg, AX.X, ALU.max))
                dve.tensor_tensor(z[:, :, :], lg, over_e(total[:, :]), ALU.subtract).then_inc(z_ready, 1)
                dve.wait_ge(ez_ready, 1)
                T(dve.tensor_reduce(total[:, :], ez[:, :, :], AX.X, ALU.add))
                T(dve.reciprocal(rtotal[:, :], total[:, :]))
                T(dve.tensor_tensor(prob[:, :, :], ez[:, :, :], over_e(rtotal[:, :]), ALU.mult))
                for k, source in enumerate((prob, prob2)):
                    T(dve.tensor_reduce(top[k][:, :], source[:, :, :], AX.X, ALU.max))
                    argfirst(first[:, :], source[:, :, :], over_e(top[k][:, :]), eq[:, :, :], cand[:, :, :], TE,
                             over_e, over_t(iota_e8[:, :]))
                    T(dve.tensor_tensor(one_hot[k][:, :, :], over_t(iota_e[:, :]), over_e(first[:, :]), ALU.is_equal))
                    if k == 0:
                        T(dve.scalar_tensor_tensor(prob2[:, :, :], one_hot[0][:, :, :], -2.0, prob[:, :, :],
                                                   ALU.mult, ALU.add))
                T(dve.tensor_reduce(counts1[:, :], one_hot[0][:, :, :].rearrange("p t e -> p e t"), AX.X, ALU.add))
                dve.engine_nop().then_inc(counted, 1)
                T(dve.tensor_tensor(both[:, :], top[0][:, :], top[1][:, :], ALU.add))
                T(dve.tensor_scalar(both[:, :], both[:, :], 1e-12, None, ALU.max))
                T(dve.reciprocal(rtotal[:, :], both[:, :]))
                for k in range(2):
                    T(dve.scalar_tensor_tensor(weight[:, k, :], top[k][:, :], 0.5, rtotal[:, :], ALU.mult, ALU.mult))
                dve.wait_ge(sim_in, 16)
                dve.wait_ge(summed, 1)
                T(dve.tensor_scalar(primary[:, :], counts_ps[:, :], 0.0, None, ALU.is_gt))
                T(dve.tensor_scalar(gap[:, :], primary[:, :], BIG, -BIG, ALU.mult, ALU.add))
                by_j = lambda a: a.unsqueeze(1).to_broadcast([P, E, E])
                by_e = lambda a: a.unsqueeze(2).to_broadcast([P, E, E])
                T(dve.tensor_tensor(simm[:, :, :], sim[:, :, :], by_j(primary[:, :]), ALU.mult))
                T(dve.tensor_tensor(simm[:, :, :], simm[:, :, :], by_j(gap[:, :]), ALU.add))
                T(dve.tensor_reduce(best[:, :], simm[:, :, :], AX.X, ALU.max))
                argfirst(best_j[:, :], simm[:, :, :], by_e(best[:, :]), eqs[:, :, :], moved[:, :, :], None, None,
                         by_j(iota_e8[:, :]))
                T(dve.tensor_scalar(use[:, :], best[:, :], THRESHOLD, None, ALU.is_ge))
                T(dve.tensor_scalar(stay[:, :], primary[:, :], -1.0, 1.0, ALU.mult, ALU.add))
                T(dve.tensor_tensor(use[:, :], use[:, :], stay[:, :], ALU.mult))
                T(dve.tensor_scalar(stay[:, :], use[:, :], -1.0, 1.0, ALU.mult, ALU.add))
                T(dve.tensor_tensor(moved[:, :, :], by_e(iota_e[:, :]), by_j(best_j[:, :]), ALU.is_equal))
                T(dve.tensor_tensor(moved[:, :, :], moved[:, :, :], by_j(use[:, :]), ALU.mult))
                T(dve.tensor_tensor(remap[:, :, :], eye_e[:, :, :], by_j(stay[:, :]), ALU.mult))
                T(dve.tensor_tensor(remap[:, :, :], remap[:, :, :], moved[:, :, :], ALU.add))
                for k in range(2):
                    T(dve.tensor_tensor(wide[:, :, :, :], one_hot[k][:, :, :].unsqueeze(2).to_broadcast([P, NT, E, E]),
                                        remap[:, :, :].unsqueeze(1).to_broadcast([P, NT, E, E]), ALU.mult))
                    T(dve.tensor_reduce(routed[k][:, :, :], wide[:, :, :, :], AX.X, ALU.add))
                dve.tensor_tensor(count[:, :, :], routed[0][:, :, :], routed[1][:, :, :], ALU.add).then_inc(counted, 1)
                dve.wait_ge(summed, 2)
                T(dve.tensor_copy(cum[0][:, :, :], prefix_ps[:, 1, :, :]))
                a, step = 0, 1
                while step < NT:
                    dve.tensor_copy(cum[1 - a][:, 0:step, :], cum[a][:, 0:step, :])
                    T(dve.tensor_tensor(cum[1 - a][:, step:, :], cum[a][:, step:, :], cum[a][:, 0:NT - step, :], ALU.add))
                    a, step = 1 - a, 2 * step
                T(dve.tensor_scalar(nblk_i[:, :], cum[a][:, NT - 1, :], float(P - 1), None, ALU.add))
                T(dve.tensor_single_scalar(nblk_j[:, :], nblk_i[:, :], 7, ALU.arith_shift_right))
                T(dve.tensor_copy(blocks[0][:, :], nblk_j[:, :]))
                b, step = 1, 1
                T(dve.tensor_copy(blocks[1][:, :], blocks[0][:, :]))
                while step < E:
                    dve.tensor_copy(blocks[3 - b][:, 0:step], blocks[b][:, 0:step])
                    T(dve.tensor_tensor(blocks[3 - b][:, step:], blocks[b][:, step:], blocks[b][:, 0:E - step], ALU.add))
                    b, step = 3 - b, 2 * step
                T(dve.tensor_tensor(starts[:, :], blocks[b][:, :], blocks[0][:, :], ALU.subtract))
                T(dve.tensor_tensor(started[:, :, :], iota_b[:, :].unsqueeze(2).to_broadcast([P, NB, E - 1]),
                                    starts[:, 1:E].unsqueeze(1).to_broadcast([P, NB, E - 1]), ALU.is_ge))
                T(dve.tensor_reduce(be_f[:, :], started[:, :, :], AX.X, ALU.add))
                T(dve.tensor_copy(block_expert[:, :], be_f[:, :]))
                T(dve.tensor_tensor(before[:, :, :], cum[a][:, :, :], prefix_ps[:, 1, :, :], ALU.subtract))
                T(dve.tensor_tensor(before[:, :, :], before[:, :, :], prefix_ps[:, 0, :, :], ALU.add))
                T(dve.tensor_scalar(starts[:, :], starts[:, :], float(P), None, ALU.mult))
                T(dve.tensor_tensor(before[:, :, :], before[:, :, :], over_t(starts[:, :]), ALU.add))
                for k in range(2):
                    T(dve.tensor_tensor(eq[:, :, :], before[:, :, :], routed[k][:, :, :], ALU.mult))
                    T(dve.tensor_reduce(pos[:, :, k], eq[:, :, :], AX.X, ALU.add))
                T(dve.tensor_tensor(eq[:, :, :], routed[0][:, :, :], routed[1][:, :, :], ALU.mult))
                T(dve.tensor_reduce(first[:, :], eq[:, :, :], AX.X, ALU.add))
                T(dve.tensor_tensor(pos[:, :, 1], pos[:, :, 1], first[:, :], ALU.add))
                T(dve.tensor_copy(pos_u[:, :, :], pos[:, :, :]))
                T(dve.tensor_copy(pos_i[:, :, :], pos[:, :, :]))
                T(dve.tensor_single_scalar(lohi_i[0][:, :, :], pos_i[:, :, :], P - 1, ALU.bitwise_and))
                T(dve.tensor_single_scalar(lohi_i[1][:, :, :], pos_i[:, :, :], 7, ALU.arith_shift_right))
                for k in range(2):
                    T(dve.tensor_copy(lohi[k][:, :, :], lohi_i[k][:, :, :]))
                lo, hi, ti = (v.rearrange("p t k -> p (t k)") for v in (lohi[0][:, :, :], lohi[1][:, :, :], t_idx[:, :, :]))
                ahead(dve, oh_used, 1 + 1)
                with dve.Fori(0, NQ // 2) as i:
                    for r in range(2):
                        q = 2 * i + r
                        dve.wait_ge(oh_used, q + 1)
                        dve.tensor_tensor(oh_lo[r][:, :, :], iota_f[:, :].unsqueeze(1).to_broadcast([P, 8, P]),
                                          lo[:, bass.ds(q * 8, 8)].unsqueeze(2).to_broadcast([P, 8, P]), ALU.is_equal)
                        dve.tensor_tensor(oh_hi[r][:, :, :], iota_b[:, :].unsqueeze(1).to_broadcast([P, 8, NB]),
                                          hi[:, bass.ds(q * 8, 8)].unsqueeze(2).to_broadcast([P, 8, NB]),
                                          ALU.is_equal).then_inc(rb, 1)
                        dve.wait_ge(rb, q + 1)
                        dve.tensor_tensor(oh_tp[r][:, :, 0, :], oh_hi[r][:, :, :],
                                          ti[:, bass.ds(q * 8, 8)].unsqueeze(2).to_broadcast([P, 8, NB]), ALU.mult)
                        dve.tensor_scalar(oh_tp[r][:, :, 1, :], oh_hi[r][:, :, :], p_idx[:, 0:1], None,
                                          ALU.mult).then_inc(oh_ready, 1)
                dve.wait_ge(oh_used, NQ + 2)
                T(dve.tensor_copy(slot_p[:, :], slots_ps[:, 1, :]))
                T(dve.scalar_tensor_tensor(slot_u[:, :], slots_ps[:, 0, :], float(P), slot_p[:, :], ALU.mult, ALU.add))

        with ExitStack() as c1:
            sb1 = lambda n, s, d=F32: c1.enter_context(nc.sbuf_tensor(f"{name}_{n}", s, d))
            ps1 = lambda n, s, d=F32: c1.enter_context(nc.psum_tensor(f"{name}_{n}", s, d))
            sem1 = lambda n: c1.enter_context(nc.semaphore(f"{name}_{n}"))
            R = 4
            idx = [sb1(f"idx{j}", [P, 1], U32) for j in range(R)]
            xg = [sb1(f"xg{j}", [P, C]) for j in range(R)]
            y = [sb1(f"y{j}", [P, C]) for j in range(R)]
            x_hi, x_lo, h_hi, h_lo = ([sb1(f"{n}{j}", [P, CC, P], F32R) for j in range(2)]
                                      for n in ("x_hi", "x_lo", "h_hi", "h_lo"))
            act_g, h = ([sb1(f"{n}{j}", [P, F]) for j in range(2)] for n in ("act_g", "h"))
            psX, psH = ([ps1(f"{n}{j}", [P, 4, P])[:, 0:CC, :] for j in range(2)] for n in ("psX", "psH"))
            psG, psY = ([ps1(f"{n}{j}", [P, 512]) for j in range(2)] for n in ("psG", "psY"))
            idx_ready = sem1("idx_ready")
            gathered = [sem1(f"gathered{j}") for j in range(R)]
            stored = [sem1(f"stored{j}") for j in range(R)]
            x_turned, gu_done, h_turned, y_done = (sem1(n) for n in ("x_turned", "gu_done", "h_turned", "y_done"))
            xhi_done, xlo_done, silu_done, h_done = (sem1(n) for n in ("xhi_done", "xlo_done", "silu_done", "h_done"))
            hhi_done, hlo_done, y_copied = (sem1(n) for n in ("hhi_done", "hlo_done", "y_copied"))
            ys_t = ys_d.rearrange("(b p) c -> b p c", p=P)
            block = c1.enter_context(nc.Block(f"{name}_experts"))

            def pipeline(engine, step):
                for k in range(R):
                    step(k, k, k, True)
                with engine.Fori(1, NB // R - 1) as n:
                    for k in range(R):
                        step(n * R + k, k, None, True)
                for k in range(R + 2):
                    step(NB - R + k, k % R, None, k < R)

            @block.gpsimd
            def _(pool):
                ahead(pool, x_turned, R - 1 + 1)
                with pool.Fori(0, NB // R) as n:
                    for j in range(R):
                        i = n * R + j
                        wait_apart(pool, x_turned, i + 1, passed)
                        pool.tensor_copy(idx[j][:, :], slot_u[:, bass.ds(i, 1)]).then_inc(idx_ready, 1)
                        wait_apart(pool, idx_ready, i + 1, passed)
                        pool.indirect_dma_start(xg[j][:, :], None, xn_d[:, :],
                                                bass.IndirectOffsetOnAxis(ap=idx[j][:, 0:1], axis=0)
                                                ).then_inc(gathered[j], 16)

            @block.tensor
            def _(pe):
                def turn_x(i, j, n):
                    at_least(pe, gathered[j], n * 16 + 16)
                    at_least(pe, xhi_done, i - 1)
                    at_least(pe, xlo_done, i - 1)
                    for c in range(CC):
                        m = pe.transpose(psX[j % 2][:, c, :], xg[j][:, c * P:(c + 1) * P], consts["ident"][:, :])
                    m.then_inc(x_turned, 1)

                def three(out, hi, lo, w, at, width):
                    n = 0
                    for s, ww in ((hi, w[0]), (lo, w[0]), (hi, w[1])):
                        for c in range(CC):
                            m = pe.matmul(out, s[:, c, :], ww[:, bass.ds(at + c * width, width)],
                                          start=(n == 0), stop=(n == 3 * CC - 1))
                            n += 1
                    return m

                def step(i, j, k, fresh):
                    head = k if k is not None else 99
                    if fresh:
                        e = pe.value_load(block_expert[0:1, bass.ds(i, 1)], min_val=0, max_val=E - 1)
                        at_least(pe, xhi_done, i + 1)
                        at_least(pe, xlo_done, i + 1)
                        at_least(pe, h_done, i - 1)
                        three(psG[j % 2][:, :], x_hi[j % 2], x_lo[j % 2], wgu, e * (CC * 2 * F), 2 * F).then_inc(gu_done, 1)
                        if not (isinstance(i, int) and i == NB - 1):
                            turn_x(i + 1, (j + 1) % R, (i + 1) // R if isinstance(i, int) else (n_of(i, j, 1)))
                    if head >= 2:
                        e = pe.value_load(block_expert[0:1, bass.ds(i - 2, 1)], min_val=0, max_val=E - 1)
                        at_least(pe, hhi_done, i - 1)
                        at_least(pe, hlo_done, i - 1)
                        at_least(pe, y_copied, i - 3)
                        three(psY[j % 2][:, 0:C], h_hi[j % 2], h_lo[j % 2], wdn, e * (CC * C), C).then_inc(y_done, 1)
                    if head >= 1 and not (isinstance(i, int) and i == NB + 1):
                        at_least(pe, h_done, i)
                        at_least(pe, hhi_done, i - 2)
                        at_least(pe, hlo_done, i - 2)
                        for c in range(CC):
                            m = pe.transpose(psH[(j - 1) % 2][:, c, :], h[(j - 1) % 2][:, c * P:(c + 1) * P],
                                             consts["ident"][:, :])
                        m.then_inc(h_turned, 1)

                loop = {}

                def n_of(i, j, d):
                    return loop["n"] + (1 if j + d >= R else 0)

                turn_x(0, 0, 0)
                for k in range(R):
                    step(k, k, k, True)
                with pe.Fori(1, NB // R - 1) as n:
                    loop["n"] = n
                    for k in range(R):
                        step(n * R + k, k, None, True)
                for k in range(R + 2):
                    step(NB - R + k, k % R, None, k < R)

            @block.scalar
            def _(act):
                def flat(t):
                    return t[:, :, :].rearrange("p c n -> p (c n)")

                def x_part(i, j):
                    at_least(act, x_turned, i + 1 + R)
                    act.activation(flat(x_hi[j % 2]), psX[j % 2].rearrange("p c n -> p (c n)"), ACT.Copy
                                   ).then_inc(xhi_done, 1)

                def step(i, j, k, fresh):
                    head = k if k is not None else 99
                    if fresh:
                        at_least(act, gu_done, i + 1)
                        act.activation(act_g[j % 2][:, :], psG[j % 2][:, 0:F], ACT.Silu).then_inc(silu_done, 1)
                        if not (isinstance(i, int) and i == NB - 1):
                            x_part(i + 1, j + 1)
                    if head >= 2:
                        at_least(act, y_done, i - 1)
                        if head == 99:
                            at_least(act, stored[(j - 2) % R], ybase(i, j))
                        act.activation(y[(j - 2) % R][:, :], psY[j % 2][:, 0:C], ACT.Copy).then_inc(y_copied, 1)
                    if head >= 1 and not (isinstance(i, int) and i == NB + 1):
                        at_least(act, h_turned, i)
                        act.activation(flat(h_hi[(j - 1) % 2]), psH[(j - 1) % 2].rearrange("p c n -> p (c n)"),
                                       ACT.Copy).then_inc(hhi_done, 1)

                loop = {}

                def ybase(i, j):
                    if isinstance(i, int):
                        return (i - 2) // R * 16
                    return loop["n"] * 16 - (16 if j < 2 else 0)

                x_part(0, 0)
                for k in range(R):
                    step(k, k, k, True)
                with act.Fori(1, NB // R - 1) as n:
                    loop["n"] = n
                    for k in range(R):
                        step(n * R + k, k, None, True)
                for k in range(R + 2):
                    step(NB - R + k, k % R, None, k < R)

            @block.vector
            def _(dve):
                def flat(t):
                    return t[:, :, :].rearrange("p c n -> p (c n)")

                def rest(out, ps, hi, done):
                    dve.tensor_tensor(flat(out), ps.rearrange("p c n -> p (c n)"), flat(hi).bitcast(F32),
                                      ALU.subtract).then_inc(done, 1)

                def step(i, j, k, fresh):
                    head = k if k is not None else 99
                    if fresh:
                        at_least(dve, silu_done, i + 1)
                        dve.tensor_tensor(h[j % 2][:, :], act_g[j % 2][:, :], psG[j % 2][:, F:2 * F], ALU.mult
                                          ).then_inc(h_done, 1)
                        if not (isinstance(i, int) and i == NB - 1):
                            at_least(dve, xhi_done, i + 2)
                            rest(x_lo[(j + 1) % 2], psX[(j + 1) % 2], x_hi[(j + 1) % 2], xlo_done)
                    if head >= 1 and not (isinstance(i, int) and i == NB + 1):
                        at_least(dve, hhi_done, i)
                        rest(h_lo[(j - 1) % 2], psH[(j - 1) % 2], h_hi[(j - 1) % 2], hlo_done)

                at_least(dve, xhi_done, 1)
                rest(x_lo[0], psX[0], x_hi[0], xlo_done)
                pipeline(dve, step)

            @block.sync
            def _(sp):
                with sp.Fori(0, NB // R) as n:
                    for j in range(R):
                        wait_apart(sp, y_copied, n * R + j + 1, passed)
                        sp.dma_start(ys_t[bass.ds(n * R + j, 1), :, :].rearrange("b p c -> (b p) c"), y[j][:, :]
                                     ).then_inc(stored[j], 16)
                for j in range(R):
                    sp.wait_ge(stored[j], 16 * (NB // R))

        with ExitStack() as c1:
            sb1 = lambda n, s, d=F32: c1.enter_context(nc.sbuf_tensor(f"{name}_{n}", s, d))
            sem1 = lambda n: c1.enter_context(nc.semaphore(f"{name}_{n}"))
            R = 4
            cidx = [[sb1(f"cidx{k}{j}", [P, 1], U32) for j in range(R)] for k in range(2)]
            yg = [[sb1(f"yg{k}{j}", [P, C]) for j in range(R)] for k in range(2)]
            half = [sb1(f"half{j}", [P, C]) for j in range(R)]
            cidx_ready, half_done, o_done = sem1("cidx_ready"), sem1("half_done"), sem1("o_done")
            got = [sem1(f"got{j}") for j in range(R)]
            o_out = sem1("o_out")
            out_t = out_d.rearrange("(t p) c -> p t c", p=P) if out_d is not None else None
            block = c1.enter_context(nc.Block(f"{name}_combine"))

            @block.gpsimd
            def _(pool):
                ahead(pool, o_done, R - 1 + 1)
                with pool.Fori(0, NT // R) as n:
                    for j in range(R):
                        t = n * R + j
                        wait_apart(pool, o_done, t + 1, passed)
                        for k in range(2):
                            pool.tensor_copy(cidx[k][j][:, :], pos_u[:, bass.ds(t, 1), k]).then_inc(cidx_ready, 1)
                        for k in range(2):
                            wait_apart(pool, cidx_ready, 2 * t + k + 1, passed)
                            pool.indirect_dma_start(yg[k][j][:, :], None, ys_d[:, :],
                                                    bass.IndirectOffsetOnAxis(ap=cidx[k][j][:, 0:1], axis=0)
                                                    ).then_inc(got[j], 16)

            @block.vector
            def _(dve):
                with dve.Fori(0, NT // R) as n:
                    for j in range(R):
                        t = n * R + j
                        dve.wait_ge(got[j], 32 * n + 32)
                        dve.scalar_tensor_tensor(half[j][:, :], yg[0][j][:, :], weight[:, 0, bass.ds(t, 1)],
                                                 X[:, bass.ds(t, 1), :].rearrange("p a c -> p (a c)"),
                                                 ALU.mult, ALU.add).then_inc(half_done, 1)
                        dve.wait_ge(half_done, t + 1)
                        dve.scalar_tensor_tensor(X[:, bass.ds(t, 1), :].rearrange("p a c -> p (a c)"), yg[1][j][:, :], weight[:, 1, bass.ds(t, 1)],
                                                 half[j][:, :], ALU.mult, ALU.add).then_inc(o_done, 1)

            @block.sync
            def _(sp):
                if out_d is None:
                    return
                with sp.Fori(0, NT // R) as n:
                    wait_apart(sp, o_done, n * R + 2 * R, passed)
                    sp.dma_start(out_t[:, bass.ds(n * R, R), :], X[:, bass.ds(n * R, R), :]).then_inc(o_out, 16)
                sp.wait_ge(o_out, 16 * (NT // R))


class Walk:

    START = 4

    def __init__(self, me, engine, sems, passed, count=None):
        self.me, self.engine, self.sems, self.passed = me, engine, sems, passed
        self.count = dict(count) if count else {s: 0 for s in sems}
        self.turn, self.per_turn = None, {}

    def on(self, name):
        return name == self.me

    def wait(self, sem, back=0, apart=False):
        if self.me is None:
            return
        n = self.count[sem] - back
        if self.turn is None or not self.per_turn[sem]:
            if n > 0:
                self.engine.wait_ge(self.sems[sem], n + self.START)
            return
        assert n + self.START > 0, (sem, n)
        value = self.turn * self.per_turn[sem] + (n + self.START)
        if apart or self.me in ("pool", "sp"):
            wait_apart(self.engine, self.sems[sem], value, self.passed)
        else:
            self.engine.wait_ge(self.sems[sem], value)

    def do(self, name, sem, make, by=1):
        self.count[sem] += by
        if self.on(name):
            make().then_inc(self.sems[sem], by)

    def turns(self, n, body):
        before, me = dict(self.count), self.me
        self.me = None
        body(0)
        self.per_turn = {s: self.count[s] - before[s] for s in self.count}
        self.me, self.count = me, dict(before)
        if me is not None:
            with self.engine.Fori(0, n) as i:
                self.turn = i
                body(i)
        self.turn = None
        self.count = {s: before[s] + n * self.per_turn[s] for s in before}


def attention(nc, sh, X, w_d, up_d, wc_d, rope_d, consts, passed):
    B, T, C, CC, H, NT = sh.B, sh.T, sh.C, sh.CC, sh.H, sh.NT
    DH, D2 = sh.DH, sh.DH // 2
    NTB = T // P
    PR = H // 2
    G = B * PR
    HALF = 512
    NH = T // HALF
    assert NTB == 8 and NH == 2 and DH == 16 and C == H * DH and G % 2 == 0
    QKW = 2 * C
    scale = float(DH) ** -0.5
    ident = consts["ident"]
    names = ("norm", "std_done", "rstd_done", "xn_done", "turned", "xhi_done", "xlo_done", "projected", "copied",
             "rot0", "rot1", "q_rot", "k_rot", "x_done",
             "v_copied", "stacking0", "stacking1", "stacked", "st_done", "exp_done", "masked", "pv_done",
             "mx_done", "max_done", "mcol_done", "misc_full", "misc_free", "m_in0", "m_in1", "oT_done",
             "o_rec_done", "y_done")
    with ExitStack() as ctx:
        sb = lambda n, s, d=F32: ctx.enter_context(nc.sbuf_tensor(f"a_{n}", s, d))
        sems = {n: ctx.enter_context(nc.semaphore(f"a_{n}")) for n in names}
        w_c = [sb(f"w_c{k}", [P, CC, C], F32R) for k in range(2)]
        causal = sb("causal", [P, HALF])
        QK = sb("QK", [P, G, NTB, 2, 2, DH])
        VY = sb("VY", [P, G, NTB, 2, DH])
        vy_tile = lambda b, t: VY[:, bass.ds(b * PR, PR), t, :, :].rearrange("p g h d -> p g (h d)")

        def phase(name, schedule, count):
            with nc.Block(name) as block:
                for me, on in (("sp", block.sync), ("pe", block.tensor), ("act", block.scalar),
                               ("dve", block.vector), ("pool", block.gpsimd)):
                    on(lambda e, me=me: schedule(Walk(me, e, sems, passed, count)))
            w = Walk(None, None, sems, passed, count)
            schedule(w)
            return w.count

        def tiles(w, src, psT, x_hi, x_lo, fill, finish, before=None):
            flat = lambda t: t[:, :, :].rearrange("p c n -> p (c n)")

            def turn(t, back=0):
                j = t % 2
                if w.on("pe"):
                    w.wait("xn_done", back)
                    w.wait("xlo_done", 1)

                def make():
                    for c in range(CC):
                        m = w.engine.transpose(psT[j][:, c * P:(c + 1) * P], src[j][:, c * P:(c + 1) * P], ident[:, :])
                    return m
                w.do("pe", "turned", make)
                if w.on("act"):
                    w.wait("turned")
                    w.wait("projected")
                w.do("act", "xhi_done", lambda: w.engine.activation(flat(x_hi[j]), psT[j][:, 0:C], ACT.Copy))
                if w.on("dve"):
                    w.wait("xhi_done")
                w.do("dve", "xlo_done", lambda: w.engine.tensor_tensor(
                    flat(x_lo[j]), psT[j][:, 0:C], flat(x_hi[j]).bitcast(F32), ALU.subtract))

            def batch(b, last):
                for t in range(NTB):
                    if before and not last:
                        before(b + 1, t)
                    if not (last and t == NTB - 1):
                        turn(t + 1)
                    if not (last and t >= NTB - 2):
                        fill(b + (t + 2) // NTB, (t + 2) % NTB)
                    finish(b, t, 0 if last and t == NTB - 1 else 1)

            fill(0, 0)
            fill(0, 1)
            turn(0, 1)
            w.turns(B - 1, lambda b: batch(b, False))
            batch(B - 1, True)

        def three(e, out, hi, lo, wts, at, n):
            k = 0
            for s, ww in ((hi, wts[0]), (lo, wts[0]), (hi, wts[1])):
                for c in range(CC):
                    m = e.matmul(out, s[:, c, :], ww[:, c, at:at + n], start=(k == 0), stop=(k == 3 * CC - 1))
                    k += 1
            return m

        with ExitStack() as c0:
            sb0 = lambda n, s, d=F32: c0.enter_context(nc.sbuf_tensor(f"a_{n}", s, d))
            w_eff = [sb0(f"w_eff{k}", [P, CC, 3 * C], F32R) for k in range(2)]
            rope = sb0("rope", [P, 2, NTB, D2])
            with ExitStack() as c1:
                sb1 = lambda n, s, d=F32: c1.enter_context(nc.sbuf_tensor(f"a_{n}", s, d))
                sem1 = lambda n: c1.enter_context(nc.semaphore(f"a_{n}"))
                down = [sb1(f"down{w}", [P, PR, C]) for w in range(3)]
                up = sb1("up", [P, 3, 2 * DH])
                wc = sb1("wc", [P, CC, C])
                ps = [[c1.enter_context(nc.psum_tensor(f"a_fold{w}{c}", [P, 512], F32)) for c in range(CC)] for w in range(3)]
                cleared, w_in, wc_in, folded, hi_done = (sem1(n) for n in ("cleared", "w_in", "wc_in", "folded", "hi_done"))
                block = c1.enter_context(nc.Block("fold"))

                @block.sync
                def _(sp):
                    for w in range(3):
                        sp.dma_start(down[w][:, :, :], w_d[w].rearrange("(r p) c -> p r c", p=P)).then_inc(w_in, 16)
                    sp.wait_ge(cleared, 1)
                    for w in range(3):
                        for h in range(2):
                            at = h * DH
                            for part in up_d[w]:
                                width = part.shape[1]
                                sp.dma_start(up[64 * h:64 * h + 64, w, at:at + width], part).then_inc(w_in, 16)
                                at += width
                    sp.dma_start(wc[:, :, :], wc_d.rearrange("(c p) n -> p c n", p=P)).then_inc(wc_in, 16)
                    sp.dma_start(rope[:, :, :, :], rope_d.rearrange("a (t p) d -> p a t d", p=P)).then_inc(wc_in, 16)
                    sp.wait_ge(wc_in, 32)

                @block.gpsimd
                def _(pool):
                    pool.memset(up[:, :, :], 0.0).then_inc(cleared, 1)
                    pool.memset(causal[:, :], 0.0).then_inc(cleared, 1)
                    for s in sems.values():
                        ahead(pool, s, Walk.START)
                    pool.wait_ge(cleared, 2)
                    last = causal[:, HALF - P:HALF]
                    pool.affine_select(last, last, [[-1, P]], ALU.is_ge, -BIG, 0, 1)

                @block.tensor
                def _(pe):
                    pe.wait_ge(w_in, 16 * (3 + 2 * 5))
                    for w in range(3):
                        for c in range(CC):
                            for r in range(PR):
                                m = pe.matmul(ps[w][c][:, r * 2 * DH:(r + 1) * 2 * DH], down[w][:, r, c * P:(c + 1) * P],
                                              up[:, w, :], start=True, stop=True)
                            m.then_inc(folded, 1)

                def parts():
                    n = 0
                    for w in range(3):
                        for c in range(CC):
                            n += 1
                            yield (folded, n, ps[w][c][:, 0:C], scale if w == 0 else 1.0,
                                   [k[:, c, w * C:(w + 1) * C] for k in w_eff])
                    for c in range(CC):
                        yield wc_in, 32, wc[:, c, :], 1.0, [k[:, c, :] for k in w_c]

                @block.scalar
                def _(act):
                    for sem, n, src, s, (hi, _) in parts():
                        act.wait_ge(sem, n)
                        act.activation(hi, src, ACT.Copy, scale=s).then_inc(hi_done, 1)

                @block.vector
                def _(dve):
                    for k, (_, _, src, s, (hi, lo)) in enumerate(parts()):
                        dve.wait_ge(hi_done, k + 1)
                        dve.scalar_tensor_tensor(lo, src, s, hi.bitcast(F32), ALU.mult, ALU.subtract)

            with ExitStack() as c1:
                sb1 = lambda n, s, d=F32: c1.enter_context(nc.sbuf_tensor(f"a_{n}", s, d))
                stats, mv = sb1("stats", [P, NTB, 6]), sb1("mv", [P, NTB, 2])
                mean, std, rstd = sb1("mean", [P, NTB]), sb1("std", [P, NTB]), sb1("rstd", [P, NTB])
                XN = [sb1(f"XN{j}", [P, C]) for j in range(2)]
                x_hi, x_lo = ([sb1(f"{n}{j}", [P, CC, P], F32R) for j in range(2)] for n in ("x_hi", "x_lo"))
                rot_a = [sb1(f"rot_a{w}", [P, PR, 2, D2]) for w in range(2)]
                rot_b = [sb1(f"rot_b{w}", [P, PR, 2, D2]) for w in range(2)]
                psT = [c1.enter_context(nc.psum_tensor(f"a_psT{j}", [P, HALF], F32)) for j in range(2)]
                psP = [c1.enter_context(nc.psum_tensor(f"a_psP{j}", [P, 2, HALF], F32)) for j in range(2)]

                def project_all(w):
                    on, wait, do, e = w.on, w.wait, w.do, w.engine
                    row = lambda b, t: X[:, bass.ds(b * NTB + t, 1), :].rearrange("p a c -> p (a c)")

                    def stat(b, t):
                        do("dve", "norm", lambda: e.bn_stats(stats[:, t, :], row(b, t)))

                    def aggregate(t):
                        if on("dve"):
                            wait("norm", NTB - 1, apart=True)
                        do("dve", "norm", lambda: e.bn_aggr(mv[:, t, :], stats[:, t, :]))

                    def deviations():
                        if on("act"):
                            wait("norm")
                            wait("rstd_done")
                        do("act", "std_done", lambda: e.activation(std[:, :], mv[:, :, 1], ACT.Sqrt,
                                                                   bias=consts["eps"][:, 0:1]))
                        if on("dve"):
                            wait("norm")
                            wait("xn_done")
                        do("dve", "rstd_done", lambda: e.tensor_copy(mean[:, :], mv[:, :, 0]))
                        if on("dve"):
                            wait("std_done")
                        do("dve", "rstd_done", lambda: e.reciprocal(rstd[:, :], std[:, :]))

                    def fill(b, t):
                        if on("dve"):
                            wait("rstd_done")
                            wait("turned", 1)
                        do("dve", "xn_done", lambda: e.tensor_scalar(XN[t % 2][:, :], row(b, t), mean[:, t:t + 1],
                                                                     rstd[:, t:t + 1], ALU.subtract, ALU.mult))

                    def before(b, t):
                        if t < 4:
                            if t == 0 and on("dve"):
                                wait("norm")
                                wait("std_done")
                                wait("rstd_done")
                            stat(b, 2 * t)
                            stat(b, 2 * t + 1)
                        elif t == 4:
                            for k in range(NTB):
                                aggregate(k)
                        elif t == 6:
                            deviations()

                    def rotate(b, t, name, which, sem):
                        ee = QK[:, bass.ds(b * PR, PR), t, which, :, D2:DH]
                        pairs = lambda a, k: a.rearrange("p g h (i two) -> p g h i two", two=2)[:, :, :, :, k]
                        table = lambda a: rope[:, a, t, :].unsqueeze(1).unsqueeze(1).to_broadcast([P, PR, 2, D2])
                        if on(name):
                            wait(sem)
                            wait("copied")
                        do(name, f"rot{which}", lambda: e.tensor_tensor(rot_a[which][:, :, :, :], ee, table(0), ALU.mult))
                        for k in range(2):
                            do(name, f"rot{which}", lambda k=k: e.tensor_tensor(
                                pairs(rot_b[which][:, :, :, :], k), pairs(ee, 1 - k), pairs(table(1), k), ALU.mult))
                        if on(name):
                            wait(f"rot{which}")
                        do(name, sem, lambda: e.tensor_tensor(ee, rot_a[which][:, :, :, :], rot_b[which][:, :, :, :], ALU.add))

                    def finish(b, t, back):
                        j = t % 2
                        if on("pe"):
                            wait("xlo_done", back)
                            wait("copied", 2)

                        def make():
                            three(e, psP[j][:, 0, :], x_hi[j], x_lo[j], w_eff, 0, QKW)
                            return three(e, psP[j][:, 1, 0:C], x_hi[j], x_lo[j], w_eff, QKW, C)
                        do("pe", "projected", make)
                        if on("act"):
                            wait("projected", apart=True)
                        do("act", "copied", lambda: e.activation(
                            QK[:, bass.ds(b * PR, PR), t, :, :, :].rearrange("p g w h d -> p w g (h d)"),
                            psP[j][:, 0, :].rearrange("p (w g d) -> p w g d", w=2, g=PR), ACT.Copy))
                        do("act", "copied", lambda: e.activation(
                            vy_tile(b, t), psP[j][:, 1, 0:C].rearrange("p (g d) -> p g d", g=PR), ACT.Copy))
                        rotate(b, t, "dve", 0, "q_rot")
                        rotate(b, t, "pool", 1, "k_rot")

                    for t in range(NTB):
                        stat(0, t)
                    for t in range(NTB):
                        aggregate(t)
                    deviations()
                    tiles(w, XN, psT, x_hi, x_lo, fill, finish, before)

                count = phase("project", project_all, None)

        with ExitStack() as c1:
            sb1 = lambda n, s, d=F32: c1.enter_context(nc.sbuf_tensor(f"a_{n}", s, d))
            VP = [sb1(f"VP{r}", [P, NTB, 2, 32]) for r in range(2)]
            stack = [sb1(f"stack{w}", [P, NTB, 2, 64]) for w in range(2)]
            QT = [sb1(f"QT{r}", [P, T], F32R) for r in range(2)]
            KT = [[sb1(f"KT{r}{h}", [P, T], F32R) for h in range(2)] for r in range(2)]
            prob = [sb1(f"prob{r}", [P, 2, HALF]) for r in range(4)]
            junk = [sb1(f"junk{r}", [P, HALF], BF16) for r in range(2)]
            mpart = [sb1(f"mpart{r}", [P, 2, NTB, 2]) for r in range(2)]
            mcol = [sb1(f"mcol{r}", [P, 4, 2]) for r in range(2)]
            mT = [sb1(f"mT{r}", [2, HALF], F32R) for r in range(2)]
            OT = sb1("OT", [P, HALF])
            o_sum = sb1("o_sum", [P, 4, 2, DH + 1])
            o_rec = sb1("o_rec", [P, 4, 2, 1])
            psS = [c1.enter_context(nc.psum_tensor(f"a_psS{j}", [P, 2, HALF], F32)) for j in range(2)]
            psM = [c1.enter_context(nc.psum_tensor(f"a_psM{j}", [P, HALF], F32)) for j in range(2)]
            psO = c1.enter_context(nc.psum_tensor("a_psO", [P, HALF], F32))
            psR = c1.enter_context(nc.psum_tensor("a_psR", [P, HALF], F32))
            init = c1.enter_context(nc.semaphore("a_init"))

            with nc.Block("clear") as block:
                @block.gpsimd
                def _(pool):
                    for w in range(2):
                        pool.memset(stack[w][:, :, :, :], 0.0).then_inc(init, 1)
                    for r in range(2):
                        pool.memset(VP[r][:, :, :, :], 0.0).then_inc(init, 1)
                    pool.wait_ge(init, 4)
                    pool.memset(stack[1][:, :, :, 3 * DH:3 * DH + 1], 1.0)
                    for r in range(2):
                        pool.memset(VP[r][:, :, :, DH:DH + 1], 1.0)

                @block.vector
                def _(dve):
                    for r in range(2):
                        for h in range(2):
                            dve.memset(KT[r][h][64 * (1 - h):64 * (1 - h) + 64, :].bitcast(F32), 0.0)
                    dve.memset(psO[:, :], 0.0)

            CHUNKS = []
            for qt in range(NTB):
                lo = qt * P // HALF * HALF
                for first in range(0, lo, HALF):
                    CHUNKS += [(h, qt, first, HALF, False) for h in range(2)]
                CHUNKS += [(h, qt, lo, (qt + 1) * P - lo, True) for h in range(2)]
            STEPS = [(qh, kt) for qh in range(NH) for kt in range((qh + 1) * HALF // P)]
            NS = len(STEPS)
            PER_STEP = len(CHUNKS) // NS
            assert len(CHUNKS) == PER_STEP * NS and NS == 12

            def span(qh, kt):
                first = max(kt * P - qh * HALF, 0)
                return first, HALF - first

            def heads(w):
                on, wait, do, e = w.on, w.wait, w.do, w.engine

                def stack_part(pair, k):
                    for which, name in ((0, "pool"), (1, "dve")):
                        src = QK[:, bass.ds(pair, 1), :, which, :, :].rearrange("p g t h d -> p (g t) h d")
                        hi_at = ((0, DH), (0, 2 * DH))[which]
                        lo_at = (2 * DH, DH)[which]
                        at = lambda a: stack[which][:, :, :, a:a + DH]
                        if k < 2:
                            if k == 0 and on(name):
                                wait("misc_full", apart=True)
                            do(name, f"stacking{which}", lambda: e.tensor_copy(at(hi_at[k]).bitcast(F32R), src))
                        else:
                            if on(name):
                                wait(f"stacking{which}", apart=True)
                            do(name, "stacked", lambda: e.tensor_tensor(at(lo_at), src, at(0), ALU.subtract))

                def misc_wait():
                    if on("pe"):
                        wait("misc_free")

                def four(make):
                    def run():
                        for k in range(4):
                            m = make(k)
                        return m
                    return run

                def turn(which, qh, copies):
                    misc_wait()
                    if on("pe"):
                        wait("stacked")
                        wait("stacking0")
                        wait("stacking1")
                    do("pe", "misc_full", four(lambda k: e.transpose(
                        psR[:, k * P:(k + 1) * P],
                        stack[which][:, qh * 4 + k, :, :].rearrange("p h d -> p (h d)"), ident[:, :])))
                    if on("act"):
                        wait("misc_full")
                    for out, rows in copies:
                        do("act", "misc_free", lambda: e.activation(out[rows, qh * HALF:(qh + 1) * HALF],
                                                                    psR[rows, :], ACT.Copy))

                def turn_q(r, qh):
                    turn(0, qh, [(QT[r], slice(0, P))])

                def turn_k(r, qh):
                    turn(1, qh, [(KT[r][h], slice(64 * h, 64 * h + 64)) for h in range(2)])

                def chunk(r, c, later):
                    h, qt, first, n, diagonal = CHUNKS[c]
                    b = c % 2
                    if on("pe"):
                        wait("max_done", 1)
                        if c == 0:
                            wait("misc_free", later)
                        if c == 8:
                            wait("misc_free")
                    do("pe", "mx_done", lambda: e.matmul(psM[b][:, 0:n], QT[r][:, qt * P:(qt + 1) * P],
                                                         KT[r][h][:, first:first + n], start=True, stop=True))
                    slot = 0 if first == 0 else 1
                    out = mpart[r][:, h, qt, slot:slot + 1]
                    if on("dve"):
                        if diagonal:
                            wait("max_done", 1)
                        wait("mx_done", apart=diagonal)
                    if diagonal:
                        do("dve", "max_done", lambda: e.tensor_tensor_reduce(
                            junk[b][:, 0:n], psM[b][:, 0:n], causal[:, HALF - n:HALF], 1.0, -3e38, ALU.add, ALU.max, out))
                    else:
                        do("dve", "max_done", lambda: e.tensor_reduce(out, psM[b][:, 0:n], AX.X, ALU.max))

                def max_column(r, qh):
                    if on("dve"):
                        wait("max_done")
                        wait("misc_full")
                    if qh == 0:
                        do("dve", "mcol_done", lambda: e.tensor_copy(
                            mcol[0][:, :, :], mpart[r][:, :, 0:4, 0].rearrange("p h t -> p t h")))
                    else:
                        do("dve", "mcol_done", lambda: e.tensor_tensor(
                            mcol[1][:, :, :], mpart[r][:, :, 4:8, 0].rearrange("p h t -> p t h"),
                            mpart[r][:, :, 4:8, 1].rearrange("p h t -> p t h"), ALU.max))

                def max_row(r, qh):
                    misc_wait()
                    if on("pe"):
                        wait("mcol_done")
                    do("pe", "misc_full", four(lambda k: e.transpose(
                        psR[0:2, k * P:(k + 1) * P], mcol[qh][:, k, :], ident[:, :])))
                    if on("act"):
                        wait("misc_full")
                        wait(f"m_in{qh}")
                    do("act", "misc_free", lambda: e.activation(mT[qh][:, :], psR[0:2, :], ACT.Copy, scale=-1.0))
                    if on("sp"):
                        wait("misc_free")
                        wait("mx_done")
                    do("sp", f"m_in{qh}", lambda: e.dma_start(
                        QT[r][3 * DH:3 * DH + 65:64, qh * HALF:(qh + 1) * HALF].bitcast(F32), mT[qh][:, :].bitcast(F32)), 16)

                def scores(r, s):
                    qh, kt = STEPS[s]
                    first, n = span(qh, kt)
                    b = s % 2
                    if on("pe"):
                        wait("exp_done", 1)
                        if kt == 0:
                            wait(f"m_in{qh}")

                    def make():
                        for h in range(2):
                            m = e.matmul(psS[b][:, h, 0:n], KT[r][h][:, kt * P:(kt + 1) * P],
                                         QT[r][:, qh * HALF + first:(qh + 1) * HALF], start=True, stop=True)
                        return m
                    do("pe", "st_done", make)
                    if on("act"):
                        wait("st_done")
                    do("act", "exp_done", lambda: e.activation(prob[s % 4][:, :, 0:n], psS[b][:, :, 0:n], ACT.Exp))
                    if kt * P >= qh * HALF:
                        a = prob[s % 4][:, :, 0:P]
                        if on("pool"):
                            wait("exp_done")
                        do("pool", "masked", lambda: e.affine_select(a, a, [[0, 2], [1, P]], ALU.is_ge, 0.0, 0, -1))

                def values(s, r, behind):
                    if on("pe"):
                        wait("exp_done", len(behind))
                        wait("masked", sum(STEPS[k][1] * P >= STEPS[k][0] * HALF for k in behind))
                        if s == 1:
                            wait("v_copied")
                        if STEPS[s][1] == 1:
                            wait("oT_done")

                    def make():
                        for k in (s - 1, s):
                            qh, kt = STEPS[k]
                            first, n = span(qh, kt)
                            last = (qh + 1) * HALF // P - 2
                            for h in range(2):
                                j = 2 * h + kt % 2
                                m = e.matmul(psO[32 * j:32 * j + 32, first:HALF],
                                             VP[r][:, kt, h, :],
                                             prob[k % 4][:, h, 0:n], start=(kt < 2), stop=(kt >= last))
                        return m
                    do("pe", "pv_done", make)

                def copy_v(r, pair):
                    if on("pool"):
                        wait("pv_done")
                    do("pool", "v_copied", lambda: e.tensor_copy(
                        VP[r][:, :, :, 0:DH], VY[:, bass.ds(pair, 1), :, :, :].rearrange("p g t h d -> p (g t) h d")))

                def out_copy():
                    if on("act"):
                        wait("pv_done")
                        wait("misc_full")
                    do("act", "oT_done", lambda: e.activation(OT[:, :], psO[:, :], ACT.Copy))

                def out_rows(qh, pair):
                    misc_wait()
                    if on("pe"):
                        wait("oT_done")
                    do("pe", "misc_full", four(lambda k: e.transpose(
                        psR[:, k * P:(k + 1) * P], OT[:, k * P:(k + 1) * P], ident[:, :])))
                    rows = lambda q, k: psR[:, :].rearrange("p (t h k d) -> p t h k d", h=2, k=2, d=32)[:, q, :, k, 0:DH + 1]
                    if on("dve"):
                        wait("misc_full")
                        wait("y_done")
                    do("dve", "misc_free", lambda: e.tensor_copy(o_sum[:, :, :, :], rows(slice(0, 4), 0)))
                    q = slice(1 if qh == 0 else 0, 4)
                    if on("dve"):
                        wait("misc_free")
                    do("dve", "misc_free", lambda: e.tensor_tensor(o_sum[:, q, :, :], rows(q, 1), o_sum[:, q, :, :], ALU.add))
                    if on("dve"):
                        wait("misc_free")
                    do("dve", "o_rec_done", lambda: e.reciprocal(o_rec[:, :, :, :], o_sum[:, :, :, DH:DH + 1]))
                    if on("dve"):
                        wait("o_rec_done")
                    do("dve", "y_done", lambda: e.tensor_tensor(
                        VY[:, bass.ds(pair, 1), qh * 4:qh * 4 + 4, :, :].rearrange("p g t h d -> p (g t) h d"),
                        o_sum[:, :, :, 0:DH], o_rec[:, :, :, :].to_broadcast([P, 4, 2, DH]), ALU.mult))

                def body(r, pair, do_s=True, do_m=True, do_t=True, tail=True):
                    nxt = 1 - r
                    for s in range(NS):
                        if do_s:
                            scores(r, s)
                            if s == 0:
                                max_row(r, 1)
                            if s % 2 and s >= 3:
                                values(s - 2, r, (s - 1, s))
                            if s == 5:
                                out_copy()
                            if s == 7:
                                out_rows(0, pair)
                            if tail and s == 1:
                                values(NS - 1, nxt, (0, 1))
                                out_copy()
                            if tail and s == 2:
                                out_rows(1, pair - 1)
                        if do_m:
                            if s == 1:
                                turn_q(nxt, 1)
                            if s == 3:
                                turn_k(nxt, 1)
                            if s == 5:
                                max_row(nxt, 0)
                            for c in range(PER_STEP * s, PER_STEP * (s + 1)):
                                chunk(nxt, c, 1 if do_s else 0)
                            if s == 3:
                                max_column(nxt, 0)
                            if s == NS - 1:
                                max_column(nxt, 1)
                            if s == 7:
                                copy_v(nxt, pair + 1)
                        if do_t:
                            if s in (4, 5, 6):
                                stack_part(pair + 2, s - 4)
                            if s == 8:
                                turn_q(r, 0)
                            if s == 10:
                                turn_k(r, 0)

                for k in range(3):
                    stack_part(0, k)
                turn_q(0, 0)
                turn_k(0, 0)
                body(1, -1, do_s=False)
                body(0, 0, tail=False)

                def two(i):
                    body(1, i * 2 + 1)
                    body(0, i * 2 + 2)

                w.turns(G // 2 - 2, two)
                body(1, G - 3)
                body(0, G - 2, do_t=False)
                body(1, G - 1, do_m=False, do_t=False)
                values(NS - 1, 1, ())
                out_copy()
                out_rows(1, G - 1)

            count = phase("heads", heads, count)

        with ExitStack() as c1:
            sb1 = lambda n, s, d=F32: c1.enter_context(nc.sbuf_tensor(f"a_{n}", s, d))
            Y = [sb1(f"Y{j}", [P, C]) for j in range(2)]
            y_hi, y_lo = ([sb1(f"{n}{j}", [P, CC, P], F32R) for j in range(2)] for n in ("y_hi", "y_lo"))
            psT = [c1.enter_context(nc.psum_tensor(f"a_psYT{j}", [P, HALF], F32)) for j in range(2)]
            psW = [c1.enter_context(nc.psum_tensor(f"a_psW{j}", [P, HALF], F32)) for j in range(2)]

            def output(w):
                on, wait, do, e = w.on, w.wait, w.do, w.engine

                def fill(b, t):
                    if on("pool"):
                        wait("turned", 1)
                    do("pool", "xn_done", lambda: e.tensor_copy(Y[t % 2][:, :].rearrange("p (g d) -> p g d", g=PR),
                                                                vy_tile(b, t)))

                def finish(b, t, back):
                    j = t % 2
                    if on("pe"):
                        wait("xlo_done", back)
                        wait("x_done", 1)
                    do("pe", "projected", lambda: three(e, psW[j][:, 0:C], y_hi[j], y_lo[j], w_c, 0, C))
                    row = X[:, bass.ds(b * NTB + t, 1), :].rearrange("p a c -> p (a c)")
                    if on("dve"):
                        wait("projected")
                    do("dve", "x_done", lambda: e.tensor_tensor(row, psW[j][:, 0:C], row, ALU.add))

                tiles(w, Y, psT, y_hi, y_lo, fill, finish)

            phase("output", output, count)


def make_constants(nc, sh, ctx):
    NT, E, NB = sh.NT, sh.E, sh.NB
    sb = lambda n, s, d=F32: ctx.enter_context(nc.sbuf_tensor(n, s, d))
    c = {
        "ident": sb("ident", [P, P]), "ones": sb("ones", [P, P]), "upper": sb("upper", [P, P]),
        "iota_e": sb("iota_e", [P, E]), "iota_e8": sb("iota_e8", [P, E]), "iota_f": sb("iota_f", [P, P]),
        "iota_b": sb("iota_b", [P, NB]), "eye_e": sb("eye_e", [P, E, E]), "t_idx": sb("t_idx", [P, NT, 2]),
        "p_idx": sb("p_idx", [P, 1]), "eps": sb("eps", [P, 1]),
    }
    with nc.semaphore("made") as made, nc.Block("constants") as block:
        @block.gpsimd
        def _(pool):
            pool.memset(c["ident"][:, :], 0.0).then_inc(made, 1)
            pool.memset(c["eye_e"][:, :, :], 0.0).then_inc(made, 1)
            pool.memset(c["ones"][:, :], 1.0).then_inc(made, 1)
            pool.memset(c["eps"][:, :], EPS)
            small = dict(allow_small_or_imprecise_dtypes=True)
            pool.iota(c["iota_e"][:, :], [[1, E]], 0, 0, **small)
            pool.iota(c["iota_e8"][:, :], [[1, E]], E, 0, **small)
            pool.iota(c["iota_f"][:, :], [[1, P]], 0, 0, **small)
            pool.iota(c["iota_b"][:, :], [[1, NB]], 0, 0, **small)
            pool.iota(c["t_idx"][:, :, :], [[1, NT], [0, 2]], 0, 0, **small)
            pool.iota(c["p_idx"][:, :], [[0, 1]], 0, 1, **small)
            pool.wait_ge(made, 3)
            pool.affine_select(c["ident"][:, :], c["ident"][:, :], [[-1, P]], ALU.not_equal, 1.0, 0, 1)
            pool.affine_select(c["eye_e"][:, :, :], c["eye_e"][:, :, :], [[-1, E], [1, E]], ALU.not_equal, 1.0, 0, 0)
            pool.affine_select(c["upper"][:, :], c["ones"][:, :], [[1, P]], ALU.is_gt, 0.0, 0, -1)
    return c


def program(nc, sh, x, wq_down, wk_down, wv_down, ups, wc, gate, gate_up, down, sim, rope, out):
    dram = lambda n, s: nc.dram_tensor(n, s, F32).ap()
    xn, ys = dram("xn", [sh.N, sh.C]), dram("ys", [sh.NB * P, sh.C])
    with ExitStack() as ctx:
        consts = make_constants(nc, sh, ctx)
        passed = ctx.enter_context(nc.semaphore("passed"))
        X = ctx.enter_context(nc.sbuf_tensor("X", [P, sh.NT, sh.C], F32))

        def ffn(name, src, dst):
            with ExitStack() as c:
                wgu = [c.enter_context(nc.sbuf_tensor(f"{name}_wgu{k}", [P, sh.E * sh.CC * 2 * sh.F], F32R)) for k in range(2)]
                wdn = [c.enter_context(nc.sbuf_tensor(f"{name}_wdn{k}", [P, sh.E * sh.CC * sh.C], F32R)) for k in range(2)]
                load_weights(nc, sh, name, gate_up, down, wgu, wdn, passed)
                moe(nc, sh, name, X, src, dst, gate, sim, xn, ys, wgu, wdn, consts, passed)

        ffn("m1", x, None)
        attention(nc, sh, X, (wq_down, wk_down, wv_down), ups, wc, rope, consts, passed)
        ffn("m2", None, out)


def rope_tables(T, D):
    inv = np.float32(1.0) / np.float32(10000.0) ** (np.arange(0, D, 2, dtype=np.float32) / np.float32(D))
    freqs = np.arange(T, dtype=np.float32)[:, None] * inv[None, :]
    emb = np.concatenate((freqs, freqs), axis=-1)
    sign = np.where(np.arange(D) % 2 == 0, np.float32(-1), np.float32(1))
    return np.stack((np.cos(emb), np.sin(emb) * sign)).astype(np.float32)


def kernel(**inputs):
    import concourse.bacc as bacc
    from concourse.bass_utils import run_bass_kernel_spmd

    a = {k[3:]: np.asarray(v) for k, v in inputs.items()}
    x = a["attn_x"]
    sh = Shapes(x, a["ffn_gate_up_proj"])
    given = {
        "x": x.reshape(sh.N, sh.C),
        "wq_down": a["attn_Wq_down"].T, "wk_down": a["attn_Wk_down"].T, "wv_down": a["attn_Wv_down"].T,
        "wq_up_c": a["attn_Wq_up_c"], "wq_up_e": a["attn_Wq_up_e"],
        "wk_up_c": a["attn_Wk_up_c"], "wk_up_e": a["attn_Wk_up_e"], "wv_up": a["attn_Wv_up"], "wc": a["attn_Wc"],
        "gate": a["ffn_gate_weight"].T, "gate_up": a["ffn_gate_up_proj"].transpose(0, 2, 1),
        "down": a["ffn_down_proj"].transpose(0, 2, 1), "sim": a["ffn_similarity_matrix"],
        "rope": rope_tables(sh.T, sh.DH // 2),
    }
    given = {k: np.ascontiguousarray(v) for k, v in given.items()}
    nc = bacc.Bacc("TRN2", target_bir_lowering=False, num_devices=1)
    d = {k: nc.dram_tensor(k, list(v.shape), F32, kind="ExternalInput").ap() for k, v in given.items()}
    out = nc.dram_tensor("out", [sh.N, sh.C], F32, kind="ExternalOutput").ap()
    ups = ((d["wq_up_c"], d["wq_up_e"]), (d["wk_up_c"], d["wk_up_e"]), (d["wv_up"],))
    program(nc, sh, d["x"], d["wq_down"], d["wk_down"], d["wv_down"], ups, d["wc"], d["gate"], d["gate_up"],
            d["down"], d["sim"], d["rope"], out)
    r = run_bass_kernel_spmd(nc, [given], core_ids=[0])
    return r.results[0]["out"].reshape(sh.B, sh.T, sh.C)
```

```python
from contextlib import ExitStack

import numpy as np

import concourse.bass as bass
import concourse.mybir as mybir

F32 = mybir.dt.float32
F32R = mybir.dt.float32r
BF16 = mybir.dt.bfloat16
I32 = mybir.dt.int32
U32 = mybir.dt.uint32
ALU = mybir.AluOpType
ACT = mybir.ActivationFunctionType
AX = mybir.AxisListType

P = 128
EPS = 1e-5
THRESHOLD = 0.7
BIG = 1e30


class Shapes:

    def __init__(self, x, gate_up, H=16):
        self.B, self.T, self.C = x.shape
        self.N = self.B * self.T
        self.NT = self.N // P
        self.E, f2, _ = gate_up.shape
        self.F = f2 // 2
        self.K = 2
        self.NB = -(-(self.K * self.N // P + self.E - 1) // 4) * 4
        self.CC = self.C // P
        self.H = H
        self.DH = self.C // H
        assert self.C == 256 and self.F == 256 and self.NT % 8 == 0 and self.NB <= P


def at_least(engine, sem, value):
    if not isinstance(value, int) or value > 0:
        engine.wait_ge(sem, value)


def ahead(engine, sem, n):
    engine.sem_inc(sem, n)


def wait_apart(engine, sem, value, passed):
    engine.wait_ge(sem, value)
    engine.sem_inc(passed, 1)


class Seq:

    def __init__(self, engine, sem):
        self.engine, self.sem, self.n = engine, sem, 0

    def then(self, instruction):
        self.n += 1
        instruction.then_inc(self.sem, 1)
        self.engine.wait_ge(self.sem, self.n)


def bcast(ap, shape):
    return ap.to_broadcast(shape)


class Walk:

    START = 32

    @staticmethod
    def rises(sem):
        return sem.startswith("gathered")

    @classmethod
    def start(cls, sem):
        return 0 if cls.rises(sem) else cls.START

    def __init__(self, me, engine, sems, waits_for, count=None):
        self.me, self.engine, self.sems, self.waits_for = me, engine, sems, waits_for
        self.count = dict(count) if count else {s: 0 for s in sems}
        self.waited, self.before = {}, {}

    def on(self, name):
        return name == self.me

    def wait(self, sem, back=0):
        if self.me is None:
            return
        assert self.waits_for[sem] == self.me, (sem, self.me)
        n = self.count[sem] - back
        if n > self.waited.get(sem, 0):
            self.engine.wait_ge(self.sems[sem], n + self.start(sem) + self.before.get(sem, 0))
            self.waited[sem] = n

    def raised(self, sem, instruction=None, by=1):
        self.count[sem] += by
        if instruction is not None:
            instruction.then_inc(self.sems[sem], by)

    def do(self, name, sem, make, by=1):
        self.raised(sem, make() if self.on(name) else None, by)

    def turns(self, n, body):
        before, me = dict(self.count), self.me
        self.me = None
        body(0)
        per_turn = {s: self.count[s] - before[s] for s in self.count}
        self.me, self.count = me, dict(before)
        if me is not None:
            with self.engine.Fori(0, n) as i:
                self.waited = {s: -self.START for s in self.sems}
                self.before = {s: i * raises for s, raises in per_turn.items() if raises and self.rises(s)}
                body(i)
                for s, raises in per_turn.items():
                    if raises and self.waits_for[s] == me and not self.rises(s):
                        assert self.waited[s] + self.start(s) >= raises, s
                        self.engine.sem_inc(self.sems[s], -raises)
            self.waited = {s: -self.START for s in self.sems}
        self.before = {}
        self.count = {s: v + n * per_turn[s] if self.rises(s) else v for s, v in before.items()}


class Weights:

    def __init__(self, nc, sh, name, ctx, gu_d, dn_d, wgu, wdn, passed):
        self.sh, self.gu_d, self.dn_d, self.wgu, self.wdn, self.passed = sh, gu_d, dn_d, wgu, wdn, passed
        self.ng, self.nd = sh.CC * 2 * sh.F, sh.CC * sh.C
        self.stage = [ctx.enter_context(nc.sbuf_tensor(f"{name}_w_stage{j}", [P, self.ng + self.nd], F32)) for j in range(2)]
        self.loaded = [ctx.enter_context(nc.semaphore(f"{name}_w_loaded{j}")) for j in range(2)]
        self.hi_done, self.lo_done = (ctx.enter_context(nc.semaphore(f"{name}_w_{n}_done")) for n in ("hi", "lo"))

    def load(self, sp):
        ahead(sp, self.lo_done, 2 * 2 + 1)
        with sp.Fori(0, self.sh.E // 2) as i:
            for j in range(2):
                wait_apart(sp, self.lo_done, 2 * (2 * i + j) + 1 + 2, self.passed)
                for part, src in ((slice(0, self.ng), self.gu_d), (slice(self.ng, None), self.dn_d)):
                    sp.dma_start(self.stage[j][:, part].rearrange("p (c f) -> p c f", c=self.sh.CC),
                                 src[bass.ds(i * 2 + j, 1), :, :].rearrange("e (c p) f -> p (e c) f", p=P)
                                 ).then_inc(self.loaded[j], 16)

    def parts(self, j, i):
        ng, nd = self.ng, self.nd
        yield self.stage[j][:, 0:ng], [w[:, bass.ds((i * 2 + j) * ng, ng)] for w in self.wgu]
        yield self.stage[j][:, ng:], [w[:, bass.ds((i * 2 + j) * nd, nd)] for w in self.wdn]

    def round(self, act):
        with act.Fori(0, self.sh.E // 2) as i:
            for j in range(2):
                act.wait_ge(self.loaded[j], 32 * i + 32)
                for src, (hi, _) in self.parts(j, i):
                    act.activation(hi, src, ACT.Copy).then_inc(self.hi_done, 1)

    def rest(self, pool):
        with pool.Fori(0, self.sh.E // 2) as i:
            for j in range(2):
                for n, (src, (hi, lo)) in enumerate(self.parts(j, i)):
                    wait_apart(pool, self.hi_done, 2 * (2 * i + j) + n + 1, self.passed)
                    pool.tensor_tensor(lo, src, hi.bitcast(F32), ALU.subtract).then_inc(self.lo_done, 1)


def moe(nc, sh, name, X, x_d, out_d, gate_d, sim_d, gu_d, dn_d, xn_d, ys_d, wgu, wdn, consts, passed):
    NT, E, C, F, CC, NB = sh.NT, sh.E, sh.C, sh.F, sh.CC, sh.NB
    G = 8
    NG = NT // G
    ctx = ExitStack()
    with ctx:
        sb = lambda n, s, d=F32: ctx.enter_context(nc.sbuf_tensor(f"{name}_{n}", s, d))
        sem = lambda n: ctx.enter_context(nc.semaphore(f"{name}_{n}"))
        weight = sb("weight", [P, 2, NT])
        pos_u = sb("pos_u", [P, NT, 2], U32)
        slot_u = sb("slot_u", [P, NB], U32)
        block_expert = sb("block_expert", [P, NB], I32)
        R = 4
        waits_for = {
            "idx_ready": "pool", "rows_used": "pool", "x_turned": "act", "xhi_done": "dve", "xlo_done": "pe",
            "gu_done": "act", "silu_done": "dve", "h_done": "pe", "h_turned": "act", "hhi_done": "dve",
            "hlo_done": "pe", "y_done": "act", "y_copied": "sp",
        }
        waits_for |= {f"gathered{j}": "pe" for j in range(R)} | {f"stored{j}": "act" for j in range(R)}
        sems = {n: sem(f"b_{n}") for n in waits_for}

        with ExitStack() as c1:
            sb1 = lambda n, s, d=F32: c1.enter_context(nc.sbuf_tensor(f"{name}_{n}", s, d))
            ps1 = lambda n, s, d=F32: c1.enter_context(nc.psum_tensor(f"{name}_{n}", s, d))
            sem1 = lambda n: c1.enter_context(nc.semaphore(f"{name}_{n}"))
            logits = ps1("logits", [P, 512])
            with ExitStack() as c2:
                sb2 = lambda n, s, d=F32: c2.enter_context(nc.sbuf_tensor(f"{name}_{n}", s, d))
                XN = [sb2(f"XN{j}", [P, G, C]) for j in range(2)]
                gate = sb2("gate", [P, CC, E])
                stats = sb2("stats", [P, G, 6])
                mv = sb2("mv", [P, G, 2])
                std, rstd = sb2("std", [P, G]), sb2("rstd", [P, G])
                xT = [sb2(f"xT{r}", [P, 2, CC, P]) for r in range(2)]
                psT = [c2.enter_context(nc.psum_tensor(f"{name}_psT{r}", [P, 2, CC, P], F32)) for r in range(2)]
                sem2 = lambda n: c2.enter_context(nc.semaphore(f"{name}_{n}"))
                x_in = [sem2(f"x_in{j}") for j in range(2)]
                xn_out = [sem2(f"xn_out{j}") for j in range(2)]
                gate_in, dv, xn_ready, std_done = (sem2(n) for n in ("gate_in", "dv", "xn_ready", "std_done"))
                turned, evacuated, scored = sem2("turned"), sem2("evacuated"), sem2("scored")
                x_t = x_d.rearrange("(t p) c -> p t c", p=P) if x_d is not None else None
                xn_t = xn_d.rearrange("(t p) c -> p t c", p=P)
                NI = NG // 2
                ND = 2 * G + 1
                block = c2.enter_context(nc.Block(f"{name}_norm"))

                @block.sync
                def _(sp):
                    sp.dma_start(gate[:, :, :], gate_d.rearrange("(c p) e -> p c e", p=P)).then_inc(gate_in, 16)
                    with sp.Fori(0, NI) as i:
                        for j in range(2 if x_d is not None else 0):
                            sp.dma_start(X[:, bass.ds((2 * i + j) * G, G), :],
                                         x_t[:, bass.ds((2 * i + j) * G, G), :]).then_inc(x_in[j], 16)
                        for j in range(2):
                            wait_apart(sp, xn_ready, (2 * i + j) * G + G, passed)
                            sp.dma_start(xn_t[:, bass.ds((2 * i + j) * G, G), :],
                                         XN[j][:, :, :]).then_inc(xn_out[j], 16)
                    for j in range(2):
                        sp.wait_ge(xn_out[j], 16 * NI + 1)

                @block.vector
                def _(dve):
                    ahead(dve, turned, G // 2 + 1)
                    for j in range(2):
                        ahead(dve, xn_out[j], 1)
                    with dve.Fori(0, NI) as i:
                        for j in range(2):
                            g = 2 * i + j
                            if x_d is not None:
                                dve.wait_ge(x_in[j], 16 * i + 16)
                            for k in range(G):
                                dve.bn_stats(stats[:, k, :], X[:, bass.ds(g * G + k, 1), :].rearrange("p a c -> p (a c)")
                                             ).then_inc(dv, 1)
                            for k in range(G):
                                wait_apart(dve, dv, g * ND + k + 1, passed)
                                dve.bn_aggr(mv[:, k, :], stats[:, k, :]).then_inc(dv, 1)
                            dve.wait_ge(std_done, g + 1)
                            dve.reciprocal(rstd[:, :], std[:, :]).then_inc(dv, 1)
                            dve.wait_ge(dv, g * ND + ND)
                            dve.wait_ge(xn_out[j], 16 * i + 1)
                            dve.wait_ge(turned, G // 2 * (2 * i + j) + 1)
                            for k in range(G):
                                dve.tensor_scalar(XN[j][:, k, :], X[:, bass.ds(g * G + k, 1), :].rearrange("p a c -> p (a c)"),
                                                  mv[:, k, 0:1], rstd[:, k:k + 1], ALU.subtract, ALU.mult
                                                  ).then_inc(xn_ready, 1)

                @block.tensor
                def _(pe):
                    pe.wait_ge(gate_in, 16)
                    ahead(pe, evacuated, 1 + 1)
                    NP = G

                    def turn(i, p):
                        j, k = p // (G // 2), 2 * (p % (G // 2))
                        q = i * NP + p
                        pe.wait_ge(xn_ready, q * 2 + 2)
                        pe.wait_ge(evacuated, q + 1)
                        for a in range(2):
                            for c in range(CC):
                                m = pe.transpose(psT[p % 2][:, a, c, :], XN[j][:, k + a, c * P:(c + 1) * P],
                                                 consts["ident"][:, :])
                        m.then_inc(turned, 1)

                    def score(i, p):
                        q = i * NP + p
                        pe.wait_ge(evacuated, q + 3)
                        for a in range(2):
                            for c in range(CC):
                                m = pe.matmul(logits[:, bass.ds((q * 2 + a) * E, E)], xT[p % 2][:, a, c, :],
                                              gate[:, c, :], start=(c == 0), stop=(c == CC - 1))
                        m.then_inc(scored, 1)

                    with pe.Fori(0, NI) as i:
                        for p in range(NP + 1):
                            if p < NP:
                                turn(i, p)
                            if p:
                                score(i, p - 1)

                @block.scalar
                def _(act):
                    ahead(act, scored, 1 + 1)
                    with act.Fori(0, NI) as i:
                        for p in range(G):
                            q = i * G + p
                            if p % (G // 2) == 0:
                                g = 2 * i + p // (G // 2)
                                act.wait_ge(dv, g * ND + 2 * G)
                                act.activation(std[:, :], mv[:, :, 1], ACT.Sqrt, bias=consts["eps"][:, 0:1]
                                               ).then_inc(std_done, 1)
                            act.wait_ge(turned, q + 2 + G // 2)
                            act.wait_ge(scored, q + 1)
                            act.activation(xT[p % 2][:, :, :, :].rearrange("p a c n -> p (a c n)"),
                                           psT[p % 2][:, :, :, :].rearrange("p a c n -> p (a c n)"),
                                           ACT.Copy).then_inc(evacuated, 1)

            TE = [P, NT, E]
            t3 = lambda n: sb1(n, TE)
            t2 = lambda n: sb1(n, [P, NT])
            t1 = lambda n, d=F32: sb1(n, [P, E], d)
            z, ez, prob, prob2, eq, cand = t3("z"), t3("ez"), t3("prob"), t3("prob2"), t3("eq"), t3("cand")
            one_hot = [t3("one_hot0"), t3("one_hot1")]
            routed = [t3("routed0"), t3("routed1")]
            total, rtotal, top = t2("total"), t2("rtotal"), [t2("top0"), t2("top1")]
            first, both = t2("first"), t2("both")
            wide = sb1("wide", [P, NT, E, E])
            count = t3("count")
            cum = [t3("cum0"), t3("cum1")]
            before = t3("before")
            pos = sb1("pos", [P, NT, 2])
            sim = sb1("sim", [P, E, E])
            simm, eqs, moved, remap = (sb1(n, [P, E, E]) for n in ("simm", "eqs", "moved", "remap"))
            primary, gap, best, best_j, use, stay = (t1(n) for n in ("primary", "gap", "best", "best_j", "use", "stay"))
            counts1 = t1("counts1")
            nblk_i, nblk_j = t1("nblk_i", I32), t1("nblk_j", I32)
            blocks = [t1("blocks0"), t1("blocks1"), t1("blocks2")]
            starts = t1("starts")
            started = sb1("started", [P, NB, E - 1])
            be_f = sb1("be_f", [P, NB])
            pos_i = sb1("pos_i", [P, NT, 2], I32)
            lohi_i = [sb1(f"lohi_i{k}", [P, NT, 2], I32) for k in range(2)]
            lohi = [sb1(f"lohi{k}", [P, NT, 2]) for k in range(2)]
            oh_lo = [sb1(f"oh_lo{r}", [P, 8, P], BF16) for r in range(2)]
            oh_hi = [sb1(f"oh_hi{r}", [P, 8, NB], BF16) for r in range(2)]
            oh_tp = [sb1(f"oh_tp{r}", [P, 8, 2, NB], BF16) for r in range(2)]
            slot_p = sb1("slot_p", [P, NB])
            counts_ps = ps1("counts_ps", [P, E])
            prefix_ps = ps1("prefix_ps", [P, 2, NT, E])
            slots_ps = ps1("slots_ps", [P, 2, NB])
            sim_in, dvs, z_ready, ez_ready = sem1("sim_in"), sem1("dvs"), sem1("z_ready"), sem1("ez_ready")
            counted, summed = sem1("counted"), sem1("summed")
            oh_ready, oh_used, rb = sem1("oh_ready"), sem1("oh_used"), sem1("rb")
            iota_e, iota_e8, iota_f, iota_b, eye_e, t_idx, p_idx = (
                consts[k] for k in ("iota_e", "iota_e8", "iota_f", "iota_b", "eye_e", "t_idx", "p_idx"))
            weights = Weights(nc, sh, name, c1, gu_d, dn_d, wgu, wdn, passed)
            block = c1.enter_context(nc.Block(f"{name}_route"))
            lg = logits[:, 0:NT * E].rearrange("p (t e) -> p t e", e=E)
            over_e = lambda a: a.unsqueeze(2).to_broadcast([P, NT, E])
            over_t = lambda a: a.unsqueeze(1).to_broadcast([P, NT, E])

            @block.sync
            def _(sp):
                sp.dma_start(sim[:, :, :], sim_d.unsqueeze(0).to_broadcast([P, E, E])).then_inc(sim_in, 16)
                weights.load(sp)

            @block.gpsimd
            def _(pool):
                for s in sems:
                    if Walk.start(s):
                        ahead(pool, sems[s], Walk.start(s))
                weights.rest(pool)

            @block.scalar
            def _(act):
                act.wait_ge(z_ready, 1)
                act.activation(ez[:, :, :], z[:, :, :], ACT.Exp).then_inc(ez_ready, 1)
                weights.round(act)

            NQ = NT * 2 // 8

            @block.tensor
            def _(pe):
                pe.wait_ge(counted, 1)
                pe.matmul(counts_ps[:, :], consts["ones"][:, :], counts1[:, :], start=True, stop=True).then_inc(summed, 1)
                pe.wait_ge(counted, 2)
                flat = count[:, :, :].rearrange("p t e -> p (t e)")
                pe.matmul(prefix_ps[:, 0, :, :].rearrange("p t e -> p (t e)"), consts["upper"][:, :], flat,
                          start=True, stop=True)
                pe.matmul(prefix_ps[:, 1, :, :].rearrange("p t e -> p (t e)"), consts["ones"][:, :], flat,
                          start=True, stop=True).then_inc(summed, 1)

                def group(q, r, first_group, last_group):
                    pe.wait_ge(oh_ready, q + 1)
                    for a in range(8):
                        m = pe.matmul(slots_ps[:, :, :].rearrange("p a b -> p (a b)"), oh_lo[r][:, a, :],
                                      oh_tp[r][:, a, :, :].rearrange("p a b -> p (a b)"),
                                      start=first_group and a == 0, stop=last_group and a == 7)
                    m.then_inc(oh_used, 1)

                group(0, 0, True, False)
                group(1, 1, False, False)
                with pe.Fori(1, NQ // 2 - 1) as i:
                    group(2 * i, 0, False, False)
                    group(2 * i + 1, 1, False, False)
                group(NQ - 2, 0, False, False)
                group(NQ - 1, 1, False, True)

            @block.vector
            def _(dve):
                seq = Seq(dve, dvs)
                T = seq.then

                def argfirst(out, source, value, eqt, candt, shape, over, iotas):
                    T(dve.tensor_tensor(eqt, source, value, ALU.is_equal))
                    T(dve.scalar_tensor_tensor(candt, eqt, -float(E), iotas, ALU.mult, ALU.add))
                    T(dve.tensor_reduce(out, candt, AX.X, ALU.min))

                T(dve.tensor_reduce(total[:, :], lg, AX.X, ALU.max))
                dve.tensor_tensor(z[:, :, :], lg, over_e(total[:, :]), ALU.subtract).then_inc(z_ready, 1)
                dve.wait_ge(ez_ready, 1)
                T(dve.tensor_reduce(total[:, :], ez[:, :, :], AX.X, ALU.add))
                T(dve.reciprocal(rtotal[:, :], total[:, :]))
                T(dve.tensor_tensor(prob[:, :, :], ez[:, :, :], over_e(rtotal[:, :]), ALU.mult))
                for k, source in enumerate((prob, prob2)):
                    T(dve.tensor_reduce(top[k][:, :], source[:, :, :], AX.X, ALU.max))
                    argfirst(first[:, :], source[:, :, :], over_e(top[k][:, :]), eq[:, :, :], cand[:, :, :], TE,
                             over_e, over_t(iota_e8[:, :]))
                    T(dve.tensor_tensor(one_hot[k][:, :, :], over_t(iota_e[:, :]), over_e(first[:, :]), ALU.is_equal))
                    if k == 0:
                        T(dve.scalar_tensor_tensor(prob2[:, :, :], one_hot[0][:, :, :], -2.0, prob[:, :, :],
                                                   ALU.mult, ALU.add))
                T(dve.tensor_reduce(counts1[:, :], one_hot[0][:, :, :].rearrange("p t e -> p e t"), AX.X, ALU.add))
                dve.engine_nop().then_inc(counted, 1)
                T(dve.tensor_tensor(both[:, :], top[0][:, :], top[1][:, :], ALU.add))
                T(dve.tensor_scalar(both[:, :], both[:, :], 1e-12, None, ALU.max))
                T(dve.reciprocal(rtotal[:, :], both[:, :]))
                for k in range(2):
                    T(dve.scalar_tensor_tensor(weight[:, k, :], top[k][:, :], 0.5, rtotal[:, :], ALU.mult, ALU.mult))
                dve.wait_ge(sim_in, 16)
                dve.wait_ge(summed, 1)
                T(dve.tensor_scalar(primary[:, :], counts_ps[:, :], 0.0, None, ALU.is_gt))
                T(dve.tensor_scalar(gap[:, :], primary[:, :], BIG, -BIG, ALU.mult, ALU.add))
                by_j = lambda a: a.unsqueeze(1).to_broadcast([P, E, E])
                by_e = lambda a: a.unsqueeze(2).to_broadcast([P, E, E])
                T(dve.tensor_tensor(simm[:, :, :], sim[:, :, :], by_j(primary[:, :]), ALU.mult))
                T(dve.tensor_tensor(simm[:, :, :], simm[:, :, :], by_j(gap[:, :]), ALU.add))
                T(dve.tensor_reduce(best[:, :], simm[:, :, :], AX.X, ALU.max))
                argfirst(best_j[:, :], simm[:, :, :], by_e(best[:, :]), eqs[:, :, :], moved[:, :, :], None, None,
                         by_j(iota_e8[:, :]))
                T(dve.tensor_scalar(use[:, :], best[:, :], THRESHOLD, None, ALU.is_ge))
                T(dve.tensor_scalar(stay[:, :], primary[:, :], -1.0, 1.0, ALU.mult, ALU.add))
                T(dve.tensor_tensor(use[:, :], use[:, :], stay[:, :], ALU.mult))
                T(dve.tensor_scalar(stay[:, :], use[:, :], -1.0, 1.0, ALU.mult, ALU.add))
                T(dve.tensor_tensor(moved[:, :, :], by_e(iota_e[:, :]), by_j(best_j[:, :]), ALU.is_equal))
                T(dve.tensor_tensor(moved[:, :, :], moved[:, :, :], by_j(use[:, :]), ALU.mult))
                T(dve.tensor_tensor(remap[:, :, :], eye_e[:, :, :], by_j(stay[:, :]), ALU.mult))
                T(dve.tensor_tensor(remap[:, :, :], remap[:, :, :], moved[:, :, :], ALU.add))
                for k in range(2):
                    T(dve.tensor_tensor(wide[:, :, :, :], one_hot[k][:, :, :].unsqueeze(2).to_broadcast([P, NT, E, E]),
                                        remap[:, :, :].unsqueeze(1).to_broadcast([P, NT, E, E]), ALU.mult))
                    T(dve.tensor_reduce(routed[k][:, :, :], wide[:, :, :, :], AX.X, ALU.add))
                dve.tensor_tensor(count[:, :, :], routed[0][:, :, :], routed[1][:, :, :], ALU.add).then_inc(counted, 1)
                dve.wait_ge(summed, 2)
                T(dve.tensor_copy(cum[0][:, :, :], prefix_ps[:, 1, :, :]))
                a, step = 0, 1
                while step < NT:
                    dve.tensor_copy(cum[1 - a][:, 0:step, :], cum[a][:, 0:step, :])
                    T(dve.tensor_tensor(cum[1 - a][:, step:, :], cum[a][:, step:, :], cum[a][:, 0:NT - step, :], ALU.add))
                    a, step = 1 - a, 2 * step
                T(dve.tensor_scalar(nblk_i[:, :], cum[a][:, NT - 1, :], float(P - 1), None, ALU.add))
                T(dve.tensor_single_scalar(nblk_j[:, :], nblk_i[:, :], 7, ALU.arith_shift_right))
                T(dve.tensor_copy(blocks[0][:, :], nblk_j[:, :]))
                b, step = 1, 1
                T(dve.tensor_copy(blocks[1][:, :], blocks[0][:, :]))
                while step < E:
                    dve.tensor_copy(blocks[3 - b][:, 0:step], blocks[b][:, 0:step])
                    T(dve.tensor_tensor(blocks[3 - b][:, step:], blocks[b][:, step:], blocks[b][:, 0:E - step], ALU.add))
                    b, step = 3 - b, 2 * step
                T(dve.tensor_tensor(starts[:, :], blocks[b][:, :], blocks[0][:, :], ALU.subtract))
                T(dve.tensor_tensor(started[:, :, :], iota_b[:, :].unsqueeze(2).to_broadcast([P, NB, E - 1]),
                                    starts[:, 1:E].unsqueeze(1).to_broadcast([P, NB, E - 1]), ALU.is_ge))
                T(dve.tensor_reduce(be_f[:, :], started[:, :, :], AX.X, ALU.add))
                T(dve.tensor_copy(block_expert[:, :], be_f[:, :]))
                T(dve.tensor_tensor(before[:, :, :], cum[a][:, :, :], prefix_ps[:, 1, :, :], ALU.subtract))
                T(dve.tensor_tensor(before[:, :, :], before[:, :, :], prefix_ps[:, 0, :, :], ALU.add))
                T(dve.tensor_scalar(starts[:, :], starts[:, :], float(P), None, ALU.mult))
                T(dve.tensor_tensor(before[:, :, :], before[:, :, :], over_t(starts[:, :]), ALU.add))
                for k in range(2):
                    T(dve.tensor_tensor(eq[:, :, :], before[:, :, :], routed[k][:, :, :], ALU.mult))
                    T(dve.tensor_reduce(pos[:, :, k], eq[:, :, :], AX.X, ALU.add))
                T(dve.tensor_tensor(eq[:, :, :], routed[0][:, :, :], routed[1][:, :, :], ALU.mult))
                T(dve.tensor_reduce(first[:, :], eq[:, :, :], AX.X, ALU.add))
                T(dve.tensor_tensor(pos[:, :, 1], pos[:, :, 1], first[:, :], ALU.add))
                T(dve.tensor_copy(pos_u[:, :, :], pos[:, :, :]))
                T(dve.tensor_copy(pos_i[:, :, :], pos[:, :, :]))
                T(dve.tensor_single_scalar(lohi_i[0][:, :, :], pos_i[:, :, :], P - 1, ALU.bitwise_and))
                T(dve.tensor_single_scalar(lohi_i[1][:, :, :], pos_i[:, :, :], 7, ALU.arith_shift_right))
                for k in range(2):
                    T(dve.tensor_copy(lohi[k][:, :, :], lohi_i[k][:, :, :]))
                lo, hi, ti = (v.rearrange("p t k -> p (t k)") for v in (lohi[0][:, :, :], lohi[1][:, :, :], t_idx[:, :, :]))
                ahead(dve, oh_used, 1 + 1)
                with dve.Fori(0, NQ // 2) as i:
                    for r in range(2):
                        q = 2 * i + r
                        dve.wait_ge(oh_used, q + 1)
                        dve.tensor_tensor(oh_lo[r][:, :, :], iota_f[:, :].unsqueeze(1).to_broadcast([P, 8, P]),
                                          lo[:, bass.ds(q * 8, 8)].unsqueeze(2).to_broadcast([P, 8, P]), ALU.is_equal)
                        dve.tensor_tensor(oh_hi[r][:, :, :], iota_b[:, :].unsqueeze(1).to_broadcast([P, 8, NB]),
                                          hi[:, bass.ds(q * 8, 8)].unsqueeze(2).to_broadcast([P, 8, NB]),
                                          ALU.is_equal).then_inc(rb, 1)
                        dve.wait_ge(rb, q + 1)
                        dve.tensor_tensor(oh_tp[r][:, :, 0, :], oh_hi[r][:, :, :],
                                          ti[:, bass.ds(q * 8, 8)].unsqueeze(2).to_broadcast([P, 8, NB]), ALU.mult)
                        dve.tensor_scalar(oh_tp[r][:, :, 1, :], oh_hi[r][:, :, :], p_idx[:, 0:1], None,
                                          ALU.mult).then_inc(oh_ready, 1)
                dve.wait_ge(oh_used, NQ + 2)
                T(dve.tensor_copy(slot_p[:, :], slots_ps[:, 1, :]))
                T(dve.scalar_tensor_tensor(slot_u[:, :], slots_ps[:, 0, :], float(P), slot_p[:, :], ALU.mult, ALU.add))

        with ExitStack() as c1:
            sb1 = lambda n, s, d=F32: c1.enter_context(nc.sbuf_tensor(f"{name}_{n}", s, d))
            ps1 = lambda n, s, d=F32: c1.enter_context(nc.psum_tensor(f"{name}_{n}", s, d))
            sem1 = lambda n: c1.enter_context(nc.semaphore(f"{name}_{n}"))
            idx = [sb1(f"idx{j}", [P, 1], U32) for j in range(R)]
            xg = [sb1(f"xg{j}", [P, C]) for j in range(R)]
            y = [sb1(f"y{j}", [P, C]) for j in range(R)]
            x_hi, x_lo, h_hi, h_lo = ([sb1(f"{n}{j}", [P, CC, P], F32R) for j in range(2)]
                                      for n in ("x_hi", "x_lo", "h_hi", "h_lo"))
            act_g, h = ([sb1(f"{n}{j}", [P, F]) for j in range(2)] for n in ("act_g", "h"))
            psX, psH = ([ps1(f"{n}{j}", [P, 4, P])[:, 0:CC, :] for j in range(2)] for n in ("psX", "psH"))
            psG, psY = ([ps1(f"{n}{j}", [P, 512]) for j in range(2)] for n in ("psG", "psY"))
            ys_t = ys_d.rearrange("(b p) c -> b p c", p=P)
            flat = lambda t: t[:, :, :].rearrange("p c n -> p (c n)")

            def blocks_of_experts(w):
                on, wait, do, raised, e = w.on, w.wait, w.do, w.raised, w.engine
                expert = {}

                def expert_of(i, k):
                    if k not in expert:
                        expert[k] = e.value_load(block_expert[0:1, bass.ds(i, 1)], min_val=0, max_val=E - 1)
                    return expert[k]

                def gather(i, j):
                    if on("pool"):
                        wait("rows_used", 1)
                    do("pool", "idx_ready", lambda: e.tensor_copy(idx[j][:, :], slot_u[:, bass.ds(i, 1)]))
                    if on("pool"):
                        wait("idx_ready")
                    do("pool", f"gathered{j}", lambda: e.indirect_dma_start(
                        xg[j][:, :], None, xn_d[:, :], bass.IndirectOffsetOnAxis(ap=idx[j][:, 0:1], axis=0)), 16)

                def split(ps, hi, lo, turned, hi_done, lo_done):
                    if on("act"):
                        wait(turned)
                    do("act", hi_done, lambda: e.activation(flat(hi), ps.rearrange("p c n -> p (c n)"), ACT.Copy))
                    if on("dve"):
                        wait(hi_done)
                    do("dve", lo_done, lambda: e.tensor_tensor(flat(lo), ps.rearrange("p c n -> p (c n)"),
                                                               flat(hi).bitcast(F32), ALU.subtract))

                def turn_x(i, j):
                    if on("pe"):
                        wait(f"gathered{j}")
                    for c in range(CC):
                        m = e.transpose(psX[j % 2][:, c, :], xg[j][:, c * P:(c + 1) * P],
                                        consts["ident"][:, :]) if on("pe") else None
                        if c == 0:
                            raised("rows_used", m)
                    raised("x_turned", m)
                    split(psX[j % 2], x_hi[j % 2], x_lo[j % 2], "x_turned", "xhi_done", "xlo_done")

                def turn_h(j, later):
                    if on("pe"):
                        wait("h_done", later)
                        for c in range(CC):
                            m = e.transpose(psH[j % 2][:, c, :], h[j % 2][:, c * P:(c + 1) * P], consts["ident"][:, :])
                    raised("h_turned", m if on("pe") else None)
                    split(psH[j % 2], h_hi[j % 2], h_lo[j % 2], "h_turned", "hhi_done", "hlo_done")

                def three(out, hi, lo, wts, at, width):
                    n = 0
                    for s, ww in ((hi, wts[0]), (lo, wts[0]), (hi, wts[1])):
                        for c in range(CC):
                            m = e.matmul(out, s[:, c, :], ww[:, bass.ds(at + c * width, width)],
                                         start=(n == 0), stop=(n == 3 * CC - 1))
                            n += 1
                    return m

                def gate_and_up(i, j, k, later):
                    def make():
                        return three(psG[j % 2][:, :], x_hi[j % 2], x_lo[j % 2], wgu, expert_of(i, k) * (CC * 2 * F), 2 * F)
                    if on("pe"):
                        wait("xlo_done", later)
                        wait("h_done", 1)
                    do("pe", "gu_done", make)
                    if on("act"):
                        wait("gu_done")
                    do("act", "silu_done", lambda: e.activation(act_g[j % 2][:, :], psG[j % 2][:, 0:F], ACT.Silu))
                    if on("dve"):
                        wait("silu_done")
                    do("dve", "h_done", lambda: e.tensor_tensor(h[j % 2][:, :], act_g[j % 2][:, :], psG[j % 2][:, F:2 * F],
                                                                ALU.mult))

                def output(i, j, k):
                    def make():
                        return three(psY[j % 2][:, 0:C], h_hi[j % 2], h_lo[j % 2], wdn, expert_of(i, k) * (CC * C), C)
                    if on("pe"):
                        wait("hlo_done")
                    do("pe", "y_done", make)
                    if on("act"):
                        wait("y_done")
                        wait(f"stored{j}")
                    do("act", "y_copied", lambda: e.activation(y[j][:, :], psY[j % 2][:, 0:C], ACT.Copy))
                    if on("sp"):
                        wait("y_copied")
                    do("sp", f"stored{j}", lambda: e.dma_start(
                        ys_t[bass.ds(i, 1), :, :].rearrange("b p c -> (b p) c"), y[j][:, :]), 16)

                def step(i, j, k):
                    left = -k if k is not None and k < 0 else 99
                    done = k if k is not None and k >= 0 else 99
                    if left > 0:
                        gate_and_up(i, j, j, 1 if left > 1 else 0)
                    if left > 2:
                        turn_x(i + 2, (j + 2) % R)
                    if left > R:
                        gather(i + R, j)
                    if done >= 2:
                        output(i - 2, (j - 2) % R, j - 2)
                    if done >= 1:
                        turn_h((j - 1) % R, 1)

                for j in range(R):
                    gather(j, j)
                turn_x(0, 0)
                turn_x(1, 1)
                for k in range(R):
                    step(k, k, k)

                def turn_of_loop(n):
                    expert.clear()
                    for k in range(R):
                        step((n + 1) * R + k, k, None)

                w.turns(NB // R - 2, turn_of_loop)
                expert.clear()
                for k in range(R):
                    step(NB - R + k, k, k - R)
                output(NB - 2, (NB - 2) % R, R - 2)
                turn_h((NB - 1) % R, 0)
                output(NB - 1, (NB - 1) % R, R - 1)
                if on("act"):
                    for j in range(R):
                        wait(f"stored{j}")

            with nc.Block(f"{name}_experts") as block:
                for me, to in (("sp", block.sync), ("pe", block.tensor), ("act", block.scalar),
                               ("dve", block.vector), ("pool", block.gpsimd)):
                    to(lambda e, me=me: blocks_of_experts(Walk(me, e, sems, waits_for)))

        with ExitStack() as c1:
            sb1 = lambda n, s, d=F32: c1.enter_context(nc.sbuf_tensor(f"{name}_{n}", s, d))
            sem1 = lambda n: c1.enter_context(nc.semaphore(f"{name}_{n}"))
            R = 4
            cidx = [[sb1(f"cidx{k}{j}", [P, 1], U32) for j in range(R)] for k in range(2)]
            yg = [[sb1(f"yg{k}{j}", [P, C]) for j in range(R)] for k in range(2)]
            half = [sb1(f"half{j}", [P, C]) for j in range(R)]
            cidx_ready, half_done, o_done = sem1("cidx_ready"), sem1("half_done"), sem1("o_done")
            got = [sem1(f"got{j}") for j in range(R)]
            o_out = sem1("o_out")
            out_t = out_d.rearrange("(t p) c -> p t c", p=P) if out_d is not None else None
            block = c1.enter_context(nc.Block(f"{name}_combine"))

            @block.gpsimd
            def _(pool):
                ahead(pool, o_done, R - 1 + 1)
                with pool.Fori(0, NT // R) as n:
                    for j in range(R):
                        t = n * R + j
                        wait_apart(pool, o_done, t + 1, passed)
                        for k in range(2):
                            pool.tensor_copy(cidx[k][j][:, :], pos_u[:, bass.ds(t, 1), k]).then_inc(cidx_ready, 1)
                        for k in range(2):
                            wait_apart(pool, cidx_ready, 2 * t + k + 1, passed)
                            pool.indirect_dma_start(yg[k][j][:, :], None, ys_d[:, :],
                                                    bass.IndirectOffsetOnAxis(ap=cidx[k][j][:, 0:1], axis=0)
                                                    ).then_inc(got[j], 16)

            @block.vector
            def _(dve):
                with dve.Fori(0, NT // R) as n:
                    for j in range(R):
                        t = n * R + j
                        dve.wait_ge(got[j], 32 * n + 32)
                        dve.scalar_tensor_tensor(half[j][:, :], yg[0][j][:, :], weight[:, 0, bass.ds(t, 1)],
                                                 X[:, bass.ds(t, 1), :].rearrange("p a c -> p (a c)"),
                                                 ALU.mult, ALU.add).then_inc(half_done, 1)
                        dve.wait_ge(half_done, t + 1)
                        dve.scalar_tensor_tensor(X[:, bass.ds(t, 1), :].rearrange("p a c -> p (a c)"), yg[1][j][:, :], weight[:, 1, bass.ds(t, 1)],
                                                 half[j][:, :], ALU.mult, ALU.add).then_inc(o_done, 1)

            @block.sync
            def _(sp):
                if out_d is None:
                    return
                with sp.Fori(0, NT // R) as n:
                    wait_apart(sp, o_done, n * R + 2 * R, passed)
                    sp.dma_start(out_t[:, bass.ds(n * R, R), :], X[:, bass.ds(n * R, R), :]).then_inc(o_out, 16)
                sp.wait_ge(o_out, 16 * (NT // R))


def attention(nc, sh, X, w_d, up_d, wc_d, rope_d, consts):
    B, T, C, CC, H, NT = sh.B, sh.T, sh.C, sh.CC, sh.H, sh.NT
    DH, D2 = sh.DH, sh.DH // 2
    NTB = T // P
    PR = H // 2
    G = B * PR
    HALF = 512
    NH = T // HALF
    assert NTB == 8 and NH == 2 and DH == 16 and C == H * DH and G % 2 == 0
    QKW = 2 * C
    scale = float(DH) ** -0.5
    ident = consts["ident"]
    waits_for = {
        "stats_done": "dve", "var_done": "act", "std_done": "dve", "rstd_done": "dve",
        "xn_done": "pe", "turned": "act", "xhi_done": "dve", "xlo_done": "pe",
        "projected": "act", "q_in": "dve", "k_in": "pool", "copied": "pe", "rot0": "dve", "rot1": "pool",
        "v_copied": "pe", "stacking0": "pool", "stacking1": "dve", "stacked": "pe", "stack_free": "pool",
        "st_done": "act", "exp_done": "pe", "pv_done": "act", "mx_done": "dve", "max_done": "pe", "mcol_done": "pe",
        "psr_full": "act", "o_full": "dve", "psr_free": "pe", "oT_done": "pe", "o_step": "dve",
        "y_free": "pool", "summed": "dve", "x_done": "pe",
    }
    with ExitStack() as ctx:
        sb = lambda n, s, d=F32: ctx.enter_context(nc.sbuf_tensor(f"a_{n}", s, d))
        sems = {n: ctx.enter_context(nc.semaphore(f"a_{n}")) for n in waits_for}
        w_c = [sb(f"w_c{k}", [P, CC, C], F32R) for k in range(2)]
        causal = sb("causal", [P, HALF])
        mask = [sb(f"mask{k}", [P, P], BF16) for k in range(2)]
        QK = sb("QK", [P, G, NTB, 2, 2, DH])
        VY = sb("VY", [P, G, NTB, 2, DH])
        vy_tile = lambda b, t: VY[:, bass.ds(b * PR, PR), t, :, :].rearrange("p g h d -> p g (h d)")

        def phase(name, schedule, count):
            with nc.Block(name) as block:
                for me, on in (("sp", block.sync), ("pe", block.tensor), ("act", block.scalar),
                               ("dve", block.vector), ("pool", block.gpsimd)):
                    on(lambda e, me=me: schedule(Walk(me, e, sems, waits_for, count)))
            w = Walk(None, None, sems, waits_for, count)
            schedule(w)
            return w.count

        def tiles(w, src, psT, x_hi, x_lo, fill, finish, extra=None, read=None):
            flat = lambda t: t[:, :, :].rearrange("p c n -> p (c n)")

            def turn(t, back=0):
                j = t % 2
                if w.on("pe"):
                    w.wait("xn_done", back)
                    w.wait("xlo_done", 1)

                for c in range(CC):
                    m = w.engine.transpose(psT[j][:, c * P:(c + 1) * P], src[j][:, c * P:(c + 1) * P],
                                           ident[:, :]) if w.on("pe") else None
                    if c == 0 and read:
                        w.raised(read, m)
                w.raised("turned", m)
                if w.on("act"):
                    w.wait("turned")
                w.do("act", "xhi_done", lambda: w.engine.activation(flat(x_hi[j]), psT[j][:, 0:C], ACT.Copy))
                if w.on("dve"):
                    w.wait("xhi_done")
                w.do("dve", "xlo_done", lambda: w.engine.tensor_tensor(
                    flat(x_lo[j]), psT[j][:, 0:C], flat(x_hi[j]).bitcast(F32), ALU.subtract))

            def batch(b, last):
                for t in range(NTB):
                    if not (last and t == NTB - 1):
                        turn(t + 1)
                    if extra and not last:
                        extra(b + 1, t)
                    if not (last and t >= NTB - 2):
                        fill(b + (t + 2) // NTB, (t + 2) % NTB)
                    finish(b, t, 0 if last and t == NTB - 1 else 1)

            fill(0, 0)
            fill(0, 1)
            turn(0, 1)
            w.turns(B - 1, lambda b: batch(b, False))
            batch(B - 1, True)

        def three(e, out, hi, lo, wts, at, n):
            k = 0
            for s, ww in ((hi, wts[0]), (lo, wts[0]), (hi, wts[1])):
                for c in range(CC):
                    m = e.matmul(out, s[:, c, :], ww[:, c, at:at + n], start=(k == 0), stop=(k == 3 * CC - 1))
                    k += 1
            return m

        with ExitStack() as c0:
            sb0 = lambda n, s, d=F32: c0.enter_context(nc.sbuf_tensor(f"a_{n}", s, d))
            w_eff = [sb0(f"w_eff{k}", [P, CC, 3 * C], F32R) for k in range(2)]
            rope = sb0("rope", [P, 2, NTB, D2])
            with ExitStack() as c1:
                sb1 = lambda n, s, d=F32: c1.enter_context(nc.sbuf_tensor(f"a_{n}", s, d))
                sem1 = lambda n: c1.enter_context(nc.semaphore(f"a_{n}"))
                down = [sb1(f"down{w}", [P, PR, C]) for w in range(3)]
                up = sb1("up", [P, 3, 2 * DH])
                wc = sb1("wc", [P, CC, C])
                ps = [[c1.enter_context(nc.psum_tensor(f"a_fold{w}{c}", [P, 512], F32)) for c in range(CC)] for w in range(3)]
                cleared, w_in, wc_in, folded, hi_done = (sem1(n) for n in ("cleared", "w_in", "wc_in", "folded", "hi_done"))
                block = c1.enter_context(nc.Block("fold"))

                @block.sync
                def _(sp):
                    for w in range(3):
                        sp.dma_start(down[w][:, :, :], w_d[w].rearrange("(r p) c -> p r c", p=P)).then_inc(w_in, 16)
                    sp.wait_ge(cleared, 1)
                    for w in range(3):
                        for h in range(2):
                            at = h * DH
                            for part in up_d[w]:
                                width = part.shape[1]
                                sp.dma_start(up[64 * h:64 * h + 64, w, at:at + width], part).then_inc(w_in, 16)
                                at += width
                    sp.dma_start(wc[:, :, :], wc_d.rearrange("(c p) n -> p c n", p=P)).then_inc(wc_in, 16)
                    sp.dma_start(rope[:, :, :, :], rope_d.rearrange("a (t p) d -> p a t d", p=P)).then_inc(wc_in, 16)
                    sp.wait_ge(wc_in, 32)

                @block.gpsimd
                def _(pool):
                    pool.memset(up[:, :, :], 0.0).then_inc(cleared, 1)
                    pool.memset(causal[:, :], 0.0).then_inc(cleared, 1)
                    pool.memset(mask[0][:, :], 0.0).then_inc(cleared, 1)
                    pool.memset(mask[1][:, :], 0.0).then_inc(cleared, 1)
                    for s in sems.values():
                        ahead(pool, s, Walk.START)
                    pool.wait_ge(cleared, 4)
                    last = causal[:, HALF - P:HALF]
                    pool.affine_select(last, last, [[-1, P]], ALU.is_ge, -BIG, 0, 1)
                    pool.affine_select(mask[0][:, :], mask[0][:, :], [[-1, P]], ALU.not_equal, 1.0, 0, 1)
                    pool.affine_select(mask[1][:, :], mask[1][:, :], [[1, P]], ALU.is_ge, -BIG, 0, -1)

                @block.tensor
                def _(pe):
                    pe.wait_ge(w_in, 16 * (3 + 2 * 5))
                    for w in range(3):
                        for c in range(CC):
                            for r in range(PR):
                                m = pe.matmul(ps[w][c][:, r * 2 * DH:(r + 1) * 2 * DH], down[w][:, r, c * P:(c + 1) * P],
                                              up[:, w, :], start=True, stop=True)
                            m.then_inc(folded, 1)

                def parts():
                    n = 0
                    for w in range(3):
                        for c in range(CC):
                            n += 1
                            yield (folded, n, ps[w][c][:, 0:C], scale if w == 0 else 1.0,
                                   [k[:, c, w * C:(w + 1) * C] for k in w_eff])
                    for c in range(CC):
                        yield wc_in, 32, wc[:, c, :], 1.0, [k[:, c, :] for k in w_c]

                @block.scalar
                def _(act):
                    for sem, n, src, s, (hi, _) in parts():
                        act.wait_ge(sem, n)
                        act.activation(hi, src, ACT.Copy, scale=s).then_inc(hi_done, 1)

                @block.vector
                def _(dve):
                    for k, (_, _, src, s, (hi, lo)) in enumerate(parts()):
                        dve.wait_ge(hi_done, k + 1)
                        dve.scalar_tensor_tensor(lo, src, s, hi.bitcast(F32), ALU.mult, ALU.subtract)

            with ExitStack() as c1:
                sb1 = lambda n, s, d=F32: c1.enter_context(nc.sbuf_tensor(f"a_{n}", s, d))
                stats, mv = sb1("stats", [P, NTB, 6]), sb1("mv", [P, NTB, 2])
                mean, std, rstd = sb1("mean", [P, NTB]), sb1("std", [P, NTB]), sb1("rstd", [P, NTB])
                XN = [sb1(f"XN{j}", [P, C]) for j in range(2)]
                x_hi, x_lo = ([sb1(f"{n}{j}", [P, CC, P], F32R) for j in range(2)] for n in ("x_hi", "x_lo"))
                rot_a = [sb1(f"rot_a{w}", [P, PR, 2, D2]) for w in range(2)]
                rot_b = [sb1(f"rot_b{w}", [P, PR, 2, D2]) for w in range(2)]
                psT = [c1.enter_context(nc.psum_tensor(f"a_psT{j}", [P, HALF], F32)) for j in range(2)]
                psP = [c1.enter_context(nc.psum_tensor(f"a_psP{j}", [P, 2, HALF], F32)) for j in range(2)]

                def project_all(w):
                    on, wait, do, e = w.on, w.wait, w.do, w.engine
                    row = lambda b, t: X[:, bass.ds(b * NTB + t, 1), :].rearrange("p a c -> p (a c)")

                    def stat(b, t):
                        do("dve", "stats_done", lambda: e.bn_stats(stats[:, t, :], row(b, t)))

                    def aggregate(t):
                        if on("dve"):
                            wait("stats_done", NTB - 1 - t)
                        do("dve", "var_done", lambda: e.bn_aggr(mv[:, t, :], stats[:, t, :]))

                    def deviations():
                        if on("act"):
                            wait("var_done")
                        do("act", "std_done", lambda: e.activation(std[:, :], mv[:, :, 1], ACT.Sqrt,
                                                                   bias=consts["eps"][:, 0:1]))
                        if on("dve"):
                            wait("std_done")
                        do("dve", "rstd_done", lambda: e.tensor_copy(mean[:, :], mv[:, :, 0]))
                        do("dve", "rstd_done", lambda: e.reciprocal(rstd[:, :], std[:, :]))

                    def fill(b, t):
                        if on("dve"):
                            wait("rstd_done")
                        do("dve", "xn_done", lambda: e.tensor_scalar(XN[t % 2][:, :], row(b, t), mean[:, t:t + 1],
                                                                     rstd[:, t:t + 1], ALU.subtract, ALU.mult))

                    def extra(b, t):
                        if t < 4:
                            if t == 0 and on("dve"):
                                wait("rstd_done")
                            stat(b, 2 * t)
                            stat(b, 2 * t + 1)
                        elif t == 4:
                            for k in range(NTB):
                                aggregate(k)
                        elif t == 6:
                            deviations()

                    def rotate(b, t, name, which, given):
                        ee = QK[:, bass.ds(b * PR, PR), t, which, :, D2:DH]
                        pairs = lambda a, k: a.rearrange("p g h (i two) -> p g h i two", two=2)[:, :, :, :, k]
                        table = lambda a: rope[:, a, t, :].unsqueeze(1).unsqueeze(1).to_broadcast([P, PR, 2, D2])
                        if on(name):
                            wait(f"rot{which}")
                            wait(given)
                        do(name, f"rot{which}", lambda: e.tensor_tensor(rot_a[which][:, :, :, :], ee, table(0), ALU.mult))
                        for k in range(2):
                            do(name, f"rot{which}", lambda k=k: e.tensor_tensor(
                                pairs(rot_b[which][:, :, :, :], k), pairs(ee, 1 - k), pairs(table(1), k), ALU.mult))
                        if on(name):
                            wait(f"rot{which}")
                        do(name, f"rot{which}", lambda: e.tensor_tensor(ee, rot_a[which][:, :, :, :], rot_b[which][:, :, :, :], ALU.add))

                    def finish(b, t, back):
                        j = t % 2
                        if on("pe"):
                            wait("xlo_done", back)
                            wait("copied", 1)

                        def make():
                            three(e, psP[j][:, 0, :], x_hi[j], x_lo[j], w_eff, 0, QKW)
                            return three(e, psP[j][:, 1, 0:C], x_hi[j], x_lo[j], w_eff, QKW, C)
                        do("pe", "projected", make)
                        if on("act"):
                            wait("projected")
                        for k, given in enumerate(("q_in", "k_in")):
                            do("act", given, lambda: e.activation(
                                QK[:, bass.ds(b * PR, PR), t, k, :, :].rearrange("p g h d -> p g (h d)"),
                                psP[j][:, 0, k * C:(k + 1) * C].rearrange("p (g d) -> p g d", g=PR), ACT.Copy))
                        do("act", "copied", lambda: e.activation(
                            vy_tile(b, t), psP[j][:, 1, 0:C].rearrange("p (g d) -> p g d", g=PR), ACT.Copy))
                        rotate(b, t, "dve", 0, "q_in")
                        rotate(b, t, "pool", 1, "k_in")

                    for t in range(NTB):
                        stat(0, t)
                    for t in range(NTB):
                        aggregate(t)
                    deviations()
                    tiles(w, XN, psT, x_hi, x_lo, fill, finish, extra)

                count = phase("project", project_all, None)

        with ExitStack() as c1:
            sb1 = lambda n, s, d=F32: c1.enter_context(nc.sbuf_tensor(f"a_{n}", s, d))
            VP = [sb1(f"VP{r}", [P, NTB, 2, 32]) for r in range(2)]
            ROW = 2 * DH
            stack = [sb1(f"stack{w}", [P, NTB, 2, 64]) for w in range(2)]
            QT = [sb1(f"QT{r}", [P, T], F32R) for r in range(2)]
            KT = [[sb1(f"KT{r}{h}", [P, T], F32R) for h in range(2)] for r in range(2)]
            prob = [sb1(f"prob{r}", [P, 2, HALF]) for r in range(4)]
            mpart = [sb1(f"mpart{r}", [P, 2, NTB, 2]) for r in range(2)]
            mcol = [sb1(f"mcol{r}", [P, 4, P]) for r in range(2)]
            OT = sb1("OT", [P, HALF])
            o_sum = sb1("o_sum", [P, 4, 2, DH + 1])
            o_rec = sb1("o_rec", [P, 4, 2, 1])
            psS = [c1.enter_context(nc.psum_tensor(f"a_psS{j}", [P, 2, HALF], F32)) for j in range(2)]
            psM = [c1.enter_context(nc.psum_tensor(f"a_psM{j}", [P, HALF], F32)) for j in range(2)]
            psO = c1.enter_context(nc.psum_tensor("a_psO", [P, HALF], F32))
            psR = c1.enter_context(nc.psum_tensor("a_psR", [P, HALF], F32))
            init = c1.enter_context(nc.semaphore("a_init"))

            with nc.Block("clear") as block:
                @block.gpsimd
                def _(pool):
                    for w in range(2):
                        pool.memset(stack[w][:, :, :, :], 0.0).then_inc(init, 1)
                    for r in range(2):
                        pool.memset(VP[r][:, :, :, :], 0.0).then_inc(init, 1)
                    pool.wait_ge(init, 4)
                    pool.memset(stack[1][:, :, :, ROW:ROW + 1], 1.0)
                    for r in range(2):
                        pool.memset(VP[r][:, :, :, DH:DH + 1], 1.0)

                @block.vector
                def _(dve):
                    for r in range(2):
                        for h in range(2):
                            dve.memset(KT[r][h][64 * (1 - h):64 * (1 - h) + 64, :].bitcast(F32), 0.0)
                    dve.memset(psO[:, :], 0.0)
                    for qh in range(NH):
                        dve.memset(mcol[qh][:, :, :], 0.0)

            CHUNKS = []
            for qt in range(NTB):
                lo = qt * P // HALF * HALF
                for first in range(0, lo, HALF):
                    CHUNKS += [(h, qt, first, HALF, False) for h in range(2)]
                CHUNKS += [(h, qt, lo, (qt + 1) * P - lo, True) for h in range(2)]
            STEPS = [(qh, kt) for qh in range(NH) for kt in range((qh + 1) * HALF // P)]
            NS = len(STEPS)
            PER_STEP = len(CHUNKS) // NS
            assert len(CHUNKS) == PER_STEP * NS and PER_STEP == 2 and NS == 12

            def span(qh, kt):
                first = max(kt * P - qh * HALF, 0)
                return first, HALF - first

            def heads(w):
                on, wait, do, e = w.on, w.wait, w.do, w.engine

                def stack_part(pair, k, which):
                    name = ("pool", "dve")[which]
                    src = QK[:, bass.ds(pair, 1), :, which, :, :].rearrange("p g t h d -> p (g t) h d")
                    hi_at = ((0, DH), (0, ROW + 1))[which]
                    lo_at = (ROW + 1, DH)[which]
                    at = lambda a: stack[which][:, :, :, a:a + DH]
                    if k < 2:
                        if k == 0 and which == 0 and on(name):
                            wait("stack_free")
                        do(name, f"stacking{which}", lambda: e.tensor_copy(at(hi_at[k]).bitcast(F32R), src))
                    else:
                        if on(name):
                            wait(f"stacking{which}")
                        do(name, "stacked", lambda: e.tensor_tensor(at(lo_at), src, at(0), ALU.subtract))

                def misc_wait():
                    if on("pe"):
                        wait("psr_free")

                def four(make, first=None):
                    for k in range(4):
                        m = make(k) if on("pe") else None
                        if k == 0 and first:
                            w.raised(first, m)
                    return m

                def turn(which, qh, copies):
                    misc_wait()
                    if on("pe"):
                        wait("stacked")
                    w.raised("psr_full", four(lambda k: e.transpose(
                        psR[:, k * P:(k + 1) * P],
                        stack[which][:, qh * 4 + k, :, :].rearrange("p h d -> p (h d)"), ident[:, :])))
                    if on("act"):
                        wait("psr_full")
                    for out, rows in copies:
                        do("act", "psr_free", lambda: e.activation(out[rows, qh * HALF:(qh + 1) * HALF],
                                                                    psR[rows, :], ACT.Copy))

                def turn_q(r, qh):
                    turn(0, qh, [(QT[r], slice(0, P))])

                def turn_k(r, qh):
                    turn(1, qh, [(KT[r][h], slice(64 * h, 64 * h + 64)) for h in range(2)])

                def chunk(r, c):
                    h, qt, first, n, diagonal = CHUNKS[c]
                    b = c % 2
                    if on("pe"):
                        wait("max_done", 1)
                        if c in (0, 8, 10):
                            wait("psr_free", 2 if c == 8 else 0)
                    do("pe", "mx_done", lambda: e.matmul(psM[b][:, 0:n], QT[r][:, qt * P:(qt + 1) * P],
                                                         KT[r][h][:, first:first + n], start=True, stop=True))
                    slot = 0 if first == 0 else 1
                    out = mpart[r][:, h, qt, slot:slot + 1]
                    if on("dve"):
                        wait("mx_done")
                    if diagonal:
                        do("dve", "max_done", lambda: e.tensor_tensor_reduce(
                            psM[b][:, 0:n], psM[b][:, 0:n], causal[:, HALF - n:HALF], 1.0, -3e38, ALU.add, ALU.max, out))
                    else:
                        do("dve", "max_done", lambda: e.tensor_reduce(out, psM[b][:, 0:n], AX.X, ALU.max))

                def max_column(r, qh):
                    out = mcol[qh][:, :, ROW:ROW + 65:64]
                    if qh == 0:
                        do("dve", "mcol_done", lambda: e.tensor_copy(out, mpart[r][:, :, 0:4, 0].rearrange("p h t -> p t h")))
                    else:
                        do("dve", "mcol_done", lambda: e.tensor_tensor(
                            out, mpart[r][:, :, 4:8, 0].rearrange("p h t -> p t h"),
                            mpart[r][:, :, 4:8, 1].rearrange("p h t -> p t h"), ALU.max))

                def max_row(r, qh, first=None):
                    misc_wait()
                    if on("pe"):
                        wait("mcol_done")
                    w.raised("psr_full", four(lambda k: e.transpose(
                        psR[:, k * P:(k + 1) * P], mcol[qh][:, k, :], ident[:, :]), first))
                    if on("act"):
                        wait("psr_full")
                    for at in (ROW, ROW + 64):
                        do("act", "psr_free", lambda: e.activation(QT[r][at:at + 1, qh * HALF:(qh + 1) * HALF],
                                                                   psR[at:at + 1, :], ACT.Copy, scale=-1.0))

                def scores(r, s):
                    qh, kt = STEPS[s]
                    first, n = span(qh, kt)
                    diagonal = kt * P >= qh * HALF
                    b = s % 2
                    if on("pe"):
                        wait("exp_done", 1)
                        if kt == 0:
                            wait("psr_free")

                    def make():
                        for h in range(2):
                            m = e.matmul(psS[b][:, h, 0:n], KT[r][h][:, kt * P:(kt + 1) * P],
                                         QT[r][:, qh * HALF + first:(qh + 1) * HALF], start=True, stop=not diagonal)
                            if diagonal:
                                m = e.matmul(psS[b][:, h, 0:P], mask[0][:, :], mask[1][:, :], start=False, stop=True)
                        return m
                    do("pe", "st_done", make)
                    if on("act"):
                        wait("st_done")
                    do("act", "exp_done", lambda: e.activation(prob[s % 4][:, :, 0:n], psS[b][:, :, 0:n], ACT.Exp))

                def values(s, r, behind):
                    if on("pe"):
                        wait("exp_done", behind)
                        if s == 1:
                            wait("v_copied")
                        if STEPS[s][1] == 1:
                            wait("oT_done")

                    def make():
                        for k in (s - 1, s):
                            qh, kt = STEPS[k]
                            first, n = span(qh, kt)
                            last = (qh + 1) * HALF // P - 2
                            for h in range(2):
                                j = 2 * h + kt % 2
                                m = e.matmul(psO[32 * j:32 * j + 32, first:HALF],
                                             VP[r][:, kt, h, :],
                                             prob[k % 4][:, h, 0:n], start=(kt < 2), stop=(kt >= last))
                        return m
                    if STEPS[s] in ((0, HALF // P - 1), (1, NTB - 1)):
                        do("pe", "pv_done", make)
                    elif on("pe"):
                        make()

                def copy_v(r, pair):
                    if on("pool"):
                        wait("stack_free")
                    do("pool", "v_copied", lambda: e.tensor_copy(
                        VP[r][:, :, :, 0:DH], VY[:, bass.ds(pair, 1), :, :, :].rearrange("p g t h d -> p (g t) h d")))

                def out_copy():
                    if on("act"):
                        wait("pv_done")
                    do("act", "oT_done", lambda: e.activation(OT[:, :], psO[:, :], ACT.Copy))

                def out_rows(qh, pair, drained):
                    misc_wait()
                    if on("pe"):
                        wait("oT_done")
                    w.raised("o_full", four(lambda k: e.transpose(
                        psR[:, k * P:(k + 1) * P], OT[:, k * P:(k + 1) * P], ident[:, :])))
                    rows = lambda q, k: psR[:, :].rearrange("p (t h k d) -> p t h k d", h=2, k=2, d=32)[:, q, :, k, 0:DH + 1]
                    q = slice(1 if qh == 0 else 0, 4)

                    def even():
                        if on("dve"):
                            wait("o_full")
                            wait("o_step")
                        do("dve", "o_step", lambda: e.tensor_copy(o_sum[:, :, :, :], rows(slice(0, 4), 0)))

                    def odd():
                        if on("dve"):
                            wait("o_step")
                        do("dve", "psr_free", lambda: e.tensor_tensor(o_sum[:, q, :, :], rows(q, 1), o_sum[:, q, :, :], ALU.add))

                    def invert():
                        if drained and on("dve"):
                            e.drain()
                        do("dve", "o_step", lambda: e.reciprocal(o_rec[:, :, :, :], o_sum[:, :, :, DH:DH + 1]))

                    def divide():
                        if on("dve"):
                            wait("o_step")
                        do("dve", "o_step", lambda: e.tensor_tensor(
                            VY[:, bass.ds(pair, 1), qh * 4:qh * 4 + 4, :, :].rearrange("p g t h d -> p (g t) h d"),
                            o_sum[:, :, :, 0:DH], o_rec[:, :, :, :].to_broadcast([P, 4, 2, DH]), ALU.mult))
                    return even, odd, invert, divide

                def body(r, pair, do_s=True, do_m=True, do_t=True, tail=True):
                    nxt = 1 - r
                    slots = {}

                    def between(step, parts):
                        for at, part in zip((0, 1, 4, 5), parts):
                            slots[2 * step + at] = part

                    for s in range(NS):
                        if do_m:
                            chunk(nxt, PER_STEP * s)
                        if 2 * s in slots:
                            slots[2 * s]()
                        if do_s:
                            scores(r, s)
                        if do_m:
                            chunk(nxt, PER_STEP * s + 1)
                        if s == 0 and do_s:
                            if not do_m and on("dve"):
                                e.drain()
                            max_column(r, 1)
                        if s == 4 and do_m:
                            max_column(nxt, 0)
                        if 2 * s + 1 in slots:
                            slots[2 * s + 1]()
                        if s == 1 and do_s:
                            max_row(r, 1)
                        if s == 2 and do_m:
                            turn_q(nxt, 1)
                        if s == 3 and do_m:
                            turn_k(nxt, 1)
                        if s == 4 and tail and do_s:
                            between(5, out_rows(1, pair - 1, not do_t))
                        if s == 6 and do_m:
                            max_row(nxt, 0, "stack_free")
                        if s == 7 and do_s:
                            between(8, out_rows(0, pair, not do_t))
                        if s == 9 and do_t:
                            turn_q(r, 0)
                        if s == 10 and do_t:
                            turn_k(r, 0)
                        if do_s and s % 2 and s >= 3:
                            values(s - 2, r, 2)
                        if do_s and s == 5:
                            out_copy()
                        if do_s and tail and s == 1:
                            values(NS - 1, nxt, 2)
                            out_copy()
                        if do_t and s in (4, 5, 6):
                            stack_part(pair + 2, s - 4, 1)
                        if do_t and s in (6, 7, 8):
                            stack_part(pair + 2, s - 6, 0)
                        if do_m and s == 9:
                            copy_v(nxt, pair + 1)

                for k in range(3):
                    for which in range(2):
                        stack_part(0, k, which)
                turn_q(0, 0)
                turn_k(0, 0)
                body(1, -1, do_s=False)
                body(0, 0, tail=False)

                def two(i):
                    body(1, i * 2 + 1)
                    body(0, i * 2 + 2)

                w.turns(G // 2 - 2, two)
                body(1, G - 3)
                body(0, G - 2, do_t=False)
                body(1, G - 1, do_m=False, do_t=False)
                values(NS - 1, 1, 0)
                out_copy()
                for part in out_rows(1, G - 1, True):
                    part()

            count = phase("heads", heads, count)

        with ExitStack() as c1:
            sb1 = lambda n, s, d=F32: c1.enter_context(nc.sbuf_tensor(f"a_{n}", s, d))
            Y = [sb1(f"Y{j}", [P, C]) for j in range(2)]
            y_hi, y_lo = ([sb1(f"{n}{j}", [P, CC, P], F32R) for j in range(2)] for n in ("y_hi", "y_lo"))
            psT = [c1.enter_context(nc.psum_tensor(f"a_psYT{j}", [P, HALF], F32)) for j in range(2)]
            psW = [c1.enter_context(nc.psum_tensor(f"a_psW{j}", [P, HALF], F32)) for j in range(2)]

            def output(w):
                on, wait, do, e = w.on, w.wait, w.do, w.engine

                def fill(b, t):
                    if on("pool"):
                        wait("y_free")
                    do("pool", "xn_done", lambda: e.tensor_copy(Y[t % 2][:, :].rearrange("p (g d) -> p g d", g=PR),
                                                                vy_tile(b, t)))

                def finish(b, t, back):
                    j = t % 2
                    if on("pe"):
                        wait("xlo_done", back)
                        wait("x_done", 1)
                    do("pe", "summed", lambda: three(e, psW[j][:, 0:C], y_hi[j], y_lo[j], w_c, 0, C))
                    row = X[:, bass.ds(b * NTB + t, 1), :].rearrange("p a c -> p (a c)")
                    if on("dve"):
                        wait("summed")
                    do("dve", "x_done", lambda: e.tensor_tensor(row, psW[j][:, 0:C], row, ALU.add))

                tiles(w, Y, psT, y_hi, y_lo, fill, finish, read="y_free")

            phase("output", output, count)


def make_constants(nc, sh, ctx):
    NT, E, NB = sh.NT, sh.E, sh.NB
    sb = lambda n, s, d=F32: ctx.enter_context(nc.sbuf_tensor(n, s, d))
    c = {
        "ident": sb("ident", [P, P]), "ones": sb("ones", [P, P]), "upper": sb("upper", [P, P]),
        "iota_e": sb("iota_e", [P, E]), "iota_e8": sb("iota_e8", [P, E]), "iota_f": sb("iota_f", [P, P]),
        "iota_b": sb("iota_b", [P, NB]), "eye_e": sb("eye_e", [P, E, E]), "t_idx": sb("t_idx", [P, NT, 2]),
        "p_idx": sb("p_idx", [P, 1]), "eps": sb("eps", [P, 1]),
    }
    with nc.semaphore("made") as made, nc.Block("constants") as block:
        @block.gpsimd
        def _(pool):
            pool.memset(c["ident"][:, :], 0.0).then_inc(made, 1)
            pool.memset(c["eye_e"][:, :, :], 0.0).then_inc(made, 1)
            pool.memset(c["ones"][:, :], 1.0).then_inc(made, 1)
            pool.memset(c["eps"][:, :], EPS)
            small = dict(allow_small_or_imprecise_dtypes=True)
            pool.iota(c["iota_e"][:, :], [[1, E]], 0, 0, **small)
            pool.iota(c["iota_e8"][:, :], [[1, E]], E, 0, **small)
            pool.iota(c["iota_f"][:, :], [[1, P]], 0, 0, **small)
            pool.iota(c["iota_b"][:, :], [[1, NB]], 0, 0, **small)
            pool.iota(c["t_idx"][:, :, :], [[1, NT], [0, 2]], 0, 0, **small)
            pool.iota(c["p_idx"][:, :], [[0, 1]], 0, 1, **small)
            pool.wait_ge(made, 3)
            pool.affine_select(c["ident"][:, :], c["ident"][:, :], [[-1, P]], ALU.not_equal, 1.0, 0, 1)
            pool.affine_select(c["eye_e"][:, :, :], c["eye_e"][:, :, :], [[-1, E], [1, E]], ALU.not_equal, 1.0, 0, 0)
            pool.affine_select(c["upper"][:, :], c["ones"][:, :], [[1, P]], ALU.is_gt, 0.0, 0, -1)
    return c


def program(nc, sh, x, wq_down, wk_down, wv_down, ups, wc, gate, gate_up, down, sim, rope, out):
    dram = lambda n, s: nc.dram_tensor(n, s, F32).ap()
    xn, ys = dram("xn", [sh.N, sh.C]), dram("ys", [sh.NB * P, sh.C])
    with ExitStack() as ctx:
        consts = make_constants(nc, sh, ctx)
        passed = ctx.enter_context(nc.semaphore("passed"))
        X = ctx.enter_context(nc.sbuf_tensor("X", [P, sh.NT, sh.C], F32))

        def ffn(name, src, dst):
            with ExitStack() as c:
                wgu = [c.enter_context(nc.sbuf_tensor(f"{name}_wgu{k}", [P, sh.E * sh.CC * 2 * sh.F], F32R)) for k in range(2)]
                wdn = [c.enter_context(nc.sbuf_tensor(f"{name}_wdn{k}", [P, sh.E * sh.CC * sh.C], F32R)) for k in range(2)]
                moe(nc, sh, name, X, src, dst, gate, sim, gate_up, down, xn, ys, wgu, wdn, consts, passed)

        ffn("m1", x, None)
        attention(nc, sh, X, (wq_down, wk_down, wv_down), ups, wc, rope, consts)
        ffn("m2", None, out)


def rope_tables(T, D):
    inv = np.float32(1.0) / np.float32(10000.0) ** (np.arange(0, D, 2, dtype=np.float32) / np.float32(D))
    freqs = np.arange(T, dtype=np.float32)[:, None] * inv[None, :]
    emb = np.concatenate((freqs, freqs), axis=-1)
    sign = np.where(np.arange(D) % 2 == 0, np.float32(-1), np.float32(1))
    return np.stack((np.cos(emb), np.sin(emb) * sign)).astype(np.float32)


def kernel(**inputs):
    import concourse.bacc as bacc
    from concourse.bass_utils import run_bass_kernel_spmd

    a = {k[3:]: np.asarray(v) for k, v in inputs.items()}
    x = a["attn_x"]
    sh = Shapes(x, a["ffn_gate_up_proj"])
    given = {
        "x": x.reshape(sh.N, sh.C),
        "wq_down": a["attn_Wq_down"].T, "wk_down": a["attn_Wk_down"].T, "wv_down": a["attn_Wv_down"].T,
        "wq_up_c": a["attn_Wq_up_c"], "wq_up_e": a["attn_Wq_up_e"],
        "wk_up_c": a["attn_Wk_up_c"], "wk_up_e": a["attn_Wk_up_e"], "wv_up": a["attn_Wv_up"], "wc": a["attn_Wc"],
        "gate": a["ffn_gate_weight"].T, "gate_up": a["ffn_gate_up_proj"].transpose(0, 2, 1),
        "down": a["ffn_down_proj"].transpose(0, 2, 1), "sim": a["ffn_similarity_matrix"],
        "rope": rope_tables(sh.T, sh.DH // 2),
    }
    given = {k: np.ascontiguousarray(v) for k, v in given.items()}
    nc = bacc.Bacc("TRN2", target_bir_lowering=False, num_devices=1)
    d = {k: nc.dram_tensor(k, list(v.shape), F32, kind="ExternalInput").ap() for k, v in given.items()}
    out = nc.dram_tensor("out", [sh.N, sh.C], F32, kind="ExternalOutput").ap()
    ups = ((d["wq_up_c"], d["wq_up_e"]), (d["wk_up_c"], d["wk_up_e"]), (d["wv_up"],))
    program(nc, sh, d["x"], d["wq_down"], d["wk_down"], d["wv_down"], ups, d["wc"], d["gate"], d["gate_up"],
            d["down"], d["sim"], d["rope"], out)
    r = run_bass_kernel_spmd(nc, [given], core_ids=[0])
    return r.results[0]["out"].reshape(sh.B, sh.T, sh.C)
```

```python
from contextlib import ExitStack

import numpy as np

import concourse.bass as bass
import concourse.mybir as mybir

F32 = mybir.dt.float32
F32R = mybir.dt.float32r
BF16 = mybir.dt.bfloat16
I32 = mybir.dt.int32
U32 = mybir.dt.uint32
ALU = mybir.AluOpType
ACT = mybir.ActivationFunctionType
AX = mybir.AxisListType

P = 128
EPS = 1e-5
THRESHOLD = 0.7
BIG = 1e30


class Shapes:

    def __init__(self, x, gate_up, H=16):
        self.B, self.T, self.C = x.shape
        self.N = self.B * self.T
        self.NT = self.N // P
        self.E, f2, _ = gate_up.shape
        self.F = f2 // 2
        self.K = 2
        self.NB = -(-(self.K * self.N // P + self.E - 1) // 4) * 4
        self.CC = self.C // P
        self.H = H
        self.DH = self.C // H
        assert self.C == 256 and self.F == 256 and self.NT % 8 == 0 and self.NB <= P


def ahead(engine, sem, n):
    engine.sem_inc(sem, n)


def wait_apart(engine, sem, value, passed):
    engine.wait_ge(sem, value)
    engine.sem_inc(passed, 1)


class Seq:

    def __init__(self, engine, sem):
        self.engine, self.sem, self.n = engine, sem, 0

    def then(self, instruction):
        self.n += 1
        instruction.then_inc(self.sem, 1)
        self.engine.wait_ge(self.sem, self.n)


class Walk:

    START = 32

    @staticmethod
    def rises(sem):
        return sem.startswith("gathered")

    @classmethod
    def start(cls, sem):
        return 0 if cls.rises(sem) else cls.START

    def __init__(self, me, engine, sems, waits_for, count=None):
        self.me, self.engine, self.sems, self.waits_for = me, engine, sems, waits_for
        self.count = dict(count) if count else {s: 0 for s in sems}
        self.waited, self.before = {}, {}

    def on(self, name):
        return name == self.me

    def wait(self, sem, back=0):
        if self.me is None:
            return
        assert self.waits_for[sem] == self.me, (sem, self.me)
        n = self.count[sem] - back
        if n > self.waited.get(sem, 0):
            self.engine.wait_ge(self.sems[sem], n + self.start(sem) + self.before.get(sem, 0))
            self.waited[sem] = n

    def raised(self, sem, instruction=None, by=1):
        self.count[sem] += by
        if instruction is not None:
            instruction.then_inc(self.sems[sem], by)

    def do(self, name, sem, make, by=1):
        self.raised(sem, make() if self.on(name) else None, by)

    def turns(self, n, body):
        before, me = dict(self.count), self.me
        self.me = None
        body(0)
        per_turn = {s: self.count[s] - before[s] for s in self.count}
        self.me, self.count = me, dict(before)
        if me is not None:
            with self.engine.Fori(0, n) as i:
                self.waited = {s: -self.START for s in self.sems}
                self.before = {s: i * raises for s, raises in per_turn.items() if raises and self.rises(s)}
                body(i)
                for s, raises in per_turn.items():
                    if raises and self.waits_for[s] == me and not self.rises(s):
                        assert self.waited[s] + self.start(s) >= raises, s
                        self.engine.sem_inc(self.sems[s], -raises)
            self.waited = {s: -self.START for s in self.sems}
        self.before = {}
        self.count = {s: v + n * per_turn[s] if self.rises(s) else v for s, v in before.items()}


class Weights:

    def __init__(self, nc, sh, name, ctx, gu_d, dn_d, wgu, wdn, passed):
        self.sh, self.gu_d, self.dn_d, self.wgu, self.wdn, self.passed = sh, gu_d, dn_d, wgu, wdn, passed
        self.ng, self.nd = sh.CC * 2 * sh.F, sh.CC * sh.C
        self.stage = [ctx.enter_context(nc.sbuf_tensor(f"{name}_w_stage{j}", [P, self.ng + self.nd], F32)) for j in range(2)]
        self.loaded = [ctx.enter_context(nc.semaphore(f"{name}_w_loaded{j}")) for j in range(2)]
        self.hi_done, self.lo_done = (ctx.enter_context(nc.semaphore(f"{name}_w_{n}_done")) for n in ("hi", "lo"))

    def load(self, sp):
        ahead(sp, self.lo_done, 2 * 2 + 1)
        with sp.Fori(0, self.sh.E // 2) as i:
            for j in range(2):
                wait_apart(sp, self.lo_done, 2 * (2 * i + j) + 1 + 2, self.passed)
                for part, src in ((slice(0, self.ng), self.gu_d), (slice(self.ng, None), self.dn_d)):
                    sp.dma_start(self.stage[j][:, part].rearrange("p (c f) -> p c f", c=self.sh.CC),
                                 src[bass.ds(i * 2 + j, 1), :, :].rearrange("e (c p) f -> p (e c) f", p=P)
                                 ).then_inc(self.loaded[j], 16)

    def parts(self, j, i):
        ng, nd = self.ng, self.nd
        yield self.stage[j][:, 0:ng], [w[:, bass.ds((i * 2 + j) * ng, ng)] for w in self.wgu]
        yield self.stage[j][:, ng:], [w[:, bass.ds((i * 2 + j) * nd, nd)] for w in self.wdn]

    def round(self, act):
        with act.Fori(0, self.sh.E // 2) as i:
            for j in range(2):
                act.wait_ge(self.loaded[j], 32 * i + 32)
                for src, (hi, _) in self.parts(j, i):
                    act.activation(hi, src, ACT.Copy).then_inc(self.hi_done, 1)

    def rest(self, pool):
        with pool.Fori(0, self.sh.E // 2) as i:
            for j in range(2):
                for n, (src, (hi, lo)) in enumerate(self.parts(j, i)):
                    wait_apart(pool, self.hi_done, 2 * (2 * i + j) + n + 1, self.passed)
                    pool.tensor_tensor(lo, src, hi.bitcast(F32), ALU.subtract).then_inc(self.lo_done, 1)


def moe(nc, sh, name, X, x_d, out_d, gate_d, sim_d, gu_d, dn_d, xn_d, ys_d, wgu, wdn, consts, passed,
        extra=None):
    NT, E, C, F, CC, NB = sh.NT, sh.E, sh.C, sh.F, sh.CC, sh.NB
    G = 8
    NG = NT // G
    ctx = ExitStack()
    with ctx:
        sb = lambda n, s, d=F32: ctx.enter_context(nc.sbuf_tensor(f"{name}_{n}", s, d))
        sem = lambda n: ctx.enter_context(nc.semaphore(f"{name}_{n}"))
        weight = sb("weight", [P, 2, NT])
        pos_u = sb("pos_u", [P, NT, 2], U32)
        slot_u = sb("slot_u", [P, NB], U32)
        block_expert = sb("block_expert", [P, NB], I32)
        R = 4
        U = 8
        assert (NB - 2 * R) % U == 0
        waits_for = {
            "idx_ready": "pool", "rows_used": "pool", "x_turned": "act", "xhi_done": "dve", "xlo_done": "pe",
            "gu_done": "act", "silu_done": "dve", "h_done": "pe", "h_turned": "act", "hhi_done": "dve",
            "hlo_done": "pe", "y_done": "act", "y_copied": "sp",
        }
        waits_for |= {f"gathered{j}": "pe" for j in range(R)} | {f"stored{j}": "act" for j in range(R)}
        sems = {n: sem(f"b_{n}") for n in waits_for}

        with ExitStack() as c1:
            sb1 = lambda n, s, d=F32: c1.enter_context(nc.sbuf_tensor(f"{name}_{n}", s, d))
            ps1 = lambda n, s, d=F32: c1.enter_context(nc.psum_tensor(f"{name}_{n}", s, d))
            sem1 = lambda n: c1.enter_context(nc.semaphore(f"{name}_{n}"))
            logits = ps1("logits", [P, 512])
            with ExitStack() as c2:
                sb2 = lambda n, s, d=F32: c2.enter_context(nc.sbuf_tensor(f"{name}_{n}", s, d))
                XN = [sb2(f"XN{j}", [P, G, C]) for j in range(2)]
                gate = sb2("gate", [P, CC, E])
                stats = sb2("stats", [P, G, 6])
                mv = sb2("mv", [P, G, 2])
                std, rstd = sb2("std", [P, G]), sb2("rstd", [P, G])
                xT = [sb2(f"xT{r}", [P, 2, CC, P]) for r in range(2)]
                psT = [c2.enter_context(nc.psum_tensor(f"{name}_psT{r}", [P, 2, CC, P], F32)) for r in range(2)]
                sem2 = lambda n: c2.enter_context(nc.semaphore(f"{name}_{n}"))
                x_in = [sem2(f"x_in{j}") for j in range(2)]
                xn_out = [sem2(f"xn_out{j}") for j in range(2)]
                gate_in, dv, xn_ready, std_done = (sem2(n) for n in ("gate_in", "dv", "xn_ready", "std_done"))
                turned, evacuated, scored = sem2("turned"), sem2("evacuated"), sem2("scored")
                x_t = x_d.rearrange("(t p) c -> p t c", p=P) if x_d is not None else None
                xn_t = xn_d.rearrange("(t p) c -> p t c", p=P)
                NI = NG // 2
                ND = 2 * G + 1
                block = c2.enter_context(nc.Block(f"{name}_norm"))

                @block.sync
                def _(sp):
                    sp.dma_start(gate[:, :, :], gate_d.rearrange("(c p) e -> p c e", p=P)).then_inc(gate_in, 16)

                    def load(i, j):
                        if x_d is not None:
                            sp.dma_start(X[:, bass.ds((2 * i + j) * G, G), :],
                                         x_t[:, bass.ds((2 * i + j) * G, G), :]).then_inc(x_in[j], 16)

                    def store(i, j):
                        wait_apart(sp, xn_ready, (2 * i + j) * G + G, passed)
                        sp.dma_start(xn_t[:, bass.ds((2 * i + j) * G, G), :], XN[j][:, :, :]).then_inc(xn_out[j], 16)

                    for j in range(2):
                        load(0, j)
                    with sp.Fori(0, NI - 1) as i:
                        for j in range(2):
                            if x_d is not None:
                                wait_apart(sp, x_in[j], 16 * i + 16, passed)
                            load(i + 1, j)
                        for j in range(2):
                            store(i, j)
                    for j in range(2):
                        store(NI - 1, j)
                    for j in range(2):
                        sp.wait_ge(xn_out[j], 16 * NI + 1)

                @block.vector
                def _(dve):
                    ahead(dve, turned, G // 2 + 1)
                    for j in range(2):
                        ahead(dve, xn_out[j], 1)
                    with dve.Fori(0, NI) as i:
                        for j in range(2):
                            g = 2 * i + j
                            if x_d is not None:
                                dve.wait_ge(x_in[j], 16 * i + 16)
                            for k in range(G):
                                dve.bn_stats(stats[:, k, :], X[:, bass.ds(g * G + k, 1), :].rearrange("p a c -> p (a c)")
                                             ).then_inc(dv, 1)
                            for k in range(G):
                                wait_apart(dve, dv, g * ND + k + 1, passed)
                                dve.bn_aggr(mv[:, k, :], stats[:, k, :]).then_inc(dv, 1)
                            dve.wait_ge(std_done, g + 1)
                            dve.reciprocal(rstd[:, :], std[:, :]).then_inc(dv, 1)
                            dve.wait_ge(dv, g * ND + ND)
                            dve.wait_ge(xn_out[j], 16 * i + 1)
                            dve.wait_ge(turned, G // 2 * (2 * i + j) + 1)
                            for k in range(G):
                                dve.tensor_scalar(XN[j][:, k, :], X[:, bass.ds(g * G + k, 1), :].rearrange("p a c -> p (a c)"),
                                                  mv[:, k, 0:1], rstd[:, k:k + 1], ALU.subtract, ALU.mult
                                                  ).then_inc(xn_ready, 1)

                @block.tensor
                def _(pe):
                    pe.wait_ge(gate_in, 16)
                    ahead(pe, evacuated, 1 + 1)
                    NP = G

                    def turn(i, p):
                        j, k = p // (G // 2), 2 * (p % (G // 2))
                        q = i * NP + p
                        pe.wait_ge(xn_ready, q * 2 + 2)
                        pe.wait_ge(evacuated, q + 1)
                        for a in range(2):
                            for c in range(CC):
                                m = pe.transpose(psT[p % 2][:, a, c, :], XN[j][:, k + a, c * P:(c + 1) * P],
                                                 consts["ident"][:, :])
                        m.then_inc(turned, 1)

                    def score(i, p):
                        q = i * NP + p
                        pe.wait_ge(evacuated, q + 3)
                        for a in range(2):
                            for c in range(CC):
                                m = pe.matmul(logits[:, bass.ds((q * 2 + a) * E, E)], xT[p % 2][:, a, c, :],
                                              gate[:, c, :], start=(c == 0), stop=(c == CC - 1))
                        m.then_inc(scored, 1)

                    with pe.Fori(0, NI) as i:
                        for p in range(NP + 1):
                            if p < NP:
                                turn(i, p)
                            if p:
                                score(i, p - 1)

                @block.scalar
                def _(act):
                    ahead(act, scored, 1 + 1)
                    with act.Fori(0, NI) as i:
                        for p in range(G):
                            q = i * G + p
                            if p % (G // 2) == 0:
                                g = 2 * i + p // (G // 2)
                                act.wait_ge(dv, g * ND + 2 * G)
                                act.activation(std[:, :], mv[:, :, 1], ACT.Sqrt, bias=consts["eps"][:, 0:1]
                                               ).then_inc(std_done, 1)
                            act.wait_ge(turned, q + 2 + G // 2)
                            act.wait_ge(scored, q + 1)
                            act.activation(xT[p % 2][:, :, :, :].rearrange("p a c n -> p (a c n)"),
                                           psT[p % 2][:, :, :, :].rearrange("p a c n -> p (a c n)"),
                                           ACT.Copy).then_inc(evacuated, 1)

            TE = [P, NT, E]
            t3 = lambda n: sb1(n, TE)
            t2 = lambda n: sb1(n, [P, NT])
            t1 = lambda n, d=F32: sb1(n, [P, E], d)
            z, ez, prob, prob2, eq, cand = t3("z"), t3("ez"), t3("prob"), t3("prob2"), t3("eq"), t3("cand")
            one_hot = [t3("one_hot0"), t3("one_hot1")]
            routed = [t3("routed0"), t3("routed1")]
            total, rtotal, top = t2("total"), t2("rtotal"), [t2("top0"), t2("top1")]
            first, both = t2("first"), t2("both")
            wide = sb1("wide", [P, NT, E, E])
            count = t3("count")
            cum = [t3("cum0"), t3("cum1")]
            before = t3("before")
            pos = sb1("pos", [P, NT, 2])
            sim = sb1("sim", [P, E, E])
            simm, eqs, moved, remap = (sb1(n, [P, E, E]) for n in ("simm", "eqs", "moved", "remap"))
            primary, gap, best, best_j, use, stay = (t1(n) for n in ("primary", "gap", "best", "best_j", "use", "stay"))
            counts1 = t1("counts1")
            nblk_i, nblk_j = t1("nblk_i", I32), t1("nblk_j", I32)
            blocks = [t1("blocks0"), t1("blocks1"), t1("blocks2")]
            starts = t1("starts")
            started = sb1("started", [P, NB, E - 1])
            be_f = sb1("be_f", [P, NB])
            pos_i = sb1("pos_i", [P, NT, 2], I32)
            lohi_i = [sb1(f"lohi_i{k}", [P, NT, 2], I32) for k in range(2)]
            lohi = [sb1(f"lohi{k}", [P, NT, 2]) for k in range(2)]
            oh_lo = [sb1(f"oh_lo{r}", [P, 8, P], BF16) for r in range(2)]
            oh_hi = [sb1(f"oh_hi{r}", [P, 8, NB], BF16) for r in range(2)]
            oh_tp = [sb1(f"oh_tp{r}", [P, 8, 2, NB], BF16) for r in range(2)]
            slot_p = sb1("slot_p", [P, NB])
            counts_ps = ps1("counts_ps", [P, E])
            prefix_ps = ps1("prefix_ps", [P, 2, NT, E])
            slots_ps = ps1("slots_ps", [P, 2, NB])
            sim_in, dvs, z_ready, ez_ready = sem1("sim_in"), sem1("dvs"), sem1("z_ready"), sem1("ez_ready")
            counted, summed = sem1("counted"), sem1("summed")
            oh_t, oh_p, oh_used, hi_made = (sem1(n) for n in ("oh_t", "oh_p", "oh_used", "hi_made"))
            iota_e, iota_e8, iota_f, iota_b, eye_e, t_idx, p_idx = (
                consts[k] for k in ("iota_e", "iota_e8", "iota_f", "iota_b", "eye_e", "t_idx", "p_idx"))
            weights = Weights(nc, sh, name, c1, gu_d, dn_d, wgu, wdn, passed)
            block = c1.enter_context(nc.Block(f"{name}_route"))
            lg = logits[:, 0:NT * E].rearrange("p (t e) -> p t e", e=E)
            over_e = lambda a: a.unsqueeze(2).to_broadcast([P, NT, E])
            over_t = lambda a: a.unsqueeze(1).to_broadcast([P, NT, E])

            NQ = NT * 2 // 8

            @block.sync
            def _(sp):
                sp.dma_start(sim[:, :, :], sim_d.unsqueeze(0).to_broadcast([P, E, E])).then_inc(sim_in, 16)
                weights.load(sp)

            @block.gpsimd
            def _(pool):
                for s in sems:
                    if Walk.start(s):
                        ahead(pool, sems[s], Walk.start(s))
                weights.rest(pool)
                ti = t_idx[:, :, :].rearrange("p t k -> p (t k)")
                with pool.Fori(0, NQ // 2) as i:
                    for r in range(2):
                        q = 2 * i + r
                        wait_apart(pool, hi_made, q + 1, passed)
                        pool.tensor_tensor(oh_tp[r][:, :, 0, :], oh_hi[r][:, :, :],
                                           ti[:, bass.ds(q * 8, 8)].unsqueeze(2).to_broadcast([P, 8, NB]),
                                           ALU.mult).then_inc(oh_t, 1)

            @block.scalar
            def _(act):
                act.wait_ge(z_ready, 1)
                act.activation(ez[:, :, :], z[:, :, :], ACT.Exp).then_inc(ez_ready, 1)
                weights.round(act)
                with act.Fori(0, NQ // 2) as i:
                    for r in range(2):
                        act.wait_ge(hi_made, 2 * i + r + 1)
                        act.activation(oh_tp[r][:, :, 1, :], oh_hi[r][:, :, :], ACT.Copy, scale=p_idx[:, 0:1]
                                       ).then_inc(oh_p, 1)

            @block.tensor
            def _(pe):
                pe.wait_ge(counted, 1)
                pe.matmul(counts_ps[:, :], consts["ones"][:, :], counts1[:, :], start=True, stop=True).then_inc(summed, 1)
                pe.wait_ge(counted, 2)
                flat = count[:, :, :].rearrange("p t e -> p (t e)")
                pe.matmul(prefix_ps[:, 0, :, :].rearrange("p t e -> p (t e)"), consts["upper"][:, :], flat,
                          start=True, stop=True)
                pe.matmul(prefix_ps[:, 1, :, :].rearrange("p t e -> p (t e)"), consts["ones"][:, :], flat,
                          start=True, stop=True).then_inc(summed, 1)

                def group(q, r, first_group, last_group):
                    pe.wait_ge(oh_t, q + 1)
                    pe.wait_ge(oh_p, q + 1)
                    for a in range(8):
                        m = pe.matmul(slots_ps[:, :, :].rearrange("p a b -> p (a b)"), oh_lo[r][:, a, :],
                                      oh_tp[r][:, a, :, :].rearrange("p a b -> p (a b)"),
                                      start=first_group and a == 0, stop=last_group and a == 7)
                    m.then_inc(oh_used, 1)

                group(0, 0, True, False)
                group(1, 1, False, False)
                with pe.Fori(1, NQ // 2 - 1) as i:
                    group(2 * i, 0, False, False)
                    group(2 * i + 1, 1, False, False)
                group(NQ - 2, 0, False, False)
                group(NQ - 1, 1, False, True)

            @block.vector
            def _(dve):
                seq = Seq(dve, dvs)
                T = seq.then

                def argfirst(out, source, value, eqt, candt, iotas):
                    T(dve.tensor_tensor(eqt, source, value, ALU.is_equal))
                    T(dve.scalar_tensor_tensor(candt, eqt, -float(E), iotas, ALU.mult, ALU.add))
                    T(dve.tensor_reduce(out, candt, AX.X, ALU.min))

                T(dve.tensor_reduce(total[:, :], lg, AX.X, ALU.max))
                dve.tensor_tensor(z[:, :, :], lg, over_e(total[:, :]), ALU.subtract).then_inc(z_ready, 1)
                dve.wait_ge(ez_ready, 1)
                T(dve.tensor_reduce(total[:, :], ez[:, :, :], AX.X, ALU.add))
                T(dve.reciprocal(rtotal[:, :], total[:, :]))
                T(dve.tensor_tensor(prob[:, :, :], ez[:, :, :], over_e(rtotal[:, :]), ALU.mult))
                for k, source in enumerate((prob, prob2)):
                    T(dve.tensor_reduce(top[k][:, :], source[:, :, :], AX.X, ALU.max))
                    argfirst(first[:, :], source[:, :, :], over_e(top[k][:, :]), eq[:, :, :], cand[:, :, :],
                             over_t(iota_e8[:, :]))
                    T(dve.tensor_tensor(one_hot[k][:, :, :], over_t(iota_e[:, :]), over_e(first[:, :]), ALU.is_equal))
                    if k == 0:
                        T(dve.scalar_tensor_tensor(prob2[:, :, :], one_hot[0][:, :, :], -2.0, prob[:, :, :],
                                                   ALU.mult, ALU.add))
                T(dve.tensor_reduce(counts1[:, :], one_hot[0][:, :, :].rearrange("p t e -> p e t"), AX.X, ALU.add))
                dve.engine_nop().then_inc(counted, 1)
                T(dve.tensor_tensor(both[:, :], top[0][:, :], top[1][:, :], ALU.add))
                T(dve.tensor_scalar(both[:, :], both[:, :], 1e-12, None, ALU.max))
                T(dve.reciprocal(rtotal[:, :], both[:, :]))
                for k in range(2):
                    T(dve.scalar_tensor_tensor(weight[:, k, :], top[k][:, :], 0.5, rtotal[:, :], ALU.mult, ALU.mult))
                dve.wait_ge(sim_in, 16)
                dve.wait_ge(summed, 1)
                T(dve.tensor_scalar(primary[:, :], counts_ps[:, :], 0.0, None, ALU.is_gt))
                T(dve.tensor_scalar(gap[:, :], primary[:, :], BIG, -BIG, ALU.mult, ALU.add))
                by_j = lambda a: a.unsqueeze(1).to_broadcast([P, E, E])
                by_e = lambda a: a.unsqueeze(2).to_broadcast([P, E, E])
                T(dve.tensor_tensor(simm[:, :, :], sim[:, :, :], by_j(primary[:, :]), ALU.mult))
                T(dve.tensor_tensor(simm[:, :, :], simm[:, :, :], by_j(gap[:, :]), ALU.add))
                T(dve.tensor_reduce(best[:, :], simm[:, :, :], AX.X, ALU.max))
                argfirst(best_j[:, :], simm[:, :, :], by_e(best[:, :]), eqs[:, :, :], moved[:, :, :],
                         by_j(iota_e8[:, :]))
                T(dve.tensor_scalar(use[:, :], best[:, :], THRESHOLD, None, ALU.is_ge))
                T(dve.tensor_scalar(stay[:, :], primary[:, :], -1.0, 1.0, ALU.mult, ALU.add))
                T(dve.tensor_tensor(use[:, :], use[:, :], stay[:, :], ALU.mult))
                T(dve.tensor_scalar(stay[:, :], use[:, :], -1.0, 1.0, ALU.mult, ALU.add))
                T(dve.tensor_tensor(moved[:, :, :], by_e(iota_e[:, :]), by_j(best_j[:, :]), ALU.is_equal))
                T(dve.tensor_tensor(moved[:, :, :], moved[:, :, :], by_j(use[:, :]), ALU.mult))
                T(dve.tensor_tensor(remap[:, :, :], eye_e[:, :, :], by_j(stay[:, :]), ALU.mult))
                T(dve.tensor_tensor(remap[:, :, :], remap[:, :, :], moved[:, :, :], ALU.add))
                for k in range(2):
                    T(dve.tensor_tensor(wide[:, :, :, :], one_hot[k][:, :, :].unsqueeze(2).to_broadcast([P, NT, E, E]),
                                        remap[:, :, :].unsqueeze(1).to_broadcast([P, NT, E, E]), ALU.mult))
                    T(dve.tensor_reduce(routed[k][:, :, :], wide[:, :, :, :], AX.X, ALU.add))
                dve.tensor_tensor(count[:, :, :], routed[0][:, :, :], routed[1][:, :, :], ALU.add).then_inc(counted, 1)
                dve.wait_ge(summed, 2)
                T(dve.tensor_copy(cum[0][:, :, :], prefix_ps[:, 1, :, :]))
                a, step = 0, 1
                while step < NT:
                    dve.tensor_copy(cum[1 - a][:, 0:step, :], cum[a][:, 0:step, :])
                    T(dve.tensor_tensor(cum[1 - a][:, step:, :], cum[a][:, step:, :], cum[a][:, 0:NT - step, :], ALU.add))
                    a, step = 1 - a, 2 * step
                T(dve.tensor_scalar(nblk_i[:, :], cum[a][:, NT - 1, :], float(P - 1), None, ALU.add))
                T(dve.tensor_single_scalar(nblk_j[:, :], nblk_i[:, :], 7, ALU.arith_shift_right))
                T(dve.tensor_copy(blocks[0][:, :], nblk_j[:, :]))
                b, step = 1, 1
                T(dve.tensor_copy(blocks[1][:, :], blocks[0][:, :]))
                while step < E:
                    dve.tensor_copy(blocks[3 - b][:, 0:step], blocks[b][:, 0:step])
                    T(dve.tensor_tensor(blocks[3 - b][:, step:], blocks[b][:, step:], blocks[b][:, 0:E - step], ALU.add))
                    b, step = 3 - b, 2 * step
                T(dve.tensor_tensor(starts[:, :], blocks[b][:, :], blocks[0][:, :], ALU.subtract))
                T(dve.tensor_tensor(started[:, :, :], iota_b[:, :].unsqueeze(2).to_broadcast([P, NB, E - 1]),
                                    starts[:, 1:E].unsqueeze(1).to_broadcast([P, NB, E - 1]), ALU.is_ge))
                T(dve.tensor_reduce(be_f[:, :], started[:, :, :], AX.X, ALU.add))
                T(dve.tensor_copy(block_expert[:, :], be_f[:, :]))
                T(dve.tensor_tensor(before[:, :, :], cum[a][:, :, :], prefix_ps[:, 1, :, :], ALU.subtract))
                T(dve.tensor_tensor(before[:, :, :], before[:, :, :], prefix_ps[:, 0, :, :], ALU.add))
                T(dve.tensor_scalar(starts[:, :], starts[:, :], float(P), None, ALU.mult))
                T(dve.tensor_tensor(before[:, :, :], before[:, :, :], over_t(starts[:, :]), ALU.add))
                for k in range(2):
                    T(dve.tensor_tensor(eq[:, :, :], before[:, :, :], routed[k][:, :, :], ALU.mult))
                    T(dve.tensor_reduce(pos[:, :, k], eq[:, :, :], AX.X, ALU.add))
                T(dve.tensor_tensor(eq[:, :, :], routed[0][:, :, :], routed[1][:, :, :], ALU.mult))
                T(dve.tensor_reduce(first[:, :], eq[:, :, :], AX.X, ALU.add))
                T(dve.tensor_tensor(pos[:, :, 1], pos[:, :, 1], first[:, :], ALU.add))
                T(dve.tensor_copy(pos_u[:, :, :], pos[:, :, :]))
                T(dve.tensor_copy(pos_i[:, :, :], pos[:, :, :]))
                T(dve.tensor_single_scalar(lohi_i[0][:, :, :], pos_i[:, :, :], P - 1, ALU.bitwise_and))
                T(dve.tensor_single_scalar(lohi_i[1][:, :, :], pos_i[:, :, :], 7, ALU.arith_shift_right))
                for k in range(2):
                    T(dve.tensor_copy(lohi[k][:, :, :], lohi_i[k][:, :, :]))
                lo, hi = (v.rearrange("p t k -> p (t k)") for v in (lohi[0][:, :, :], lohi[1][:, :, :]))
                ahead(dve, oh_used, 1 + 1)
                with dve.Fori(0, NQ // 2) as i:
                    for r in range(2):
                        q = 2 * i + r
                        dve.wait_ge(oh_used, q + 1)
                        dve.tensor_tensor(oh_lo[r][:, :, :], iota_f[:, :].unsqueeze(1).to_broadcast([P, 8, P]),
                                          lo[:, bass.ds(q * 8, 8)].unsqueeze(2).to_broadcast([P, 8, P]), ALU.is_equal)
                        dve.tensor_tensor(oh_hi[r][:, :, :], iota_b[:, :].unsqueeze(1).to_broadcast([P, 8, NB]),
                                          hi[:, bass.ds(q * 8, 8)].unsqueeze(2).to_broadcast([P, 8, NB]),
                                          ALU.is_equal).then_inc(hi_made, 1)
                dve.wait_ge(oh_used, NQ + 2)
                T(dve.tensor_copy(slot_p[:, :], slots_ps[:, 1, :]))
                T(dve.scalar_tensor_tensor(slot_u[:, :], slots_ps[:, 0, :], float(P), slot_p[:, :], ALU.mult, ALU.add))

        with ExitStack() as c1:
            sb1 = lambda n, s, d=F32: c1.enter_context(nc.sbuf_tensor(f"{name}_{n}", s, d))
            ps1 = lambda n, s, d=F32: c1.enter_context(nc.psum_tensor(f"{name}_{n}", s, d))
            sem1 = lambda n: c1.enter_context(nc.semaphore(f"{name}_{n}"))
            idx = [sb1(f"idx{j}", [P, 1], U32) for j in range(R)]
            xg = [sb1(f"xg{j}", [P, C]) for j in range(R)]
            y = [sb1(f"y{j}", [P, C]) for j in range(R)]
            x_hi, x_lo, h_hi, h_lo = ([sb1(f"{n}{j}", [P, CC, P], F32R) for j in range(2)]
                                      for n in ("x_hi", "x_lo", "h_hi", "h_lo"))
            act_g, h = ([sb1(f"{n}{j}", [P, F]) for j in range(2)] for n in ("act_g", "h"))
            psX, psH = ([ps1(f"{n}{j}", [P, 4, P])[:, 0:CC, :] for j in range(2)] for n in ("psX", "psH"))
            psG, psY = ([ps1(f"{n}{j}", [P, 512]) for j in range(2)] for n in ("psG", "psY"))
            ys_t = ys_d.rearrange("(b p) c -> b p c", p=P)
            flat = lambda t: t[:, :, :].rearrange("p c n -> p (c n)")

            def blocks_of_experts(w):
                on, wait, do, raised, e = w.on, w.wait, w.do, w.raised, w.engine
                expert = {}

                def expert_of(i, k):
                    if k not in expert:
                        expert[k] = e.value_load(block_expert[0:1, bass.ds(i, 1)], min_val=0, max_val=E - 1)
                    return expert[k]

                def gather(i, j):
                    if on("pool"):
                        wait("rows_used", 1)
                    do("pool", "idx_ready", lambda: e.tensor_copy(idx[j][:, :], slot_u[:, bass.ds(i, 1)]))
                    if on("pool"):
                        wait("idx_ready")
                    do("pool", f"gathered{j}", lambda: e.indirect_dma_start(
                        xg[j][:, :], None, xn_d[:, :], bass.IndirectOffsetOnAxis(ap=idx[j][:, 0:1], axis=0)), 16)

                def split(ps, hi, lo, turned, hi_done, lo_done):
                    if on("act"):
                        wait(turned)
                    do("act", hi_done, lambda: e.activation(flat(hi), ps.rearrange("p c n -> p (c n)"), ACT.Copy))
                    if on("dve"):
                        wait(hi_done)
                    do("dve", lo_done, lambda: e.tensor_tensor(flat(lo), ps.rearrange("p c n -> p (c n)"),
                                                               flat(hi).bitcast(F32), ALU.subtract))

                def turn_x(j):
                    if on("pe"):
                        wait(f"gathered{j}")
                    for c in range(CC):
                        m = e.transpose(psX[j % 2][:, c, :], xg[j][:, c * P:(c + 1) * P],
                                        consts["ident"][:, :]) if on("pe") else None
                        if c == 0:
                            raised("rows_used", m)
                    raised("x_turned", m)
                    split(psX[j % 2], x_hi[j % 2], x_lo[j % 2], "x_turned", "xhi_done", "xlo_done")

                def turn_h(j, later):
                    if on("pe"):
                        wait("h_done", later)
                        for c in range(CC):
                            m = e.transpose(psH[j % 2][:, c, :], h[j % 2][:, c * P:(c + 1) * P], consts["ident"][:, :])
                    raised("h_turned", m if on("pe") else None)
                    split(psH[j % 2], h_hi[j % 2], h_lo[j % 2], "h_turned", "hhi_done", "hlo_done")

                def three(out, hi, lo, wts, at, width):
                    n = 0
                    for s, ww in ((hi, wts[0]), (lo, wts[0]), (hi, wts[1])):
                        for c in range(CC):
                            m = e.matmul(out, s[:, c, :], ww[:, bass.ds(at + c * width, width)],
                                         start=(n == 0), stop=(n == 3 * CC - 1))
                            n += 1
                    return m

                def gate_and_up(i, j, k, later):
                    def make():
                        return three(psG[j % 2][:, :], x_hi[j % 2], x_lo[j % 2], wgu, expert_of(i, k) * (CC * 2 * F), 2 * F)
                    if on("pe"):
                        wait("xlo_done", later)
                        wait("h_done", 1)
                    do("pe", "gu_done", make)
                    if on("act"):
                        wait("gu_done")
                    do("act", "silu_done", lambda: e.activation(act_g[j % 2][:, :], psG[j % 2][:, 0:F], ACT.Silu))
                    if on("dve"):
                        wait("silu_done")
                    do("dve", "h_done", lambda: e.tensor_tensor(h[j % 2][:, :], act_g[j % 2][:, :], psG[j % 2][:, F:2 * F],
                                                                ALU.mult))

                def output(i, j, k):
                    def make():
                        return three(psY[j % 2][:, 0:C], h_hi[j % 2], h_lo[j % 2], wdn, expert_of(i, k) * (CC * C), C)
                    if on("pe"):
                        wait("hlo_done")
                    do("pe", "y_done", make)
                    if on("act"):
                        wait("y_done")
                        wait(f"stored{j}")
                    do("act", "y_copied", lambda: e.activation(y[j][:, :], psY[j % 2][:, 0:C], ACT.Copy))
                    if on("sp"):
                        wait("y_copied")
                    do("sp", f"stored{j}", lambda: e.dma_start(
                        ys_t[bass.ds(i, 1), :, :].rearrange("b p c -> (b p) c"), y[j][:, :]), 16)

                def step(i, j, k, number=None):
                    number = j if number is None else number
                    left = -k if k is not None and k < 0 else 99
                    done = k if k is not None and k >= 0 else 99
                    if left > 0:
                        gate_and_up(i, j, number, 1 if left > 1 else 0)
                    if left > 2:
                        turn_x((j + 2) % R)
                    if left > R:
                        gather(i + R, j)
                    if done >= 2:
                        output(i - 2, (j - 2) % R, number - 2)
                    if done >= 1:
                        turn_h((j - 1) % R, 1)

                for j in range(R):
                    gather(j, j)
                turn_x(0)
                turn_x(1)
                for k in range(R):
                    step(k, k, k)

                def turn_of_loop(n):
                    expert.clear()
                    for k in range(U):
                        step(n * U + (R + k), k % R, None, k)

                w.turns((NB - 2 * R) // U, turn_of_loop)
                expert.clear()
                for k in range(R):
                    step(NB - R + k, k, k - R)
                output(NB - 2, (NB - 2) % R, R - 2)
                turn_h((NB - 1) % R, 0)
                output(NB - 1, (NB - 1) % R, R - 1)
                if on("act"):
                    for j in range(R):
                        wait(f"stored{j}")

            with nc.Block(f"{name}_experts") as block:
                for me, to in (("sp", block.sync), ("pe", block.tensor), ("act", block.scalar),
                               ("dve", block.vector), ("pool", block.gpsimd)):
                    to(lambda e, me=me: blocks_of_experts(Walk(me, e, sems, waits_for)))

        with ExitStack() as c1:
            sb1 = lambda n, s, d=F32: c1.enter_context(nc.sbuf_tensor(f"{name}_{n}", s, d))
            sem1 = lambda n: c1.enter_context(nc.semaphore(f"{name}_{n}"))
            R = 4
            cidx = [sb1(f"cidx{j}", [P, 2], U32) for j in range(R)]
            yg = [[sb1(f"yg{k}{j}", [P, C]) for j in range(R)] for k in range(2)]
            half = [sb1(f"half{j}", [P, C]) for j in range(R)]
            cidx_ready, half_done, o_done = sem1("cidx_ready"), sem1("half_done"), sem1("o_done")
            got = [sem1(f"got{j}") for j in range(R)]
            o_out = sem1("o_out")
            out_t = out_d.rearrange("(t p) c -> p t c", p=P) if out_d is not None else None
            if extra:
                extra.open(c1)
            block = c1.enter_context(nc.Block(f"{name}_combine"))

            @block.tensor
            def _(pe):
                if extra:
                    extra.tensor(pe)

            @block.scalar
            def _(act):
                if extra:
                    extra.scalar(act)

            @block.gpsimd
            def _(pool):
                if extra:
                    extra.gpsimd(pool)
                with pool.Fori(0, NT // R) as n:
                    for j in range(R):
                        wait_apart(pool, cidx_ready, n * R + j + 1, passed)
                        for k in range(2):
                            pool.indirect_dma_start(yg[k][j][:, :], None, ys_d[:, :],
                                                    bass.IndirectOffsetOnAxis(ap=cidx[j][:, k:k + 1], axis=0)
                                                    ).then_inc(got[j], 16)

            @block.vector
            def _(dve):
                def index(t, j):
                    dve.tensor_copy(cidx[j][:, :], pos_u[:, bass.ds(t, 1), :].rearrange("p a k -> p (a k)")
                                    ).then_inc(cidx_ready, 1)

                def combine(n, j):
                    t = n * R + j
                    row = X[:, bass.ds(t, 1), :].rearrange("p a c -> p (a c)")
                    dve.wait_ge(got[j], 32 * n + 32)
                    dve.scalar_tensor_tensor(half[j][:, :], yg[0][j][:, :], weight[:, 0, bass.ds(t, 1)], row,
                                             ALU.mult, ALU.add).then_inc(half_done, 1)
                    dve.wait_ge(half_done, t + 1)
                    dve.scalar_tensor_tensor(row, yg[1][j][:, :], weight[:, 1, bass.ds(t, 1)], half[j][:, :],
                                             ALU.mult, ALU.add).then_inc(o_done, 1)

                for j in range(R):
                    index(j, j)
                with dve.Fori(0, NT // R - 1) as n:
                    for j in range(R):
                        combine(n, j)
                        dve.wait_ge(o_done, n * R + j + 1)
                        index(n * R + R + j, j)
                for j in range(R):
                    combine(NT // R - 1, j)
                if extra:
                    extra.vector(dve)

            @block.sync
            def _(sp):
                if extra:
                    extra.sync(sp)
                if out_d is None:
                    return
                with sp.Fori(0, NT // R) as n:
                    wait_apart(sp, o_done, n * R + R, passed)
                    sp.dma_start(out_t[:, bass.ds(n * R, R), :], X[:, bass.ds(n * R, R), :]).then_inc(o_out, 16)
                sp.wait_ge(o_out, 16 * (NT // R))


ATTENTION_WAITS = {
    "stats_done": "dve", "var_done": "act", "std_done": "dve", "rstd_done": "dve",
    "xn_done": "pe", "turned": "act", "xhi_done": "dve", "xlo_done": "pe",
    "projected": "act", "q_in": "dve", "k_in": "pool", "copied": "pe", "rot0": "dve", "rot1": "pool",
    "v_copied": "pe", "stacking0": "pool", "stacking1": "dve", "stacked": "pe", "stack_free": "pool",
    "st_done": "act", "exp_done": "pe", "pv_done": "act", "mx_done": "dve", "max_done": "pe", "mcol_done": "pe",
    "psr_full": "act", "o_full": "dve", "psr_free": "pe", "oT_done": "pe", "o_step": "dve",
    "y_free": "pool", "summed": "dve", "x_done": "pe",
}

QUERIES = 512


class AttentionWeights:

    def __init__(self, nc, sh, ctx, w_d, up_d, wc_d, rope_d):
        sb = lambda n, s, d=F32: ctx.enter_context(nc.sbuf_tensor(f"a_{n}", s, d))
        self.nc, self.w_d, self.up_d, self.wc_d, self.rope_d = nc, w_d, up_d, wc_d, rope_d
        self.PR, self.DH, self.CC, self.C = sh.H // 2, sh.DH, sh.CC, sh.C
        self.scale = float(sh.DH) ** -0.5
        n = sh.CC * 3 * sh.C
        self.shared = sb("shared", [P, 2 * n], F32R)
        self.w_eff = [self.shared[:, k * n:(k + 1) * n].rearrange("p (c n) -> p c n", c=sh.CC) for k in range(2)]
        self.w_c = [sb(f"w_c{k}", [P, sh.CC, sh.C], F32R) for k in range(2)]
        self.rope = sb("rope", [P, 2, sh.T // P, sh.DH // 2])
        self.causal = sb("causal", [P, QUERIES])
        self.mask = [sb(f"mask{k}", [P, P], BF16) for k in range(2)]
        self.sems = {n: ctx.enter_context(nc.semaphore(f"a_{n}")) for n in ATTENTION_WAITS}

    def open(self, c1):
        sb1 = lambda n, s, d=F32: c1.enter_context(self.nc.sbuf_tensor(f"a_{n}", s, d))
        sem1 = lambda n: c1.enter_context(self.nc.semaphore(f"a_{n}"))
        self.down = [sb1(f"down{w}", [P, self.PR, self.C]) for w in range(3)]
        self.up = sb1("up", [P, 3, 2 * self.DH])
        self.wc = sb1("wc", [P, self.CC, self.C])
        self.ps = [[c1.enter_context(self.nc.psum_tensor(f"a_fold{w}{c}", [P, 512], F32)) for c in range(self.CC)]
                   for w in range(3)]
        self.cleared, self.w_in, self.wc_in, self.folded, self.hi_done = (
            sem1(n) for n in ("cleared", "w_in", "wc_in", "folded", "hi_done"))

    def sync(self, sp):
        for w in range(3):
            sp.dma_start(self.down[w][:, :, :], self.w_d[w].rearrange("(r p) c -> p r c", p=P)).then_inc(self.w_in, 16)
        sp.wait_ge(self.cleared, 1)
        for w in range(3):
            for h in range(2):
                at = h * self.DH
                for part in self.up_d[w]:
                    width = part.shape[1]
                    sp.dma_start(self.up[64 * h:64 * h + 64, w, at:at + width], part).then_inc(self.w_in, 16)
                    at += width
        sp.dma_start(self.wc[:, :, :], self.wc_d.rearrange("(c p) n -> p c n", p=P)).then_inc(self.wc_in, 16)
        sp.dma_start(self.rope[:, :, :, :], self.rope_d.rearrange("a (t p) d -> p a t d", p=P)).then_inc(self.wc_in, 16)
        sp.wait_ge(self.wc_in, 32)

    def gpsimd(self, pool):
        pool.memset(self.up[:, :, :], 0.0).then_inc(self.cleared, 1)
        pool.memset(self.causal[:, :], 0.0).then_inc(self.cleared, 1)
        pool.memset(self.mask[0][:, :], 0.0).then_inc(self.cleared, 1)
        pool.memset(self.mask[1][:, :], 0.0).then_inc(self.cleared, 1)
        for s in self.sems.values():
            ahead(pool, s, Walk.START)
        pool.wait_ge(self.cleared, 4)
        last = self.causal[:, QUERIES - P:QUERIES]
        pool.affine_select(last, last, [[-1, P]], ALU.is_ge, -BIG, 0, 1)
        pool.affine_select(self.mask[0][:, :], self.mask[0][:, :], [[-1, P]], ALU.not_equal, 1.0, 0, 1)
        pool.affine_select(self.mask[1][:, :], self.mask[1][:, :], [[1, P]], ALU.is_ge, -BIG, 0, -1)

    def tensor(self, pe):
        pe.wait_ge(self.w_in, 16 * (3 + 2 * 5))
        for w in range(3):
            for c in range(self.CC):
                for r in range(self.PR):
                    m = pe.matmul(self.ps[w][c][:, r * 2 * self.DH:(r + 1) * 2 * self.DH], self.down[w][:, r, c * P:(c + 1) * P],
                                  self.up[:, w, :], start=True, stop=True)
                m.then_inc(self.folded, 1)

    def parts(self):
        n = 0
        for w in range(3):
            for c in range(self.CC):
                n += 1
                yield (self.folded, n, self.ps[w][c][:, 0:self.C], self.scale if w == 0 else 1.0,
                       [k[:, c, w * self.C:(w + 1) * self.C] for k in self.w_eff])
        for c in range(self.CC):
            yield self.wc_in, 32, self.wc[:, c, :], 1.0, [k[:, c, :] for k in self.w_c]

    def scalar(self, act):
        for sem, n, src, s, (hi, _) in self.parts():
            act.wait_ge(sem, n)
            act.activation(hi, src, ACT.Copy, scale=s).then_inc(self.hi_done, 1)

    def vector(self, dve):
        for k, (_, _, src, s, (hi, lo)) in enumerate(self.parts()):
            dve.wait_ge(self.hi_done, k + 1)
            dve.scalar_tensor_tensor(lo, src, s, hi.bitcast(F32), ALU.mult, ALU.subtract)


def attention(nc, sh, X, made, consts):
    B, T, C, CC, H = sh.B, sh.T, sh.C, sh.CC, sh.H
    DH, D2 = sh.DH, sh.DH // 2
    NTB = T // P
    PR = H // 2
    G = B * PR
    HALF = QUERIES
    NH = T // HALF
    assert NTB == 8 and NH == 2 and DH == 16 and C == H * DH and G % 2 == 0
    QKW = 2 * C
    ident = consts["ident"]
    with ExitStack() as ctx:
        sb = lambda n, s, d=F32: ctx.enter_context(nc.sbuf_tensor(f"a_{n}", s, d))
        sems, w_eff, w_c, rope, causal, mask = made.sems, made.w_eff, made.w_c, made.rope, made.causal, made.mask
        QK = sb("QK", [P, G, NTB, 2, 2, DH])
        VY = sb("VY", [P, G, NTB, 2, DH])
        vy_tile = lambda b, t: VY[:, bass.ds(b * PR, PR), t, :, :].rearrange("p g h d -> p g (h d)")

        def phase(name, schedule, count):
            with nc.Block(name) as block:
                for me, on in (("sp", block.sync), ("pe", block.tensor), ("act", block.scalar),
                               ("dve", block.vector), ("pool", block.gpsimd)):
                    on(lambda e, me=me: schedule(Walk(me, e, sems, ATTENTION_WAITS, count)))
            w = Walk(None, None, sems, ATTENTION_WAITS, count)
            schedule(w)
            return w.count

        def tiles(w, src, psT, x_hi, x_lo, fill, finish, extra=None, read=None):
            flat = lambda t: t[:, :, :].rearrange("p c n -> p (c n)")

            def turn(t, back=0):
                j = t % 2
                if w.on("pe"):
                    w.wait("xn_done", back)
                    w.wait("xlo_done", 1)

                for c in range(CC):
                    m = w.engine.transpose(psT[j][:, c * P:(c + 1) * P], src[j][:, c * P:(c + 1) * P],
                                           ident[:, :]) if w.on("pe") else None
                    if c == 0 and read:
                        w.raised(read, m)
                w.raised("turned", m)
                if w.on("act"):
                    w.wait("turned")
                w.do("act", "xhi_done", lambda: w.engine.activation(flat(x_hi[j]), psT[j][:, 0:C], ACT.Copy))
                if w.on("dve"):
                    w.wait("xhi_done")
                w.do("dve", "xlo_done", lambda: w.engine.tensor_tensor(
                    flat(x_lo[j]), psT[j][:, 0:C], flat(x_hi[j]).bitcast(F32), ALU.subtract))

            def batch(b, last):
                for t in range(NTB):
                    if not (last and t == NTB - 1):
                        turn(t + 1)
                    if extra and not last and t == NTB - 2:
                        extra(b + 1, t)
                    if not (last and t >= NTB - 2):
                        fill(b + (t + 2) // NTB, (t + 2) % NTB)
                    if extra and not last and t < NTB - 2:
                        extra(b + 1, t)
                    finish(b, t, 0 if last and t == NTB - 1 else 1)

            fill(0, 0)
            fill(0, 1)
            turn(0, 1)
            w.turns(B - 1, lambda b: batch(b, False))
            batch(B - 1, True)

        def three(e, out, hi, lo, wts, at, n):
            k = 0
            for s, ww in ((hi, wts[0]), (lo, wts[0]), (hi, wts[1])):
                for c in range(CC):
                    m = e.matmul(out, s[:, c, :], ww[:, c, at:at + n], start=(k == 0), stop=(k == 3 * CC - 1))
                    k += 1
            return m

        with ExitStack() as c1:
            sb1 = lambda n, s, d=F32: c1.enter_context(nc.sbuf_tensor(f"a_{n}", s, d))
            stats, mv = sb1("stats", [P, NTB, 6]), sb1("mv", [P, NTB, 2])
            mean, std, rstd = sb1("mean", [P, NTB]), sb1("std", [P, NTB]), sb1("rstd", [P, NTB])
            XN = [sb1(f"XN{j}", [P, C]) for j in range(2)]
            x_hi, x_lo = ([sb1(f"{n}{j}", [P, CC, P], F32R) for j in range(2)] for n in ("x_hi", "x_lo"))
            rot_a = [sb1(f"rot_a{w}", [P, PR, 2, D2]) for w in range(2)]
            rot_b = [sb1(f"rot_b{w}", [P, PR, 2, D2]) for w in range(2)]
            psT = [c1.enter_context(nc.psum_tensor(f"a_psT{j}", [P, HALF], F32)) for j in range(2)]
            psP = [c1.enter_context(nc.psum_tensor(f"a_psP{j}", [P, 2, HALF], F32)) for j in range(2)]

            def project_all(w):
                on, wait, do, e = w.on, w.wait, w.do, w.engine
                row = lambda b, t: X[:, bass.ds(b * NTB + t, 1), :].rearrange("p a c -> p (a c)")

                def stat(b, t):
                    do("dve", "stats_done", lambda: e.bn_stats(stats[:, t, :], row(b, t)))

                def aggregate(t):
                    if on("dve"):
                        wait("stats_done", NTB - 1 - t)
                    do("dve", "var_done", lambda: e.bn_aggr(mv[:, t, :], stats[:, t, :]))

                def deviations():
                    if on("act"):
                        wait("var_done")
                    do("act", "std_done", lambda: e.activation(std[:, :], mv[:, :, 1], ACT.Sqrt,
                                                               bias=consts["eps"][:, 0:1]))
                    if on("dve"):
                        wait("std_done")
                    do("dve", "rstd_done", lambda: e.tensor_copy(mean[:, :], mv[:, :, 0]))
                    do("dve", "rstd_done", lambda: e.reciprocal(rstd[:, :], std[:, :]))

                def fill(b, t):
                    if on("dve"):
                        wait("rstd_done")
                    do("dve", "xn_done", lambda: e.tensor_scalar(XN[t % 2][:, :], row(b, t), mean[:, t:t + 1],
                                                                 rstd[:, t:t + 1], ALU.subtract, ALU.mult))

                def extra(b, t):
                    if t < 4:
                        if t == 0 and on("dve"):
                            wait("rstd_done")
                        stat(b, 2 * t)
                        stat(b, 2 * t + 1)
                    elif t < 6:
                        for k in range(4 * (t - 4), 4 * (t - 3)):
                            aggregate(k)
                    elif t == 6:
                        deviations()

                def rotate(b, t, name, which, given):
                    ee = QK[:, bass.ds(b * PR, PR), t, which, :, D2:DH]
                    pairs = lambda a, k: a.rearrange("p g h (i two) -> p g h i two", two=2)[:, :, :, :, k]
                    table = lambda a: rope[:, a, t, :].unsqueeze(1).unsqueeze(1).to_broadcast([P, PR, 2, D2])
                    if on(name):
                        wait(f"rot{which}")
                        wait(given)
                    do(name, f"rot{which}", lambda: e.tensor_tensor(rot_a[which][:, :, :, :], ee, table(0), ALU.mult))
                    for k in range(2):
                        do(name, f"rot{which}", lambda k=k: e.tensor_tensor(
                            pairs(rot_b[which][:, :, :, :], k), pairs(ee, 1 - k), pairs(table(1), k), ALU.mult))
                    if on(name):
                        wait(f"rot{which}")
                    do(name, f"rot{which}", lambda: e.tensor_tensor(ee, rot_a[which][:, :, :, :], rot_b[which][:, :, :, :], ALU.add))

                def finish(b, t, back):
                    j = t % 2
                    if on("pe"):
                        wait("xlo_done", back)
                        wait("copied", 1)

                    def make():
                        three(e, psP[j][:, 0, :], x_hi[j], x_lo[j], w_eff, 0, QKW)
                        return three(e, psP[j][:, 1, 0:C], x_hi[j], x_lo[j], w_eff, QKW, C)
                    do("pe", "projected", make)
                    if on("act"):
                        wait("projected")
                    for k, given in enumerate(("q_in", "k_in")):
                        do("act", given, lambda: e.activation(
                            QK[:, bass.ds(b * PR, PR), t, k, :, :].rearrange("p g h d -> p g (h d)"),
                            psP[j][:, 0, k * C:(k + 1) * C].rearrange("p (g d) -> p g d", g=PR), ACT.Copy))
                    do("act", "copied", lambda: e.activation(
                        vy_tile(b, t), psP[j][:, 1, 0:C].rearrange("p (g d) -> p g d", g=PR), ACT.Copy))
                    rotate(b, t, "dve", 0, "q_in")
                    rotate(b, t, "pool", 1, "k_in")

                for t in range(NTB):
                    stat(0, t)
                for t in range(NTB):
                    aggregate(t)
                deviations()
                tiles(w, XN, psT, x_hi, x_lo, fill, finish, extra)

            count = phase("project", project_all, None)

        with ExitStack() as c1:
            sb1 = lambda n, s, d=F32: c1.enter_context(nc.sbuf_tensor(f"a_{n}", s, d))
            VP = [sb1(f"VP{r}", [P, NTB, 2, 32]) for r in range(2)]
            ROW = 2 * DH
            stack = [sb1(f"stack{w}", [P, NTB, 2, 64]) for w in range(2)]
            assert 3 * T <= made.shared.shape[-1]
            shared = [made.shared[:, k * T:(k + 1) * T] for k in range(3)]
            QT = shared[0:2]
            KT = [[shared[2], sb1("KT01", [P, T], F32R)], [sb1(f"KT1{h}", [P, T], F32R) for h in range(2)]]
            prob = [sb1(f"prob{r}", [P, 2, HALF]) for r in range(4)]
            mpart = [sb1(f"mpart{r}", [P, 2, NTB, 2]) for r in range(2)]
            mcol = [sb1(f"mcol{r}", [P, 4, P]) for r in range(2)]
            OT = sb1("OT", [P, HALF])
            o_sum = sb1("o_sum", [P, 4, 2, DH + 1])
            o_rec = sb1("o_rec", [P, 4, 2, 1])
            psS = [c1.enter_context(nc.psum_tensor(f"a_psS{j}", [P, 2, HALF], F32)) for j in range(2)]
            psM = [c1.enter_context(nc.psum_tensor(f"a_psM{j}", [P, HALF], F32)) for j in range(2)]
            psO = c1.enter_context(nc.psum_tensor("a_psO", [P, HALF], F32))
            psR = c1.enter_context(nc.psum_tensor("a_psR", [P, HALF], F32))
            init = c1.enter_context(nc.semaphore("a_init"))

            with nc.Block("clear") as block:
                @block.gpsimd
                def _(pool):
                    for w in range(2):
                        pool.memset(stack[w][:, :, :, :], 0.0).then_inc(init, 1)
                    for r in range(2):
                        pool.memset(VP[r][:, :, :, :], 0.0).then_inc(init, 1)
                    pool.wait_ge(init, 4)
                    pool.memset(stack[1][:, :, :, ROW:ROW + 1], 1.0)
                    for r in range(2):
                        pool.memset(VP[r][:, :, :, DH:DH + 1], 1.0)

                @block.vector
                def _(dve):
                    for r in range(2):
                        for h in range(2):
                            dve.memset(KT[r][h][64 * (1 - h):64 * (1 - h) + 64, :].bitcast(F32), 0.0)
                    dve.memset(psO[:, :], 0.0)
                    for qh in range(NH):
                        dve.memset(mcol[qh][:, :, :], 0.0)

            CHUNKS = []
            for qt in range(NTB):
                lo = qt * P // HALF * HALF
                for first in range(0, lo, HALF):
                    CHUNKS += [(h, qt, first, HALF, False) for h in range(2)]
                CHUNKS += [(h, qt, lo, (qt + 1) * P - lo, True) for h in range(2)]
            STEPS = [(qh, kt) for qh in range(NH) for kt in range((qh + 1) * HALF // P)]
            NS = len(STEPS)
            PER_STEP = len(CHUNKS) // NS
            assert len(CHUNKS) == PER_STEP * NS and PER_STEP == 2 and NS == 12

            def span(qh, kt):
                first = max(kt * P - qh * HALF, 0)
                return first, HALF - first

            def heads(w):
                on, wait, do, e = w.on, w.wait, w.do, w.engine

                def stack_part(pair, k, which):
                    name = ("pool", "dve")[which]
                    src = QK[:, bass.ds(pair, 1), :, which, :, :].rearrange("p g t h d -> p (g t) h d")
                    hi_at = ((0, DH), (0, ROW + 1))[which]
                    lo_at = (ROW + 1, DH)[which]
                    at = lambda a: stack[which][:, :, :, a:a + DH]
                    if k < 2:
                        if k == 0 and which == 0 and on(name):
                            wait("stack_free")
                        do(name, f"stacking{which}", lambda: e.tensor_copy(at(hi_at[k]).bitcast(F32R), src))
                    else:
                        if on(name):
                            wait(f"stacking{which}")
                        do(name, "stacked", lambda: e.tensor_tensor(at(lo_at), src, at(0), ALU.subtract))

                def misc_wait():
                    if on("pe"):
                        wait("psr_free")

                def four(make, first=None):
                    for k in range(4):
                        m = make(k) if on("pe") else None
                        if k == 0 and first:
                            w.raised(first, m)
                    return m

                def turn(which, qh, copies):
                    misc_wait()
                    if on("pe"):
                        wait("stacked")
                    w.raised("psr_full", four(lambda k: e.transpose(
                        psR[:, k * P:(k + 1) * P],
                        stack[which][:, qh * 4 + k, :, :].rearrange("p h d -> p (h d)"), ident[:, :])))
                    if on("act"):
                        wait("psr_full")
                    for out, rows in copies:
                        do("act", "psr_free", lambda: e.activation(out[rows, qh * HALF:(qh + 1) * HALF],
                                                                    psR[rows, :], ACT.Copy))

                def turn_q(r, qh):
                    turn(0, qh, [(QT[r], slice(0, P))])

                def turn_k(r, qh):
                    turn(1, qh, [(KT[r][h], slice(64 * h, 64 * h + 64)) for h in range(2)])

                def chunk(r, c):
                    h, qt, first, n, diagonal = CHUNKS[c]
                    b = c % 2
                    if on("pe"):
                        wait("max_done", 1)
                        if c in (0, 8, 10):
                            wait("psr_free", 2 if c == 8 else 0)
                    do("pe", "mx_done", lambda: e.matmul(psM[b][:, 0:n], QT[r][:, qt * P:(qt + 1) * P],
                                                         KT[r][h][:, first:first + n], start=True, stop=True))
                    slot = 0 if first == 0 else 1
                    out = mpart[r][:, h, qt, slot:slot + 1]
                    if on("dve"):
                        wait("mx_done")
                    if diagonal:
                        do("dve", "max_done", lambda: e.tensor_tensor_reduce(
                            psM[b][:, 0:n], psM[b][:, 0:n], causal[:, HALF - n:HALF], 1.0, -3e38, ALU.add, ALU.max, out))
                    else:
                        do("dve", "max_done", lambda: e.tensor_reduce(out, psM[b][:, 0:n], AX.X, ALU.max))

                def max_column(r, qh):
                    out = mcol[qh][:, :, ROW:ROW + 65:64]
                    if qh == 0:
                        do("dve", "mcol_done", lambda: e.tensor_copy(out, mpart[r][:, :, 0:4, 0].rearrange("p h t -> p t h")))
                    else:
                        do("dve", "mcol_done", lambda: e.tensor_tensor(
                            out, mpart[r][:, :, 4:8, 0].rearrange("p h t -> p t h"),
                            mpart[r][:, :, 4:8, 1].rearrange("p h t -> p t h"), ALU.max))

                def max_row(r, qh, first=None):
                    misc_wait()
                    if on("pe"):
                        wait("mcol_done")
                    w.raised("psr_full", four(lambda k: e.transpose(
                        psR[:, k * P:(k + 1) * P], mcol[qh][:, k, :], ident[:, :]), first))
                    if on("act"):
                        wait("psr_full")
                    for at in (ROW, ROW + 64):
                        do("act", "psr_free", lambda: e.activation(QT[r][at:at + 1, qh * HALF:(qh + 1) * HALF],
                                                                   psR[at:at + 1, :], ACT.Copy, scale=-1.0))

                def scores(r, s):
                    qh, kt = STEPS[s]
                    first, n = span(qh, kt)
                    diagonal = kt * P >= qh * HALF
                    b = s % 2
                    if on("pe"):
                        wait("exp_done", 1)
                        if kt == 0:
                            wait("psr_free")

                    def make():
                        for h in range(2):
                            m = e.matmul(psS[b][:, h, 0:n], KT[r][h][:, kt * P:(kt + 1) * P],
                                         QT[r][:, qh * HALF + first:(qh + 1) * HALF], start=True, stop=not diagonal)
                            if diagonal:
                                m = e.matmul(psS[b][:, h, 0:P], mask[0][:, :], mask[1][:, :], start=False, stop=True)
                        return m
                    do("pe", "st_done", make)
                    if on("act"):
                        wait("st_done")
                    do("act", "exp_done", lambda: e.activation(prob[s % 4][:, :, 0:n], psS[b][:, :, 0:n], ACT.Exp))

                def values(s, r, behind):
                    if on("pe"):
                        wait("exp_done", behind)
                        if s == 1:
                            wait("v_copied")
                        if STEPS[s][1] == 1:
                            wait("oT_done")

                    def make():
                        for k in (s - 1, s):
                            qh, kt = STEPS[k]
                            first, n = span(qh, kt)
                            last = (qh + 1) * HALF // P - 2
                            for h in range(2):
                                j = 2 * h + kt % 2
                                m = e.matmul(psO[32 * j:32 * j + 32, first:HALF],
                                             VP[r][:, kt, h, :],
                                             prob[k % 4][:, h, 0:n], start=(kt < 2), stop=(kt >= last))
                        return m
                    if STEPS[s] in ((0, HALF // P - 1), (1, NTB - 1)):
                        do("pe", "pv_done", make)
                    elif on("pe"):
                        make()

                def copy_v(r, pair):
                    if on("pool"):
                        wait("stack_free")
                    do("pool", "v_copied", lambda: e.tensor_copy(
                        VP[r][:, :, :, 0:DH], VY[:, bass.ds(pair, 1), :, :, :].rearrange("p g t h d -> p (g t) h d")))

                def out_copy():
                    if on("act"):
                        wait("pv_done")
                    do("act", "oT_done", lambda: e.activation(OT[:, :], psO[:, :], ACT.Copy))

                def out_rows(qh, pair, drained):
                    misc_wait()
                    if on("pe"):
                        wait("oT_done")
                    w.raised("o_full", four(lambda k: e.transpose(
                        psR[:, k * P:(k + 1) * P], OT[:, k * P:(k + 1) * P], ident[:, :])))
                    rows = lambda q, k: psR[:, :].rearrange("p (t h k d) -> p t h k d", h=2, k=2, d=32)[:, q, :, k, 0:DH + 1]
                    q = slice(1 if qh == 0 else 0, 4)

                    def even():
                        if on("dve"):
                            wait("o_full")
                            wait("o_step")
                        do("dve", "o_step", lambda: e.tensor_copy(o_sum[:, :, :, :], rows(slice(0, 4), 0)))

                    def odd():
                        if on("dve"):
                            wait("o_step")
                        do("dve", "psr_free", lambda: e.tensor_tensor(o_sum[:, q, :, :], rows(q, 1), o_sum[:, q, :, :], ALU.add))

                    def invert():
                        if drained and on("dve"):
                            e.drain()
                        do("dve", "o_step", lambda: e.reciprocal(o_rec[:, :, :, :], o_sum[:, :, :, DH:DH + 1]))

                    def divide():
                        if on("dve"):
                            wait("o_step")
                        do("dve", "o_step", lambda: e.tensor_tensor(
                            VY[:, bass.ds(pair, 1), qh * 4:qh * 4 + 4, :, :].rearrange("p g t h d -> p (g t) h d"),
                            o_sum[:, :, :, 0:DH], o_rec[:, :, :, :].to_broadcast([P, 4, 2, DH]), ALU.mult))
                    return even, odd, invert, divide

                def body(r, pair, do_s=True, do_m=True, do_t=True, tail=True):
                    nxt = 1 - r
                    slots = {}

                    def between(step, parts):
                        for at, part in zip((0, 1, 4, 5), parts):
                            slots[2 * step + at] = part

                    def first_chunk(s):
                        if do_m:
                            chunk(nxt, PER_STEP * s)
                        if 2 * s in slots:
                            slots[2 * s]()

                    def second_chunk(s):
                        if do_m:
                            chunk(nxt, PER_STEP * s + 1)
                        if s == 0 and do_s:
                            if not do_m and on("dve"):
                                e.drain()
                            max_column(r, 1)
                        if s == 4 and do_m:
                            max_column(nxt, 0)
                        if 2 * s + 1 in slots:
                            slots[2 * s + 1]()

                    def transposes(s):
                        if s == 1 and do_s:
                            max_row(r, 1)
                        if s == 2 and do_m:
                            turn_q(nxt, 1)
                        if s == 3 and do_m:
                            turn_k(nxt, 1)
                        if s == 4 and tail and do_s:
                            between(5, out_rows(1, pair - 1, not do_t))
                        if s == 6 and do_m:
                            max_row(nxt, 0, "stack_free")
                        if s == 8 and do_s:
                            between(9, out_rows(0, pair, not do_t))
                        if s == 10 and do_t:
                            turn_q(r, 0)
                        if s == 11 and do_t:
                            turn_k(r, 0)

                    def score(s):
                        if do_s:
                            scores(r, s)

                    def value(s):
                        if do_s and s % 2 and s >= 3:
                            values(s - 2, r, 2)
                        if do_s and s == 5:
                            out_copy()
                        if do_s and tail and s == 1:
                            values(NS - 1, nxt, 2)
                            out_copy()

                    for s in range(NS):
                        for part in (first_chunk, score, second_chunk, transposes, value):
                            part(s)
                        if do_t and s in (4, 5, 6):
                            stack_part(pair + 2, s - 4, 1)
                        if do_t and s in (6, 7, 8):
                            stack_part(pair + 2, s - 6, 0)
                        if do_m and s == 9:
                            copy_v(nxt, pair + 1)

                for k in range(3):
                    for which in range(2):
                        stack_part(0, k, which)
                turn_q(0, 0)
                turn_k(0, 0)
                body(1, -1, do_s=False)
                body(0, 0, tail=False)

                def two(i):
                    body(1, i * 2 + 1)
                    body(0, i * 2 + 2)

                w.turns(G // 2 - 2, two)
                body(1, G - 3)
                body(0, G - 2, do_t=False)
                body(1, G - 1, do_m=False, do_t=False)
                values(NS - 1, 1, 0)
                out_copy()
                for part in out_rows(1, G - 1, True):
                    part()

            count = phase("heads", heads, count)

        with ExitStack() as c1:
            sb1 = lambda n, s, d=F32: c1.enter_context(nc.sbuf_tensor(f"a_{n}", s, d))
            Y = [sb1(f"Y{j}", [P, C]) for j in range(2)]
            y_hi, y_lo = ([sb1(f"{n}{j}", [P, CC, P], F32R) for j in range(2)] for n in ("y_hi", "y_lo"))
            psT = [c1.enter_context(nc.psum_tensor(f"a_psYT{j}", [P, HALF], F32)) for j in range(2)]
            psW = [c1.enter_context(nc.psum_tensor(f"a_psW{j}", [P, HALF], F32)) for j in range(2)]

            def output(w):
                on, wait, do, e = w.on, w.wait, w.do, w.engine

                def fill(b, t):
                    if on("pool"):
                        wait("y_free")
                    do("pool", "xn_done", lambda: e.tensor_copy(Y[t % 2][:, :].rearrange("p (g d) -> p g d", g=PR),
                                                                vy_tile(b, t)))

                def finish(b, t, back):
                    j = t % 2
                    if on("pe"):
                        wait("xlo_done", back)
                        wait("x_done", 1)
                    do("pe", "summed", lambda: three(e, psW[j][:, 0:C], y_hi[j], y_lo[j], w_c, 0, C))
                    row = X[:, bass.ds(b * NTB + t, 1), :].rearrange("p a c -> p (a c)")
                    if on("dve"):
                        wait("summed")
                    do("dve", "x_done", lambda: e.tensor_tensor(row, psW[j][:, 0:C], row, ALU.add))

                tiles(w, Y, psT, y_hi, y_lo, fill, finish, read="y_free")

            phase("output", output, count)


def make_constants(nc, sh, ctx):
    NT, E, NB = sh.NT, sh.E, sh.NB
    sb = lambda n, s, d=F32: ctx.enter_context(nc.sbuf_tensor(n, s, d))
    c = {
        "ident": sb("ident", [P, P]), "ones": sb("ones", [P, P]), "upper": sb("upper", [P, P]),
        "iota_e": sb("iota_e", [P, E]), "iota_e8": sb("iota_e8", [P, E]), "iota_f": sb("iota_f", [P, P]),
        "iota_b": sb("iota_b", [P, NB]), "eye_e": sb("eye_e", [P, E, E]), "t_idx": sb("t_idx", [P, NT, 2]),
        "p_idx": sb("p_idx", [P, 1]), "eps": sb("eps", [P, 1]),
    }
    with nc.semaphore("made") as made, nc.Block("constants") as block:
        @block.gpsimd
        def _(pool):
            pool.memset(c["ident"][:, :], 0.0).then_inc(made, 1)
            pool.memset(c["eye_e"][:, :, :], 0.0).then_inc(made, 1)
            pool.memset(c["ones"][:, :], 1.0).then_inc(made, 1)
            pool.memset(c["eps"][:, :], EPS)
            small = dict(allow_small_or_imprecise_dtypes=True)
            pool.iota(c["iota_e"][:, :], [[1, E]], 0, 0, **small)
            pool.iota(c["iota_e8"][:, :], [[1, E]], E, 0, **small)
            pool.iota(c["iota_f"][:, :], [[1, P]], 0, 0, **small)
            pool.iota(c["iota_b"][:, :], [[1, NB]], 0, 0, **small)
            pool.iota(c["t_idx"][:, :, :], [[1, NT], [0, 2]], 0, 0, **small)
            pool.iota(c["p_idx"][:, :], [[0, 1]], 0, 1, **small)
            pool.wait_ge(made, 3)
            pool.affine_select(c["ident"][:, :], c["ident"][:, :], [[-1, P]], ALU.not_equal, 1.0, 0, 1)
            pool.affine_select(c["eye_e"][:, :, :], c["eye_e"][:, :, :], [[-1, E], [1, E]], ALU.not_equal, 1.0, 0, 0)
            pool.affine_select(c["upper"][:, :], c["ones"][:, :], [[1, P]], ALU.is_gt, 0.0, 0, -1)
    return c


def program(nc, sh, x, wq_down, wk_down, wv_down, ups, wc, gate, gate_up, down, sim, rope, out):
    dram = lambda n, s: nc.dram_tensor(n, s, F32).ap()
    xn, ys = dram("xn", [sh.N, sh.C]), dram("ys", [sh.NB * P, sh.C])
    with ExitStack() as ctx:
        consts = make_constants(nc, sh, ctx)
        passed = ctx.enter_context(nc.semaphore("passed"))
        X = ctx.enter_context(nc.sbuf_tensor("X", [P, sh.NT, sh.C], F32))

        made = AttentionWeights(nc, sh, ctx, (wq_down, wk_down, wv_down), ups, wc, rope)

        def ffn(name, src, dst, extra=None):
            with ExitStack() as c:
                wgu = [c.enter_context(nc.sbuf_tensor(f"{name}_wgu{k}", [P, sh.E * sh.CC * 2 * sh.F], F32R)) for k in range(2)]
                wdn = [c.enter_context(nc.sbuf_tensor(f"{name}_wdn{k}", [P, sh.E * sh.CC * sh.C], F32R)) for k in range(2)]
                moe(nc, sh, name, X, src, dst, gate, sim, gate_up, down, xn, ys, wgu, wdn, consts, passed, extra)

        ffn("m1", x, None, made)
        attention(nc, sh, X, made, consts)
        ffn("m2", None, out)


def rope_tables(T, D):
    inv = np.float32(1.0) / np.float32(10000.0) ** (np.arange(0, D, 2, dtype=np.float32) / np.float32(D))
    freqs = np.arange(T, dtype=np.float32)[:, None] * inv[None, :]
    emb = np.concatenate((freqs, freqs), axis=-1)
    sign = np.where(np.arange(D) % 2 == 0, np.float32(-1), np.float32(1))
    return np.stack((np.cos(emb), np.sin(emb) * sign)).astype(np.float32)


def kernel(**inputs):
    import concourse.bacc as bacc
    from concourse.bass_utils import run_bass_kernel_spmd

    a = {k[3:]: np.asarray(v) for k, v in inputs.items()}
    x = a["attn_x"]
    sh = Shapes(x, a["ffn_gate_up_proj"])
    given = {
        "x": x.reshape(sh.N, sh.C),
        "wq_down": a["attn_Wq_down"].T, "wk_down": a["attn_Wk_down"].T, "wv_down": a["attn_Wv_down"].T,
        "wq_up_c": a["attn_Wq_up_c"], "wq_up_e": a["attn_Wq_up_e"],
        "wk_up_c": a["attn_Wk_up_c"], "wk_up_e": a["attn_Wk_up_e"], "wv_up": a["attn_Wv_up"], "wc": a["attn_Wc"],
        "gate": a["ffn_gate_weight"].T, "gate_up": a["ffn_gate_up_proj"].transpose(0, 2, 1),
        "down": a["ffn_down_proj"].transpose(0, 2, 1), "sim": a["ffn_similarity_matrix"],
        "rope": rope_tables(sh.T, sh.DH // 2),
    }
    given = {k: np.ascontiguousarray(v) for k, v in given.items()}
    nc = bacc.Bacc("TRN2", target_bir_lowering=False, num_devices=1)
    d = {k: nc.dram_tensor(k, list(v.shape), F32, kind="ExternalInput").ap() for k, v in given.items()}
    out = nc.dram_tensor("out", [sh.N, sh.C], F32, kind="ExternalOutput").ap()
    ups = ((d["wq_up_c"], d["wq_up_e"]), (d["wk_up_c"], d["wk_up_e"]), (d["wv_up"],))
    program(nc, sh, d["x"], d["wq_down"], d["wk_down"], d["wv_down"], ups, d["wc"], d["gate"], d["gate_up"],
            d["down"], d["sim"], d["rope"], out)
    r = run_bass_kernel_spmd(nc, [given], core_ids=[0])
    return r.results[0]["out"].reshape(sh.B, sh.T, sh.C)
```
